# Optimizing a Trainium2 kernel written in Bass

```python
import numpy as np
import jax
import jax.numpy as jnp

def _softmax(x, axis=-1):
    return jax.nn.softmax(x, axis=axis)

def _gelu(x):
    return jax.nn.gelu(x, approximate=True)

def _silu(x):
    return jax.nn.silu(x)

def _sigmoid(x):
    return jax.nn.sigmoid(x)

def _layernorm(x, axis=-1, eps=1e-05):
    m = jnp.mean(x, axis=axis, keepdims=True)
    v = jnp.var(x, axis=axis, keepdims=True)
    return (x - m) / jnp.sqrt(v + eps)

def _scatter_add(tgt, idx, src, axis=0):
    return tgt.at[idx].add(src)

def _segment_sum(src, seg, n):
    return jax.ops.segment_sum(src, seg, n)
kernel_name = 'mk_decoder_postln_d1_seqx_r4_54f300'

def setup_inputs(seed: int=0):
    np.random.seed(seed)
    _w = jnp.asarray

    def _rec_inputs():
        import jax
        import jax.numpy as jnp
        _rk = jax.random.key(seed)
        x = -0.000125 + 0.9999 * jax.random.normal(jax.random.fold_in(_rk, 1), (1, 2048, 256), jnp.float32)
        _lenS = 2048 - jax.random.randint(jax.random.fold_in(_rk, 7), (1,), 0, max(1, 2048 // 4) + 1, jnp.int32)
        _lenS2 = 1601 - jax.random.randint(jax.random.fold_in(_rk, 8), (1,), 0, max(1, 1601 // 4) + 1, jnp.int32)
        _ctx_1024P = jax.random.normal(jax.random.fold_in(_rk, 11), (1, 16, 256), jnp.float32)
        _ctx_1024c = jax.random.dirichlet(jax.random.fold_in(_rk, 511), 0.3 * jnp.ones((16,), jnp.float32), (1, 1601))
        _ctx_1024t = jnp.einsum('bsk,bkd->bsd', _ctx_1024c, _ctx_1024P)
        _ctx_1024t = _ctx_1024t * jax.lax.rsqrt(jnp.mean(jnp.square(_ctx_1024t)) + 1e-12) * 0.953939
        ctx_1024 = 4.13588e-05 + 0.999923 * (_ctx_1024t + 0.3 * jax.random.normal(jax.random.fold_in(_rk, 611), (1, 1601, 256), jnp.float32))
        return (x, ctx_1024)
    x, ctx_1024 = _rec_inputs()

    def _L0_attn_setup():
        import jax, jax.numpy as jnp
        import numpy as np
        D_MODEL = 256
        N_HEADS = 16
        D_HEAD = D_MODEL // N_HEADS
        key = jax.random.key(seed)
        ks = jax.random.split(key, 9)
        s = 1.0 / np.sqrt(D_MODEL)
        inp = {'x': jax.random.normal(ks[0], (2, 512, D_MODEL), dtype=jnp.float32), 'wq': jax.random.uniform(ks[1], (D_MODEL, D_MODEL), jnp.float32, -s, s), 'bq': jnp.zeros((D_MODEL,), jnp.float32), 'wk': jax.random.uniform(ks[2], (D_MODEL, D_MODEL), jnp.float32, -s, s), 'bk': jnp.zeros((D_MODEL,), jnp.float32), 'wv': jax.random.uniform(ks[3], (D_MODEL, D_MODEL), jnp.float32, -s, s), 'bv': jnp.zeros((D_MODEL,), jnp.float32), 'wo': jax.random.uniform(ks[4], (D_MODEL, D_MODEL), jnp.float32, -s, s), 'bo': jnp.zeros((D_MODEL,), jnp.float32)}
        return inp
    _L0_attn_all = _L0_attn_setup()
    _L0_attn_in = {k: v for k, v in _L0_attn_all.items() if k in ('wq', 'bq', 'wk', 'bk', 'wv', 'bv', 'wo', 'bo')}
    del _L0_attn_all

    def _L0_xattn_setup():
        import jax, jax.numpy as jnp
        import numpy as np
        key = jax.random.key(seed)
        k1, k2, k3 = jax.random.split(key, 3)
        B, Nq, K, c = (8, 1024, 256, 256)
        query = jax.random.normal(k1, (B, Nq, c), dtype=jnp.float32)
        text_features = jax.random.normal(k2, (B, K, c), dtype=jnp.float32)
        learnable_matrix = jax.random.normal(k3, (c, c), dtype=jnp.float32)
        return {'query': query, 'text_features': text_features, 'learnable_matrix': learnable_matrix}
    _L0_xattn_all = _L0_xattn_setup()
    _L0_xattn_in = {k: v for k, v in _L0_xattn_all.items() if k in ('learnable_matrix',)}
    del _L0_xattn_all

    def _L0_ffn_setup():
        import jax, jax.numpy as jnp
        import numpy as np
        D_MODEL = 256
        N_EXPERTS = 8
        TOP_K = 2
        HIDDEN = 4 * D_MODEL
        key = jax.random.key(seed)
        ks = jax.random.split(key, 6)
        B, S = (2, 512)
        x = jax.random.normal(ks[0], (B, S, D_MODEL), dtype=jnp.float32)
        shared_w1 = jax.random.normal(ks[1], (HIDDEN, D_MODEL), dtype=jnp.float32) * 0.02
        shared_w2 = jax.random.normal(ks[2], (D_MODEL, HIDDEN), dtype=jnp.float32) * 0.02
        experts_w1 = jax.random.normal(ks[3], (N_EXPERTS, HIDDEN, D_MODEL), dtype=jnp.float32) * 0.02
        experts_w2 = jax.random.normal(ks[4], (N_EXPERTS, D_MODEL, HIDDEN), dtype=jnp.float32) * 0.02
        gate_w = jax.random.normal(ks[5], (N_EXPERTS, D_MODEL), dtype=jnp.float32) * 0.02
        return {'x': x, 'shared_w1': shared_w1, 'shared_w2': shared_w2, 'experts_w1': experts_w1, 'experts_w2': experts_w2, 'gate_w': gate_w}
    _L0_ffn_all = _L0_ffn_setup()
    _L0_ffn_in = {k: v for k, v in _L0_ffn_all.items() if k in ('shared_w1', 'shared_w2', 'experts_w1', 'experts_w2', 'gate_w')}
    del _L0_ffn_all
    return {'x': x, 'ctx_1024': ctx_1024, 'L0_attn_wq': _L0_attn_in['wq'], 'L0_attn_bq': _L0_attn_in['bq'], 'L0_attn_wk': _L0_attn_in['wk'], 'L0_attn_bk': _L0_attn_in['bk'], 'L0_attn_wv': _L0_attn_in['wv'], 'L0_attn_bv': _L0_attn_in['bv'], 'L0_attn_wo': _L0_attn_in['wo'], 'L0_attn_bo': _L0_attn_in['bo'], 'L0_xattn_learnable_matrix': _L0_xattn_in['learnable_matrix'], 'L0_ffn_shared_w1': _L0_ffn_in['shared_w1'], 'L0_ffn_shared_w2': _L0_ffn_in['shared_w2'], 'L0_ffn_experts_w1': _L0_ffn_in['experts_w1'], 'L0_ffn_experts_w2': _L0_ffn_in['experts_w2'], 'L0_ffn_gate_w': _L0_ffn_in['gate_w']}

def reference(x, ctx_1024, L0_attn_wq, L0_attn_bq, L0_attn_wk, L0_attn_bk, L0_attn_wv, L0_attn_bv, L0_attn_wo, L0_attn_bo, L0_xattn_learnable_matrix, L0_ffn_shared_w1, L0_ffn_shared_w2, L0_ffn_experts_w1, L0_ffn_experts_w2, L0_ffn_gate_w):
    import jax
    import jax.numpy as jnp

    def _L0_attn_ref(x, wq, bq, wk, bk, wv, bv, wo, bo):
        import jax, jax.numpy as jnp
        import numpy as np
        D_MODEL = 256
        N_HEADS = 16
        D_HEAD = D_MODEL // N_HEADS
        B, S, D = x.shape
        H, Dh = (N_HEADS, D_HEAD)
        q = (x @ wq + bq).reshape(B, S, H, Dh).transpose(0, 2, 1, 3)
        k = (x @ wk + bk).reshape(B, S, H, Dh).transpose(0, 2, 1, 3)
        v = (x @ wv + bv).reshape(B, S, H, Dh).transpose(0, 2, 1, 3)
        scores = jnp.einsum('bhqd,bhkd->bhqk', q, k) / jnp.sqrt(jnp.float32(Dh))
        causal = jnp.tril(jnp.ones((S, S), dtype=bool))
        scores = jnp.where(causal[None, None], scores, jnp.float32(-jnp.inf))
        attn = jax.nn.softmax(scores, axis=-1)
        out = jnp.einsum('bhqk,bhkd->bhqd', attn, v)
        out = out.transpose(0, 2, 1, 3).reshape(B, S, D)
        return out @ wo + bo

    def _L0_xattn_ref(query, text_features, learnable_matrix):
        import jax, jax.numpy as jnp
        import numpy as np
        t_prime = jnp.matmul(text_features, learnable_matrix)
        t_act = jax.nn.gelu(t_prime, approximate=False)
        weight_map = jnp.einsum('bqc,bkc->bqk', query, t_act)
        out = jnp.einsum('bqk,bkc->bqc', weight_map, text_features)
        return out

    def _L0_ffn_ref(x, shared_w1, shared_w2, experts_w1, experts_w2, gate_w):
        import jax, jax.numpy as jnp
        import numpy as np
        D_MODEL = 256
        N_EXPERTS = 8
        TOP_K = 2
        HIDDEN = 4 * D_MODEL
        B, S, D = x.shape
        T = B * S
        x_flat = x.reshape(T, D)
        shared = jnp.einsum('td,dh->th', x_flat, shared_w1.T)
        shared = jnp.einsum('th,hd->td', jax.nn.silu(shared), shared_w2.T)
        gate_logits = x_flat @ gate_w.T
        top_k_gates, top_k_idx = jax.lax.top_k(gate_logits, TOP_K)
        top_k_gates = jax.nn.softmax(top_k_gates, axis=1)
        gates = jnp.zeros((T, N_EXPERTS), dtype=x.dtype)
        gates = gates.at[jnp.arange(T)[:, None], top_k_idx].set(top_k_gates)
        h = jnp.einsum('td,ehd->teh', x_flat, experts_w1)
        expert_out = jnp.einsum('teh,edh->ted', jax.nn.silu(h), experts_w2)
        selected = jnp.einsum('ted,te->td', expert_out, gates)
        return (shared + selected).reshape(B, S, D)
    x = _layernorm(x + _L0_attn_ref(x, L0_attn_wq, L0_attn_bq, L0_attn_wk, L0_attn_bk, L0_attn_wv, L0_attn_bv, L0_attn_wo, L0_attn_bo), axis=-1)
    x = _layernorm(x + _L0_xattn_ref(x, ctx_1024, L0_xattn_learnable_matrix), axis=-1)
    x = _layernorm(x + _L0_ffn_ref(x, L0_ffn_shared_w1, L0_ffn_shared_w2, L0_ffn_experts_w1, L0_ffn_experts_w2, L0_ffn_gate_w), axis=-1)
    return x

_drawn_inputs = setup_inputs


def setup_inputs(seed=0):
    import zlib

    import numpy as np

    out = dict(_drawn_inputs(seed))
    spreads = {'L0_attn_bq': (0.0, 0.8),
     'L0_attn_bk': (0.0, 0.8),
     'L0_attn_bv': (0.0, 0.1),
     'L0_attn_bo': (0.0, 0.1)}
    factors = {'L0_attn_wq': 4.734, 'L0_attn_wk': 4.654}
    for name, (base, spread) in spreads.items():
        noise = np.random.default_rng([zlib.crc32(name.encode()), seed]).standard_normal(out[name].shape)
        drawn = base * np.exp(spread * noise) if base else spread * noise
        out[name] = jnp.asarray(drawn.astype(out[name].dtype))
    for name, factor in factors.items():
        out[name] = (out[name] * factor).astype(out[name].dtype)
    return out
```

```python
import numpy as np
import concourse.bass as bass
from concourse import mybir
from contextlib import ExitStack

S = 2048
D = 256
H = 16
DH = D // H
CTX = 1601
HID = 1024
NE = 8
P = 128
DC = D // P
NT = S // P
QB = 512
NQ = S // QB
TPQ = QB // P
HC = HID // P
CT = (CTX + P - 1) // P
CLAST = CTX - (CT - 1) * P
EPS = 1e-5
NEG = -1.0e30
WSCALE = 256.0

SLOTS = 4
MROW = 96
ZROW = SLOTS * DH
NSTACK = 4

QUADS = [(qb, 4 * k) for qb in range(NQ) for k in range(qb + 1)]
NQUAD = len(QUADS)
PIECES = [(t, c, min(QB, (t + 1) * P - c)) for t in range(NT) for c in range(0, (t + 1) * P, QB)]
NPIECE = len(PIECES)
PIECES_OF_QUAD = [5, 5, 5, 5, 4, 4, 4, 4, 4, 0]
assert sum(PIECES_OF_QUAD) == NPIECE and len(PIECES_OF_QUAD) == NQUAD
VW = 32


def decoder_layer(nc, x, xT, ctx_n, ctxT, wq, wk, wv, wo, b_qk, bv, bo, lm, w1T, w2T, gT, out):
    f32, f16, bf16, u32 = mybir.dt.float32, mybir.dt.float16, mybir.dt.bfloat16, mybir.dt.uint32
    ALU = mybir.AluOpType
    ACT = mybir.ActivationFunctionType
    X = mybir.AxisListType.X

    q_split = nc.dram_tensor("q_split", (2, D, S), f16).ap()
    k_split = nc.dram_tensor("k_split", (2, D, S), f16).ap()

    whole = ExitStack()
    with whole:
        def keep(name, shape, dt):
            return whole.enter_context(nc.sbuf_tensor(name, shape, dt))

        res = keep("res", [P, NT, D], f32)
        wo_split = keep("wo_split", [P, 2, DC, D], f16)
        xm = keep("xm", [P, DC, D], f32)
        gate_split = keep("gate_split", [P, 2, DC, NE], f16)
        bo_rows = keep("bo_rows", [P, D], f32)
        ident32 = keep("ident32", [P, P], f32)
        eps_col = keep("eps_col", [P, 1], f32)
        attn = keep("attn", [P, NT, DH + D], f32)
        with ExitStack() as two:
            values = two.enter_context(nc.sbuf_tensor("values", [P, H, NT, VW], f32))
            qstack = two.enter_context(nc.sbuf_tensor("qstack", [P, NSTACK, S], f16))
            kstack = two.enter_context(nc.sbuf_tensor("kstack", [P, NSTACK, S], f16))
            project(nc, f32, f16, ALU, ACT, x, xT, ctx_n, ctxT, wq, wk, wv, wo, b_qk, bv, bo, lm, gT,
                    q_split, k_split, res, wo_split, xm, gate_split, bo_rows, ident32, eps_col,
                    attn, values, qstack, kstack)
            attend(nc, f32, f16, bf16, ALU, ACT, X, q_split, k_split, ident32, attn, values, qstack, kstack)
        with ExitStack() as three:
            x2T = three.enter_context(nc.sbuf_tensor("x2T", [P, 2, DC, S], f16))
            gates = three.enter_context(nc.sbuf_tensor("gates", [P, NT, NE + 1], f32))
            mix(nc, f32, f16, u32, ALU, ACT, res, attn, wo_split, xm, gate_split, bo_rows, ident32,
                eps_col, x2T, gates)
            feed_forward(nc, f32, f16, ALU, ACT, res, x2T, gates, eps_col, w1T, w2T, out)


def project(nc, f32, f16, ALU, ACT, x, xT, ctx_n, ctxT, wq, wk, wv, wo, b_qk, bv, bo, lm, gT,
            q_split, k_split, res, wo_split, xm, gate_split, bo_rows, ident32, eps_col,
            attn, values, qstack, kstack):
    es = ExitStack()
    with es:
        def sb(name, shape, dt):
            return es.enter_context(nc.sbuf_tensor(name, shape, dt))

        def sem(name):
            return es.enter_context(nc.semaphore(name))

        xT_sb = sb("xT_sb", [P, DC, S], f32)
        x_split = sb("x_split", [P, 2, DC, S], f16)
        w_in = sb("w_in", [P, 4, DC, D], f32)
        w_split = sb("w_split", [P, 3, 2, DC, D], f16)
        g_in = sb("g_in", [P, DC, NE], f32)
        lm_sb = sb("lm_sb", [P, DC, D], f32)
        ctxT_sb = sb("ctxT_sb", [P, DC, CTX], f32)
        ctx_sb = sb("ctx_sb", [P, CT, D], f32)
        t_act = sb("t_act", [P, CT, D], f32)
        b_cols = sb("b_cols", [P, 2, DC], f32)
        bq_scaled = sb("bq_scaled", [P, DC], f32)
        bv_rows = sb("bv_rows", [P, D], f32)
        qk32 = sb("qk32", [P, 2, QB], f32)
        qk16 = sb("qk16", [P, 4, 2, QB], f16)
        proj = [es.enter_context(nc.psum_tensor(f"proj{i}", [P, QB], f32)) for i in range(2)]
        vps = [es.enter_context(nc.psum_tensor(f"vps{i}", [P, D], f32)) for i in range(2)]
        tps = [es.enter_context(nc.psum_tensor(f"tps{i}", [P, D], f32)) for i in range(2)]
        mps = es.enter_context(nc.psum_tensor("mps", [P, DC, D], f32))

        xT_in, w_loaded, small_in, ctx_in, res_in = sem("xT_in"), sem("w_loaded"), sem("small_in"), sem("ctx_in"), sem("res_in")
        pool_zeroed, pool_done, stacks_set = sem("pool_zeroed"), sem("pool_done"), sem("stacks_set")
        hi_done, split_done = sem("hi_done"), sem("split_done")
        qk_ready, qk_copied, qk_hi, qk_lo = sem("qk_ready"), sem("qk_copied"), sem("qk_hi"), sem("qk_lo")
        qk_stored = [sem(f"qk_stored{n}") for n in range(4)]
        bias_scaled = sem("bias_scaled")
        v_ready, v_done = sem("v_ready"), sem("v_done")
        t_ready, t_done, m_ready, m_copied = sem("t_ready"), sem("t_done"), sem("m_ready"), sem("m_copied")

        block = es.enter_context(nc.Block())

        @block.sync
        def _(sp):
            for c in range(DC):
                sp.dma_start(xT_sb[:, c, :], xT[c * P:(c + 1) * P, :]).then_inc(xT_in, 16)
            for n, w in enumerate((wq, wk, wv, wo)):
                sp.dma_start(w_in[:, n], w.rearrange("(c p) n -> p c n", p=P)).then_inc(w_loaded, 16)
            sp.dma_start(res[:], x.rearrange("(t p) d -> p t d", p=P)).then_inc(res_in, 16)
            for q in range(NQ):
                for n in range(4):
                    sp.wait_ge(qk_lo, 4 * q + n + 1)
                    what, c = n // 2, n % 2
                    for half in range(2):
                        sp.dma_start((q_split, k_split)[what][half, c * P:(c + 1) * P, q * QB:(q + 1) * QB],
                                     qk16[:, n, half, :]).then_inc(qk_stored[n], 16)
            sp.wait_ge(res_in, 16)
            for n in range(4):
                sp.wait_ge(qk_stored[n], 16 * 2 * NQ)

        @block.scalar
        def _(act):
            nc.scalar.dma_start(b_cols[:], b_qk).then_inc(small_in, 16)
            nc.scalar.dma_start(g_in[:], gT.rearrange("(c p) n -> p c n", p=P)).then_inc(small_in, 16)
            nc.scalar.dma_start(bo_rows[:], bo.partition_broadcast(P)).then_inc(small_in, 16)
            nc.scalar.dma_start(bv_rows[:], bv.partition_broadcast(P)).then_inc(small_in, 16)
            for c in range(DC):
                nc.scalar.dma_start(ctxT_sb[:, c, :], ctxT[c * P:(c + 1) * P, :]).then_inc(ctx_in, 16)
            nc.scalar.dma_start(lm_sb[:], lm.rearrange("(c p) n -> p c n", p=P)).then_inc(ctx_in, 16)
            nc.scalar.dma_start(ctx_sb[:, 0:CT - 1, :], ctx_n[0:(CT - 1) * P, :].rearrange("(t p) d -> p t d", p=P)).then_inc(ctx_in, 16)
            nc.scalar.dma_start(ctx_sb[0:CLAST, CT - 1, :], ctx_n[(CT - 1) * P:CTX, :]).then_inc(ctx_in, 16)
            act.wait_ge(small_in, 16 * 4)
            nc.scalar.activation(bq_scaled[:], b_cols[:, 0], ACT.Copy, scale=0.25).then_inc(bias_scaled, 1)
            act.wait_ge(bias_scaled, 1)
            for g in range(4 * NQ):
                what, c = (g % 4) // 2, g % 2
                act.wait_ge(qk_ready, g + 1)
                if g >= 2:
                    act.wait_ge(qk_lo, g - 1)
                nc.scalar.activation(qk32[:, g % 2], proj[g % 2][:], ACT.Identity,
                                     bias=bq_scaled[:, c:c + 1] if what == 0 else b_cols[:, 1, c:c + 1],
                                     scale=DH ** -0.5 if what == 0 else 1.0).then_inc(qk_copied, 1)
            for t in range(CT):
                n = P if t < CT - 1 else CLAST
                act.wait_ge(t_ready, t + 1)
                nc.scalar.activation(t_act[0:n, t], tps[t % 2][0:n], ACT.Gelu).then_inc(t_done, 1)

        @block.gpsimd
        def _(pool):
            nc.gpsimd.memset(ident32[:], 0.0).then_inc(pool_zeroed, 1)
            nc.gpsimd.memset(eps_col[:], EPS).then_inc(pool_done, 1)
            nc.gpsimd.memset(values[:, :, :, DH:VW], 0.0).then_inc(pool_zeroed, 1)
            pool.wait_ge(pool_zeroed, 2)
            nc.gpsimd.affine_select(out=ident32[:], in_=ident32[:], compare_op=ALU.not_equal, fill=1.0,
                                    base=0, pattern=[[-1, P]], channel_multiplier=1).then_inc(pool_done, 1)
            nc.gpsimd.memset(values[:, :, :, DH:DH + 1], 1.0).then_inc(pool_done, 1)
            pool.wait_ge(pool_done, 3)

        @block.vector
        def _(dve):
            def split(hi, lo, whole_, n):
                nc.vector.tensor_copy(hi, whole_).then_inc(hi_done, 1)
                dve.wait_ge(hi_done, n)
                nc.vector.tensor_tensor(lo, whole_, hi, ALU.subtract).then_inc(split_done, 1)

            nc.vector.memset(kstack[ZROW:P], 0.0).then_inc(stacks_set, 1)
            nc.vector.memset(qstack[ZROW:P], 0.0).then_inc(stacks_set, 1)
            dve.wait_ge(stacks_set, 1)
            nc.vector.memset(kstack[MROW:MROW + 1], 1.0).then_inc(stacks_set, 1)
            dve.wait_ge(w_loaded, 16 * 4)
            for n in range(2):
                split(w_split[:, n, 0], w_split[:, n, 1], w_in[:, n], n + 1)
            dve.wait_ge(xT_in, 16 * DC)
            for q in range(NQ):
                cols = slice(q * QB, (q + 1) * QB)
                split(x_split[:, 0, :, cols], x_split[:, 1, :, cols], xT_sb[:, :, cols], 3 + q)
            split(w_split[:, 2, 0], w_split[:, 2, 1], w_in[:, 2], 3 + NQ)
            split(wo_split[:, 0], wo_split[:, 1], w_in[:, 3], 4 + NQ)
            dve.wait_ge(small_in, 16 * 4)
            split(gate_split[:, 0], gate_split[:, 1], g_in[:], 5 + NQ)
            for g in range(4 * NQ):
                dve.wait_ge(qk_copied, g + 1)
                if g >= 4:
                    dve.wait_ge(qk_stored[g % 4], 32 * (g // 4))
                nc.vector.tensor_copy(qk16[:, g % 4, 0], qk32[:, g % 2]).then_inc(qk_hi, 1)
                dve.wait_ge(qk_hi, g + 1)
                nc.vector.tensor_tensor(qk16[:, g % 4, 1], qk32[:, g % 2], qk16[:, g % 4, 0],
                                        ALU.subtract).then_inc(qk_lo, 1)
            for t in range(NT):
                dve.wait_ge(v_ready, t + 1)
                nc.vector.tensor_tensor(values[:, :, t, 0:DH], vps[t % 2][:].rearrange("p (h d) -> p h d", d=DH),
                                        bv_rows[:].rearrange("p (h d) -> p h d", d=DH), ALU.add).then_inc(v_done, 1)
            dve.wait_ge(m_ready, 1)
            nc.vector.tensor_copy(xm[:], mps[:]).then_inc(m_copied, 1)

        @block.tensor
        def _(pe):
            products = [(0, 0), (0, 1), (1, 0)]
            for g in range(4 * NQ):
                q, what, c = g // 4, (g % 4) // 2, g % 2
                pe.wait_ge(split_done, 3 + q)
                if g >= 2:
                    pe.wait_ge(qk_copied, g - 1)
                n = 0
                for k in range(DC):
                    for a, b in products:
                        mm = nc.tensor.matmul(proj[g % 2][:], w_split[:, what, a, k, c * P:(c + 1) * P],
                                              x_split[:, b, k, q * QB:(q + 1) * QB], start=(n == 0), stop=(n == 5))
                        n += 1
                mm.then_inc(qk_ready, 1)
            pe.wait_ge(split_done, 3 + NQ)
            for t in range(NT):
                if t >= 2:
                    pe.wait_ge(v_done, t - 1)
                n = 0
                for k in range(DC):
                    for a, b in products:
                        mm = nc.tensor.matmul(vps[t % 2][:], x_split[:, a, k, t * P:(t + 1) * P],
                                              w_split[:, 2, b, k], start=(n == 0), stop=(n == 5))
                        n += 1
                mm.then_inc(v_ready, 1)
            pe.wait_ge(ctx_in, 16 * 5)
            for t in range(CT):
                n = P if t < CT - 1 else CLAST
                if t >= 2:
                    pe.wait_ge(t_done, t - 1)
                for k in range(DC):
                    mm = nc.tensor.matmul(tps[t % 2][0:n], ctxT_sb[:, k, t * P:t * P + n], lm_sb[:, k],
                                          start=(k == 0), stop=(k == DC - 1))
                mm.then_inc(t_ready, 1)
            for c in range(DC):
                for t in range(CT):
                    n = P if t < CT - 1 else CLAST
                    pe.wait_ge(t_done, t + 1)
                    mm = nc.tensor.matmul(mps[:, c], t_act[0:n, t, c * P:(c + 1) * P], ctx_sb[0:n, t],
                                          start=(t == 0), stop=(t == CT - 1))
            mm.then_inc(m_ready, 1)


def attend(nc, f32, f16, bf16, ALU, ACT, X, q_split, k_split, ident32, attn, values, qstack, kstack):
    es = ExitStack()
    with es:
        def sb(name, shape, dt):
            return es.enter_context(nc.sbuf_tensor(name, shape, dt))

        def sem(name):
            return es.enter_context(nc.semaphore(name))

        ident16 = sb("ident16", [P, P], bf16)
        hide_keys = sb("hide_keys", [P, P], bf16)
        hide_queries = sb("hide_queries", [P, P], bf16)
        zeros16 = sb("zeros16", [P, P], bf16)
        ones16 = sb("ones16", [P, QB], bf16)
        fold = sb("fold", [P, VW], f32)
        probs = sb("probs", [P, 2, TPQ * QB], f32)
        v_head = sb("v_head", [P, 2, NT, VW], f32)
        partial = sb("partial", [P, NT, NQ], f32)
        neg_max = sb("neg_max", [P, NT], f32)
        max_row = sb("max_row", [NT, P], f16)
        acc_sb = sb("acc_sb", [P, 2, QB], f32)
        inv = sb("inv", [P, TPQ, 1], f32)
        scores = [es.enter_context(nc.psum_tensor(f"scores{i}", [P, 2 * QB], f32)) for i in range(2)]
        piece = [es.enter_context(nc.psum_tensor(f"piece{i}", [P, QB], f32)) for i in range(2)]
        acc = es.enter_context(nc.psum_tensor("acc", [P, QB], f32))
        misc = es.enter_context(nc.psum_tensor("misc", [P, QB], f32))
        folded = misc[:, 0:TPQ * VW].rearrange("p (t v) -> p t v", v=VW)
        maxT = misc[0:NT, 256:256 + P]

        const_zero, const_done = sem("const_zero"), sem("const_done")
        stack_in = [sem(f"stack_in{n}") for n in range(NSTACK)]
        max_in = sem("max_in")
        scores_ready, exp_done = sem("scores_ready"), sem("exp_done")
        piece_ready, piece_done = sem("piece_ready"), sem("piece_done")
        max_found, maxT_ready, max_row_ready = sem("max_found"), sem("maxT_ready"), sem("max_row_ready")
        v_ready, pv_done, acc_copied = sem("v_ready"), sem("pv_done"), sem("acc_copied")
        folded_ready, inv_ready, normed = sem("folded_ready"), sem("inv_ready"), sem("normed")

        half_width = []
        for qb, k0 in QUADS:
            w = [QB - P * j if k0 == qb * TPQ else QB for j in range(TPQ)]
            half_width.append((w[0:2], w[2:4]))

        block = es.enter_context(nc.Block())

        @block.sync
        def _(sp):
            def load_stack(h, slot):
                for s in range(SLOTS):
                    for dst, src, half in ((qstack, q_split, s // 2), (kstack, k_split, s % 2)):
                        sp.dma_start(dst[s * DH:(s + 1) * DH, slot, :],
                                     src[half, bass.ds(h * DH, DH), :]).then_inc(stack_in[slot], 16)

            def load_max(slot, n):
                sp.wait_ge(max_row_ready, n)
                sp.dma_start(qstack[MROW:MROW + 1, slot, :], max_row[:, :]).then_inc(max_in, 16)

            for h in range(NSTACK):
                load_stack(h, h)
            load_max(0, 1)

            def turn(i, last):
                for j in range(NSTACK):
                    if not (last and j == NSTACK - 1):
                        load_max((j + 1) % NSTACK, i + j + 2)
                    if not last:
                        sp.wait_ge(scores_ready, i * (2 * NQUAD) + 2 * NQUAD * (j + 1))
                        load_stack(i + (j + NSTACK), j)

            with sp.Fori(0, H // NSTACK - 1) as k:
                turn(k * NSTACK, False)
            turn(H - NSTACK, True)

        @block.gpsimd
        def _(pool):
            nc.gpsimd.memset(ident16[:], 0.0).then_inc(const_zero, 1)
            nc.gpsimd.memset(hide_keys[:], 0.0).then_inc(const_zero, 1)
            nc.gpsimd.memset(hide_queries[:], 0.0).then_inc(const_zero, 1)
            nc.gpsimd.memset(zeros16[:], 0.0).then_inc(const_done, 1)
            nc.gpsimd.memset(ones16[:], 1.0).then_inc(const_done, 1)
            nc.gpsimd.memset(fold[:], 0.0).then_inc(const_zero, 1)
            nc.gpsimd.memset(v_head[:, 1], 1.0).then_inc(const_done, 1)
            nc.gpsimd.memset(partial[:], NEG * 10.0).then_inc(const_done, 1)
            pool.wait_ge(const_zero, 4)
            nc.gpsimd.affine_select(out=ident16[:], in_=ident16[:], compare_op=ALU.not_equal, fill=1.0,
                                    base=0, pattern=[[-1, P]], channel_multiplier=1).then_inc(const_done, 1)
            nc.gpsimd.affine_select(out=hide_keys[:], in_=hide_keys[:], compare_op=ALU.is_ge, fill=NEG,
                                    base=0, pattern=[[-1, P]], channel_multiplier=1).then_inc(const_done, 1)
            nc.gpsimd.affine_select(out=hide_queries[:], in_=hide_queries[:], compare_op=ALU.is_ge, fill=NEG,
                                    base=0, pattern=[[1, P]], channel_multiplier=-1).then_inc(const_done, 1)
            for r in range(P // VW):
                pool.wait_ge(const_zero, 4 + r)
                nc.gpsimd.affine_select(out=fold[:], in_=fold[:], compare_op=ALU.not_equal, fill=1.0,
                                        base=-VW * r, pattern=[[-1, VW]], channel_multiplier=1).then_inc(const_zero, 1)
            pool.wait_ge(const_zero, 4 + P // VW)

            def copy_values(h, n, slot, first):
                if not first:
                    pool.wait_ge(pv_done, n * NQUAD - (NQUAD - 2))
                nc.gpsimd.tensor_copy(v_head[:, slot], values[:, bass.ds(h, 1)].rearrange("p o t v -> p (o t) v")).then_inc(v_ready, 1)

            copy_values(0, 0, 0, True)
            copy_values(1, 1, 1, False)
            with pool.Fori(1, H // 2) as k:
                for j in range(2):
                    copy_values(k * 2 + j, k * 2 + j, j, False)

        @block.scalar
        def _(act):
            act.wait_ge(const_done, 7)
            for half in range(2):
                for j in range(2):
                    at = (2 * half + j) * QB
                    fill = nc.scalar.activation(probs[:, 1, at:at + QB], ones16[:], ACT.Copy)
                fill.then_inc(exp_done, 1)

            def head(h, last):
                for s, (qb, k0) in enumerate(QUADS):
                    for half in range(2):
                        w = sum(half_width[s][half])
                        act.wait_ge(scores_ready, h * (2 * NQUAD) + (2 * s + half + 1))
                        if half == 0:
                            act.wait_ge(pv_done, h * NQUAD + (s + 1))
                        nc.scalar.activation(probs[:, s % 2, half * 2 * QB:half * 2 * QB + w],
                                             scores[half][:, 0:w], ACT.Exp).then_inc(exp_done, 1)
                    for b in range(NQ):
                        if b < NQ - 1 and s == LAST_QUAD[b] + 1:
                            act.wait_ge(pv_done, h * NQUAD + (LAST_QUAD[b] + 3))
                            act.wait_ge(folded_ready, h * NQ + (b + 1))
                            nc.scalar.activation(acc_sb[:, b % 2], acc[:], ACT.Copy).then_inc(acc_copied, 1)
                    if s == 0:
                        act.wait_ge(pv_done, h * NQUAD + 2)
                        act.wait_ge(folded_ready, h * NQ + 1)
                        nc.scalar.activation(acc_sb[:, (NQ - 1) % 2], acc[:], ACT.Copy).then_inc(acc_copied, 1)

            with act.Fori(0, H) as h:
                head(h, False)
            act.wait_ge(pv_done, H * NQUAD + 2)
            act.wait_ge(folded_ready, H * NQ + 1)
            nc.scalar.activation(acc_sb[:, (NQ - 1) % 2], acc[:], ACT.Copy).then_inc(acc_copied, 1)

        @block.tensor
        def _(pe):
            pe.wait_ge(const_done, 7)
            pe.wait_ge(const_zero, 4 + P // VW)

            def form_piece(h, slot, n):
                t, c, w = PIECES[n]
                bank = piece[n % 2]
                if not (isinstance(h, int) and h == 0 and n < 2):
                    pe.wait_ge(piece_done, h * NPIECE + (n - 1))
                diagonal = c + w == (t + 1) * P
                mm = nc.tensor.matmul(bank[:, 0:w], qstack[0:MROW, slot, t * P:(t + 1) * P],
                                      kstack[0:MROW, slot, c:c + w], start=True, stop=not diagonal)
                if diagonal:
                    mm = nc.tensor.matmul(bank[:, w - P:w], ident16[:], hide_keys[:], start=False, stop=True)
                mm.then_inc(piece_ready, 1)

            nc.tensor.matmul(acc[:], zeros16[:], ones16[:], start=True, stop=False).then_inc(pv_done, 1)
            nc.tensor.matmul(misc[:, 0:P], zeros16[:], ident16[:], start=True, stop=True).then_inc(folded_ready, 1)
            pe.wait_ge(stack_in[0], STACK_DMAS)
            for n in range(NPIECE):
                form_piece(0, 0, n)
            pe.wait_ge(max_found, 1)
            nc.tensor.transpose(maxT, neg_max[:], ident32[:]).then_inc(maxT_ready, 1)

            def scores_half(h, slot, s, half):
                qb, k0 = QUADS[s]
                pe.wait_ge(exp_done, h * (2 * NQUAD) + (2 * s + half + 1))
                at = 0
                for j in (2 * half, 2 * half + 1):
                    w = half_width[s][half][j % 2]
                    kt = k0 + j
                    diagonal = k0 == qb * TPQ
                    mm = nc.tensor.matmul(scores[half][:, at:at + w], kstack[0:MROW + 1, slot, kt * P:(kt + 1) * P],
                                          qstack[0:MROW + 1, slot, (qb + 1) * QB - w:(qb + 1) * QB],
                                          start=True, stop=not diagonal)
                    if diagonal:
                        mm = nc.tensor.matmul(scores[half][:, at:at + P], ident16[:], hide_queries[:],
                                              start=False, stop=True)
                    at += w
                mm.then_inc(scores_ready, 1)

            def weigh(h, slot, s, exps):
                qb, k0 = QUADS[s]
                pe.wait_ge(exp_done, exps)
                first, last = k0 == 0, s == LAST_QUAD[qb]
                if first:
                    pe.wait_ge(acc_copied, h * NQ + (qb + 1))
                    pe.wait_ge(v_ready, h + 1)
                if qb == 0:
                    nc.tensor.matmul(acc[:], zeros16[:], ones16[:], start=True, stop=False)
                for j in range(TPQ):
                    w = half_width[s][j // 2][j % 2]
                    at = j // 2 * 2 * QB + (0 if j % 2 == 0 else half_width[s][j // 2][0])
                    mm = nc.tensor.matmul(acc[VW * j:VW * (j + 1), QB - w:QB], v_head[:, slot, k0 + j],
                                          probs[:, s % 2, at:at + w], start=first and qb > 0, stop=last)
                mm.then_inc(pv_done, 1)

            def fold_block(n, qb):
                pe.wait_ge(acc_copied, n)
                pe.wait_ge(normed, n)
                for t in range(TPQ):
                    mm = nc.tensor.matmul(folded[:, t], acc_sb[:, qb % 2, t * P:(t + 1) * P], fold[:],
                                          start=True, stop=True)
                mm.then_inc(folded_ready, 1)


            def head(i, j, last):
                h = i + j
                slot, next_slot = j, (j + 1) % NSTACK
                piece_n = 0
                pe.wait_ge(max_in, h * 16 + 16)
                if not last:
                    pe.wait_ge(stack_in[next_slot], (i // NSTACK + 1 + (j + 1) // NSTACK) * STACK_DMAS
                               if isinstance(i, int) else i * (STACK_DMAS // NSTACK) + (1 + (j + 1) // NSTACK) * STACK_DMAS)
                for s in range(NQUAD):
                    todo = 0 if last else PIECES_OF_QUAD[s]

                    def some(m):
                        nonlocal piece_n, todo
                        for _ in range(min(m, todo)):
                            form_piece(h + 1, next_slot, piece_n)
                            piece_n += 1
                            todo -= 1

                    scores_half(h, slot, s, 0)
                    some(2)
                    scores_half(h, slot, s, 1)
                    some(2)
                    if s == NQUAD - 1 and not last:
                        pe.wait_ge(max_found, h + 2)
                        pe.wait_ge(normed, h * NQ + (NQ + 1))
                        nc.tensor.transpose(maxT, neg_max[:], ident32[:]).then_inc(maxT_ready, 1)
                    if s == 0:
                        weigh(None, (j + 1) % 2, NQUAD - 1, h * (2 * NQUAD) + 2)
                    else:
                        weigh(h, j % 2, s - 1, h * (2 * NQUAD) + (2 * s + 2))
                    some(5)
                    if s == 1:
                        fold_block(h * NQ + 1, NQ - 1)
                    for b in range(NQ - 1):
                        if s == LAST_QUAD[b] + 2:
                            fold_block(h * NQ + (b + 2), b)

            turns(pe, head)
            weigh(None, (H - 1) % 2, NQUAD - 1, H * 2 * NQUAD + 2)
            fold_block(H * NQ + 1, NQ - 1)

        @block.vector
        def _(dve):
            dve.wait_ge(const_done, 7)
            nc.vector.memset(attn[:, :, 0:DH], 0.0).then_inc(normed, 1)
            def reduce_piece(h, n):
                t, c, w = PIECES[n]
                dve.wait_ge(piece_ready, h * NPIECE + (n + 1))
                nc.vector.tensor_reduce(out=partial[:, t, c // QB:c // QB + 1], in_=piece[n % 2][:, 0:w],
                                        axis=X, op=ALU.max).then_inc(piece_done, 1)

            def find_max(h):
                dve.wait_ge(piece_done, h * NPIECE + NPIECE)
                nc.vector.tensor_reduce(out=neg_max[:], in_=partial[:], axis=X, op=ALU.max, negate=True).then_inc(max_found, 1)

            def copy_max(h, first):
                dve.wait_ge(maxT_ready, h + 1)
                if not first:
                    dve.wait_ge(max_in, h * 16)
                nc.vector.tensor_copy(max_row[:], maxT).then_inc(max_row_ready, 1)

            def norm_block(h, n, qb, pad):
                dve.wait_ge(folded_ready, n + 1)
                nc.vector.reciprocal(inv[:], folded[:, :, DH:DH + 1]).then_inc(inv_ready, 1)
                dve.wait_ge(inv_ready, n)
                nc.vector.tensor_tensor(attn[:, qb * TPQ:(qb + 1) * TPQ, bass.ds(h * DH + pad * DH, DH)],
                                        folded[:, :, 0:DH], inv[:].broadcast_to([P, TPQ, DH]), ALU.mult).then_inc(normed, 1)

            for n in range(NPIECE):
                reduce_piece(0, n)
            find_max(0)
            copy_max(0, True)

            def head(i, j, last):
                h = i + j
                piece_n = 0
                for s in range(NQUAD):
                    if not last:
                        for _ in range(PIECES_OF_QUAD[s]):
                            reduce_piece(h + 1, piece_n)
                            piece_n += 1
                    if s == NQUAD - 2 and not last:
                        find_max(h + 1)
                    for b in range(NQ - 1):
                        if s == LAST_QUAD[b] + 2:
                            norm_block(h, h * NQ + (b + 2), b, 1)
                    if s == 1:
                        norm_block(h, h * NQ + 1, NQ - 1, 0)
                    if s == NQUAD - 1 and not last:
                        copy_max(h + 1, False)

            turns(dve, head)
            norm_block(H, H * NQ + 1, NQ - 1, 0)


LAST_QUAD = [max(s for s, (b, _) in enumerate(QUADS) if b == qb) for qb in range(NQ)]
STACK_DMAS = 16 * 2 * SLOTS


def turns(engine, head):
    with engine.Fori(0, H // NSTACK - 1) as k:
        for j in range(NSTACK):
            head(k * NSTACK, j, False)
    for j in range(NSTACK):
        head(H - NSTACK, j, j == NSTACK - 1)


def mix(nc, f32, f16, u32, ALU, ACT, res, attn, wo_split, xm, gate_split, bo_rows, ident32,
        eps_col, x2T, gates):
    es = ExitStack()
    with es:
        def sb(name, shape, dt):
            return es.enter_context(nc.sbuf_tensor(name, shape, dt))

        def sem(name):
            return es.enter_context(nc.semaphore(name))

        yT = sb("yT", [P, 2, 2, DC, QB], f16)
        yT32 = sb("yT32", [P, 2, DC, QB], f32)
        summed = sb("summed", [P, 2, TPQ, D], f32)
        stats = sb("stats", [P, 2, TPQ, 6], f32)
        mean_var = sb("mean_var", [P, 2, TPQ, 2], f32)
        sd = sb("sd", [P, 2, TPQ], f32)
        rstd = sb("rstd", [P, 2, TPQ], f32)
        logits = sb("logits", [P, NT, NE], f32)
        top = sb("top", [P, NT, 8], f32)
        top_at = sb("top_at", [P, NT, 8], u32)
        at32 = sb("at32", [P, NT, 2], f32)
        gap = sb("gap", [P, NT, 1], f32)
        gap_exp = sb("gap_exp", [P, NT, 1], f32)
        den = sb("den", [P, NT, 1], f32)
        pair = sb("pair", [P, NT, 2], f32)
        experts = sb("experts", [P, 1, NE], f32)
        hot = sb("hot", [P, 2, NT, NE], f32)
        tps = [es.enter_context(nc.psum_tensor(f"turned{i}", [P, DC, QB], f32)) for i in range(2)]
        ops = [es.enter_context(nc.psum_tensor(f"ops{i}", [P, TPQ, D], f32)) for i in range(2)]

        biased, turned, hi_done, lo_done = sem("biased"), sem("turned"), sem("hi_done"), sem("lo_done")
        product, added, stats_done, aggr_done = sem("product"), sem("added"), sem("stats_done"), sem("aggr_done")
        sd_done, rstd_done, ln_done = sem("sd_done"), sem("rstd_done"), sem("ln_done")
        logits_done, top_done, vstep, exp_done, experts_ready = sem("logits_done"), sem("top_done"), sem("vstep"), sem("exp_done"), sem("experts_ready")
        NI = 3 * NQ
        NM = 2 * NQ
        block = es.enter_context(nc.Block())

        def halves(n):
            if n < NM:
                return yT[:, n % 2]
            g = n - NM
            return x2T[:, :, :, g * QB:(g + 1) * QB]

        def los(n):
            return n + 1 if n < NQ else n + 1 - NQ

        @block.tensor
        def _(pe):
            def wait_read(n):
                pe.wait_ge(hi_done, n + 1)
                if n // NQ != 1:
                    pe.wait_ge(lo_done, los(n))

            def turn(n):
                step, g = divmod(n, NQ)
                if n >= 2:
                    wait_read(n - 2)
                if step:
                    pe.wait_ge(ln_done, (n - NQ + 1))
                for c in range(DC):
                    for t in range(TPQ):
                        tile = g * TPQ + t
                        src = attn[:, tile, DH + c * P:DH + (c + 1) * P] if step == 0 else res[:, tile, c * P:(c + 1) * P]
                        mm = nc.tensor.transpose(tps[n % 2][:, c, t * P:(t + 1) * P], src, ident32[:])
                mm.then_inc(turned, 1)

            def multiply(n):
                step = n // NQ
                w = (wo_split, xm, gate_split)[step]
                width = D if step < 2 else NE
                wait_read(n)
                if n >= 2:
                    pe.wait_ge(added, n - 1)
                for t in range(TPQ):
                    if step == 1:
                        for k in range(DC):
                            mm = nc.tensor.matmul(ops[n % 2][:, t], yT32[:, n % 2, k, t * P:(t + 1) * P], w[:, k],
                                                  start=(k == 0), stop=(k == DC - 1))
                        continue
                    m = 0
                    for k in range(DC):
                        for a, b in ((0, 0), (0, 1), (1, 0)):
                            mm = nc.tensor.matmul(ops[n % 2][:, t, 0:width], halves(n)[:, a, k, t * P:(t + 1) * P],
                                                  w[:, b, k], start=(m == 0), stop=(m == 5))
                            m += 1
                mm.then_inc(product, 1)

            turn(0)
            for n in range(NI):
                if n + 1 < NI:
                    turn(n + 1)
                multiply(n)

        @block.scalar
        def _(act):
            def hi(n):
                act.wait_ge(turned, n + 1)
                if 2 <= n < NM:
                    act.wait_ge(product, n - 1)
                nc.scalar.activation(yT32[:, n % 2] if n // NQ == 1 else halves(n)[:, 0], tps[n % 2][:],
                                     ACT.Copy).then_inc(hi_done, 1)

            hi(0)
            for n in range(NI):
                if n + 1 < NI:
                    hi(n + 1)
                if n < NM:
                    act.wait_ge(aggr_done, TPQ * (n + 1))
                    if n >= 2:
                        act.wait_ge(rstd_done, n - 1)
                    nc.scalar.activation(sd[:, n % 2], mean_var[:, n % 2, :, 1], ACT.Sqrt, bias=eps_col[:]).then_inc(sd_done, 1)
            act.wait_ge(vstep, 1)
            nc.scalar.activation(gap_exp[:], gap[:], ACT.Exp).then_inc(exp_done, 1)

        @block.gpsimd
        def _(pool):
            for g in range(NQ):
                nc.gpsimd.tensor_tensor(res[:, g * TPQ:(g + 1) * TPQ], res[:, g * TPQ:(g + 1) * TPQ],
                                        bo_rows[:].rearrange("p (o d) -> p o d", o=1).broadcast_to([P, TPQ, D]), ALU.add).then_inc(biased, 1)
            nc.gpsimd.iota(experts[:], pattern=[[0, 1], [1, NE]], base=0, channel_multiplier=0,
                           allow_small_or_imprecise_dtypes=True).then_inc(experts_ready, 1)
            for n in range(NM):
                pool.wait_ge(rstd_done, n + 1)
                pool.wait_ge(added, n + 1)
                g = n % NQ
                for t in range(TPQ):
                    ln = nc.gpsimd.tensor_scalar(res[:, g * TPQ + t], summed[:, n % 2, t], mean_var[:, n % 2, t, 0:1],
                                                 rstd[:, n % 2, t:t + 1], ALU.subtract, ALU.mult)
                ln.then_inc(ln_done, 1)

        @block.vector
        def _(dve):
            def lo(n):
                if n // NQ == 1:
                    return
                dve.wait_ge(hi_done, n + 1)
                nc.vector.tensor_tensor(halves(n)[:, 1], tps[n % 2][:], halves(n)[:, 0], ALU.subtract).then_inc(lo_done, 1)

            lo(0)
            for n in range(NI):
                if n + 1 < NI:
                    lo(n + 1)
                step, g = divmod(n, NQ)
                tiles = slice(g * TPQ, (g + 1) * TPQ)
                dve.wait_ge(product, n + 1)
                if step == 2:
                    nc.vector.tensor_copy(logits[:, tiles], ops[n % 2][:, :, 0:NE]).then_inc(added, 1)
                    continue
                if step == 0:
                    dve.wait_ge(biased, g + 1)
                else:
                    dve.wait_ge(ln_done, n - NQ + 1)
                if n >= 2:
                    dve.wait_ge(ln_done, n - 1)
                nc.vector.tensor_tensor(summed[:, n % 2], ops[n % 2][:], res[:, tiles], ALU.add).then_inc(added, 1)
                dve.wait_ge(added, n + 1)
                if n >= 2:
                    dve.wait_ge(sd_done, n - 1)
                for t in range(TPQ):
                    nc.vector.bn_stats(stats[:, n % 2, t], summed[:, n % 2, t]).then_inc(stats_done, 1)
                for t in range(TPQ):
                    dve.wait_ge(stats_done, n * TPQ + t + 1)
                    nc.vector.bn_aggr(mean_var[:, n % 2, t], stats[:, n % 2, t]).then_inc(aggr_done, 1)
                dve.wait_ge(sd_done, n + 1)
                nc.vector.reciprocal(rstd[:, n % 2], sd[:, n % 2]).then_inc(rstd_done, 1)
            dve.wait_ge(added, NI)
            for t in range(NT):
                nc.vector.max(top[:, t], logits[:, t]).then_inc(top_done, 1)
            for t in range(NT):
                dve.wait_ge(top_done, t + 1)
                nc.vector.max_index(top_at[:, t], top[:, t], logits[:, t]).then_inc(top_done, 1)
            nc.vector.tensor_tensor(gap[:], top[:, :, 1:2], top[:, :, 0:1], ALU.subtract).then_inc(vstep, 1)
            dve.wait_ge(top_done, 2 * NT)
            nc.vector.tensor_copy(at32[:], top_at[:, :, 0:2]).then_inc(vstep, 1)
            dve.wait_ge(exp_done, 1)
            nc.vector.tensor_scalar(den[:], gap_exp[:], 1.0, WSCALE, ALU.add, ALU.mult).then_inc(vstep, 1)
            dve.wait_ge(vstep, 3)
            nc.vector.reciprocal(pair[:, :, 0:1], den[:]).then_inc(vstep, 1)
            dve.wait_ge(vstep, 4)
            nc.vector.tensor_tensor(pair[:, :, 1:2], pair[:, :, 0:1], gap_exp[:], ALU.mult).then_inc(vstep, 1)
            dve.wait_ge(experts_ready, 1)
            for r in range(2):
                nc.vector.tensor_tensor(hot[:, r], experts[:].broadcast_to([P, NT, NE]),
                                        at32[:, :, r:r + 1].broadcast_to([P, NT, NE]), ALU.is_equal).then_inc(vstep, 1)
            dve.wait_ge(vstep, 7)
            for r in range(2):
                nc.vector.tensor_tensor(hot[:, r], hot[:, r], pair[:, :, r:r + 1].broadcast_to([P, NT, NE]),
                                        ALU.mult).then_inc(vstep, 1)
            nc.vector.memset(gates[:, :, NE:NE + 1], 1.0 / WSCALE).then_inc(vstep, 1)
            dve.wait_ge(vstep, 10)
            nc.vector.tensor_tensor(gates[:, :, 0:NE], hot[:, 0], hot[:, 1], ALU.add).then_inc(vstep, 1)


def feed_forward(nc, f32, f16, ALU, ACT, res, x2T, gates, eps_col, w1T, w2T, out):
    es = ExitStack()
    with es:
        def sb(name, shape, dt):
            return es.enter_context(nc.sbuf_tensor(name, shape, dt))

        def sem(name):
            return es.enter_context(nc.semaphore(name))

        NX = NE + 1
        w1_in = sb("w1_in", [P, DC, HID], f32)
        w2_in = sb("w2_in", [P, HC, D], f32)
        w1 = sb("w1", [P, 2, 2, DC, HID], f16)
        w2 = sb("w2", [P, 2, 2, HC, D], f16)
        hid32 = sb("hid32", [P, 2, QB], f32)
        hid = sb("hid", [P, 2, 2, HC, QB], f16)
        stats = sb("f_stats", [P, NT, 6], f32)
        mean_var = sb("f_mean_var", [P, NT, 2], f32)
        sd = sb("f_sd", [P, NT], f32)
        rstd = sb("f_rstd", [P, NT], f32)
        final = sb("final", [P, NT, D], f32)
        hps = [es.enter_context(nc.psum_tensor(f"hps{i}", [P, QB], f32)) for i in range(2)]
        yps = [es.enter_context(nc.psum_tensor(f"yps{i}", [P, TPQ, D], f32)) for i in range(2)]

        w1_loaded, w2_loaded, w_hi, w_lo = sem("w1_loaded"), sem("w2_loaded"), sem("w_hi"), sem("w_lo")
        h_ready, silu_done, hid_hi, hid_lo = sem("h_ready"), sem("silu_done"), sem("hid_hi"), sem("hid_lo")
        y_ready, y_added = sem("y_ready"), sem("y_added")
        stats_done, aggr_done, sd_done, rstd_done, final_done, stored = (
            sem("f_stats_done"), sem("f_aggr_done"), sem("f_sd_done"), sem("f_rstd_done"), sem("final_done"), sem("stored"))
        block = es.enter_context(nc.Block())

        def per_expert(engine, body):
            with engine.Fori(0, NE // 2) as k:
                for j in range(2):
                    body(k * 2, j, False)
            body(NE, 0, True)

        @block.sync
        def _(sp):
            def load(e):
                sp.dma_start(w1_in[:], w1T[bass.ds(e, 1)].rearrange("o (c p) h -> p (o c) h", p=P)).then_inc(w1_loaded, 16)
                sp.dma_start(w2_in[:], w2T[bass.ds(e, 1)].rearrange("o (c p) d -> p (o c) d", p=P)).then_inc(w2_loaded, 16)

            load(0)
            with sp.Fori(1, NX) as e:
                sp.wait_ge(w_lo, e * 2)
                load(e)
            for b in range(NQ):
                sp.wait_ge(final_done, TPQ * (b + 1))
                sp.dma_start(out[b * QB:(b + 1) * QB, :].rearrange("(t p) d -> p t d", p=P),
                             final[:, b * TPQ:(b + 1) * TPQ]).then_inc(stored, 16)
            sp.wait_ge(stored, 16 * NQ)

        @block.gpsimd
        def _(pool):
            for e in range(NX):
                slot = e % 2
                if e >= 2:
                    pool.wait_ge(y_ready, e * NQ - NQ)
                pool.wait_ge(w1_loaded, e * 16 + 16)
                nc.gpsimd.tensor_scalar(w1[:, slot, 0], w1_in[:], WSCALE, None, ALU.mult).then_inc(w_hi, 1)
                pool.wait_ge(w2_loaded, e * 16 + 16)
                nc.gpsimd.tensor_scalar(w2[:, slot, 0], w2_in[:], WSCALE, None, ALU.mult).then_inc(w_hi, 1)


        @block.scalar
        def _(act):
            def activate(n, b):
                for j in range(HC):
                    act.wait_ge(h_ready, n * HC + (j + 1))
                    if not (isinstance(n, int) and n == 0 and j < 2):
                        act.wait_ge(hid_lo, n * HC + (j - 1))
                    nc.scalar.activation(hid32[:, j % 2], hps[j % 2][:], ACT.Silu, scale=1.0 / WSCALE).then_inc(silu_done, 1)
                    if j == 0 and not (isinstance(n, int) and n < 2):
                        act.wait_ge(y_ready, n - 1)
                    act.wait_ge(silu_done, n * HC + (j + 1))
                    nc.scalar.activation(hid[:, b % 2, 0, j], hid32[:, j % 2], ACT.Copy).then_inc(hid_hi, 1)

            activate(0, 0)

            def expert(i, j, last):
                for b in range(NQ):
                    if not (last and b == NQ - 1):
                        activate(i * NQ + (j * NQ + b + 1), b + 1)

            per_expert(act, expert)
            for b in range(NQ):
                act.wait_ge(aggr_done, TPQ * (b + 1))
                nc.scalar.activation(sd[:, b * TPQ:(b + 1) * TPQ], mean_var[:, b * TPQ:(b + 1) * TPQ, 1], ACT.Sqrt,
                                     bias=eps_col[:]).then_inc(sd_done, 1)

        @block.tensor
        def _(pe):
            def widen(e, slot, n, b):
                if b == 0:
                    pe.wait_ge(w_hi, e * 2 + 2)
                    pe.wait_ge(w_lo, e * 2 + 2)
                for j in range(HC):
                    if not (isinstance(n, int) and n == 0 and j < 2):
                        pe.wait_ge(silu_done, n * HC + (j - 1))
                    m = 0
                    for k in range(DC):
                        for a, c in ((0, 0), (0, 1), (1, 0)):
                            mm = nc.tensor.matmul(hps[j % 2][:], w1[:, slot, a, k, j * P:(j + 1) * P],
                                                  x2T[:, c, k, b * QB:(b + 1) * QB], start=(m == 0), stop=(m == 5))
                            m += 1
                    mm.then_inc(h_ready, 1)

            def narrow(slot, n, b):
                pe.wait_ge(hid_hi, n * HC + HC)
                pe.wait_ge(hid_lo, n * HC + HC)
                for t in range(TPQ):
                    m = 0
                    for j in range(HC):
                        for a, c in ((0, 0), (0, 1), (1, 0)):
                            mm = nc.tensor.matmul(yps[b % 2][:, t], hid[:, b % 2, a, j, t * P:(t + 1) * P],
                                                  w2[:, slot, c, j], start=(m == 0), stop=(m == 3 * HC - 1))
                            m += 1
                mm.then_inc(y_ready, 1)

            widen(0, 0, 0, 0)

            def expert(i, j, last):
                for b in range(NQ):
                    n = i * NQ + (j * NQ + b)
                    if b < NQ - 1:
                        widen(i + j, j, n + 1, b + 1)
                    elif not last:
                        widen(i + j + 1, 1 - j, n + 1, 0)
                    narrow(j, n, b)

            per_expert(pe, expert)

        @block.vector
        def _(dve):
            def weights(e, which, slot):
                dve.wait_ge(w_hi, e * 2 + (which + 1))
                src, dst = ((w1_in, w1), (w2_in, w2))[which]
                nc.vector.scalar_tensor_tensor(out=dst[:, slot, 1], in0=src[:], scalar=WSCALE, in1=dst[:, slot, 0],
                                               op0=ALU.mult, op1=ALU.subtract).then_inc(w_lo, 1)

            def second_halves(n, b):
                for j in range(HC):
                    dve.wait_ge(hid_hi, n * HC + (j + 1))
                    nc.vector.tensor_tensor(hid[:, b % 2, 1, j], hid32[:, j % 2], hid[:, b % 2, 0, j], ALU.subtract).then_inc(hid_lo, 1)

            nc.vector.memset(stats[:, 0], 0.0).then_inc(y_added, 1)
            weights(0, 0, 0)
            weights(0, 1, 0)
            second_halves(0, 0)

            def expert(i, j, last):
                for b in range(NQ):
                    n = i * NQ + (j * NQ + b)
                    if not (last and b == NQ - 1):
                        second_halves(n + 1, b + 1)
                    dve.wait_ge(y_ready, n + 1)
                    dve.wait_ge(y_added, n * TPQ + 1)
                    for t in range(TPQ):
                        tile = b * TPQ + t
                        nc.vector.scalar_tensor_tensor(out=res[:, tile], in0=yps[b % 2][:, t],
                                                       scalar=gates[:, tile, NE:NE + 1] if last else gates[:, tile, bass.ds(i + j, 1)],
                                                       in1=res[:, tile], op0=ALU.mult, op1=ALU.add).then_inc(y_added, 1)
                    if b < 2 and not last:
                        weights(i + j + 1, b, 1 - j)

            per_expert(dve, expert)
            for t in range(NT):
                dve.wait_ge(y_added, NX * NQ * TPQ - NT + t + 2)
                nc.vector.bn_stats(stats[:, t], res[:, t]).then_inc(stats_done, 1)
            for t in range(NT):
                dve.wait_ge(stats_done, t + 1)
                nc.vector.bn_aggr(mean_var[:, t], stats[:, t]).then_inc(aggr_done, 1)
            for b in range(NQ):
                tiles = slice(b * TPQ, (b + 1) * TPQ)
                dve.wait_ge(sd_done, b + 1)
                nc.vector.reciprocal(rstd[:, tiles], sd[:, tiles]).then_inc(rstd_done, 1)
                dve.wait_ge(rstd_done, b + 1)
                for t in range(b * TPQ, (b + 1) * TPQ):
                    nc.vector.tensor_scalar(final[:, t], res[:, t], mean_var[:, t, 0:1], rstd[:, t:t + 1],
                                            ALU.subtract, ALU.mult).then_inc(final_done, 1)


def kernel(**inputs):
    import numpy as np
    import concourse.bacc as bacc
    from concourse import mybir
    from concourse.bass_utils import run_bass_kernel_spmd

    a = {k: np.asarray(v) for k, v in inputs.items()}
    arrays = {
        "x": a["x"][0],
        "xT": a["x"][0].T,
        "ctx_n": a["ctx_1024"][0],
        "ctxT": a["ctx_1024"][0].T,
        "wq": a["L0_attn_wq"], "wk": a["L0_attn_wk"], "wv": a["L0_attn_wv"], "wo": a["L0_attn_wo"],
        "b_qk": np.stack([a["L0_attn_bq"], a["L0_attn_bk"]]).reshape(2, DC, P).transpose(2, 0, 1),
        "bv": a["L0_attn_bv"], "bo": a["L0_attn_bo"],
        "lm": a["L0_xattn_learnable_matrix"],
        "w1T": np.concatenate([a["L0_ffn_experts_w1"], a["L0_ffn_shared_w1"][None]]).transpose(0, 2, 1),
        "w2T": np.concatenate([a["L0_ffn_experts_w2"], a["L0_ffn_shared_w2"][None]]).transpose(0, 2, 1),
        "gT": a["L0_ffn_gate_w"].T,
    }
    arrays = {k: np.ascontiguousarray(v) for k, v in arrays.items()}
    nc = bacc.Bacc("TRN2", target_bir_lowering=False, num_devices=1)
    args = {k: nc.dram_tensor(k, v.shape, mybir.dt.from_np(v.dtype), kind="ExternalInput").ap() for k, v in arrays.items()}
    out = nc.dram_tensor("out", (S, D), mybir.dt.float32, kind="ExternalOutput").ap()
    decoder_layer(nc, out=out, **args)
    r = run_bass_kernel_spmd(nc, [arrays], core_ids=[0])
    return r.results[0]["out"].reshape(1, S, D)
```

```python
import numpy as np
import concourse.bass as bass
from concourse import mybir
from contextlib import ExitStack

S = 2048
D = 256
H = 16
DH = D // H
CTX = 1601
HID = 1024
NE = 8
P = 128
DC = D // P
NT = S // P
QB = 512
NQ = S // QB
TPQ = QB // P
HC = HID // P
CT = (CTX + P - 1) // P
CLAST = CTX - (CT - 1) * P
EPS = 1e-5
NX = NE + 1
WE = 2 * DC * HID
WU = NX * WE // H
MAX_TILES = 2 * NT + NE - 1
NSLOT = MAX_TILES * P
NEG = -1.0e30
WSCALE = 256.0

SLOTS = 4
MROW = 96
ZROW = SLOTS * DH
NSTACK = 4

QUADS = [(qb, 4 * k) for qb in range(NQ) for k in range(qb + 1)]
NQUAD = len(QUADS)
PIECES = [(t, c, min(QB, (t + 1) * P - c)) for t in range(NT) for c in range(0, (t + 1) * P, QB)]
NPIECE = len(PIECES)
VW = 32
LAST_QUAD = [max(s for s, (b, _) in enumerate(QUADS) if b == qb) for qb in range(NQ)]
STACK_DMAS = 16 * 2 * SLOTS
NRING = 3


PLACES = {4: (0, 1, 1, 2), 5: (0, 1, 1, 2, 2)}


def ring_order(last):
    quads = [[[], [], []] for _ in range(NQUAD)]
    if not last:
        load = [[0, []] for _ in range(NQUAD - 2)]
        for n in sorted(range(NPIECE), key=lambda n: -PIECES[n][2]):
            least = min(load, key=lambda x: x[0])
            least[0] += PIECES[n][2] + 64
            least[1].append(n)
        for s, (_, mine) in enumerate(load):
            for k, n in enumerate(mine):
                quads[s][PLACES[len(mine)][k]].append(("piece", n))
        quads[NQUAD - 2][1].append(("max", 0))
    quads[1][1].insert(0, ("fold", NQ - 1))
    for b in range(NQ - 1):
        quads[LAST_QUAD[b] + 2][1].insert(0, ("fold", b))
    return quads


RING = ring_order(False)
RING_OF_HEAD = [x for quad in RING for place in quad for x in place]
RING_OF_LAST = [x for quad in ring_order(True) for place in quad for x in place]
NENTRY = len(RING_OF_HEAD)
NFIRST = NPIECE + 1
NENTRIES = NFIRST + (H - 1) * NENTRY + len(RING_OF_LAST) + 1
assert NENTRY % NRING == 0


def entries_before(h, kind, n, last):
    order = RING_OF_LAST if last else RING_OF_HEAD
    return h * NENTRY + (NFIRST + order.index((kind, n)) + 1)


def decoder_layer(nc, x, xT, ctx_n, ctxT, wq, wk, wv, wo, b_qk, bv, bo, lm, w_all, gT, out):
    f32, f16, bf16, u32 = mybir.dt.float32, mybir.dt.float16, mybir.dt.bfloat16, mybir.dt.uint32
    ALU = mybir.AluOpType
    ACT = mybir.ActivationFunctionType
    X = mybir.AxisListType.X

    q_split = nc.dram_tensor("q_split", (2, D, S), f16).ap()
    k_split = nc.dram_tensor("k_split", (2, D, S), f16).ap()
    w_split_d = nc.dram_tensor("w_split_d", (2, P, NX * WE), f16).ap()
    sorted_x = nc.dram_tensor("sorted_x", (NSLOT, D), f32).ap()
    sorted_y = nc.dram_tensor("sorted_y", (NSLOT, D), f32).ap()

    whole = ExitStack()
    with whole:
        def keep(name, shape, dt):
            return whole.enter_context(nc.sbuf_tensor(name, shape, dt))

        res = keep("res", [P, NT, D], f32)
        wo_split = keep("wo_split", [P, 2, DC, D], f16)
        xm = keep("xm", [P, DC, D], f32)
        gate_split = keep("gate_split", [P, 2, DC, NE], f16)
        bo_rows = keep("bo_rows", [P, D], f32)
        ident32 = keep("ident32", [P, P], f32)
        eps_col = keep("eps_col", [P, 1], f32)
        weight_of = keep("weight_of", [P, NT, 2], f32)
        slot_of = keep("slot_of", [P, 2, NT], u32)
        column_of = keep("column_of", [P, MAX_TILES], u32)
        with ExitStack() as two:
            attn = two.enter_context(nc.sbuf_tensor("attn", [P, NT, DH + D], f32))
            with ExitStack() as three:
                values = three.enter_context(nc.sbuf_tensor("values", [P, H, NT, VW], f32))
                qstack = three.enter_context(nc.sbuf_tensor("qstack", [P, NSTACK, S], f16))
                kstack = three.enter_context(nc.sbuf_tensor("kstack", [P, NSTACK, S], f16))
                project(nc, f32, f16, ALU, ACT, x, xT, ctx_n, ctxT, wq, wk, wv, wo, b_qk, bv, bo, lm, gT,
                        q_split, k_split, sorted_x, res, wo_split, xm, gate_split, bo_rows, ident32, eps_col,
                        attn, values, qstack, kstack)
                attend(nc, f32, f16, bf16, ALU, ACT, X, q_split, k_split, w_all, w_split_d, ident32, attn, values,
                       qstack, kstack)
            with ExitStack() as four:
                weights = four.enter_context(nc.sbuf_tensor("weights", [P, 2, NX * WE], f16))
                shared_in = four.enter_context(nc.semaphore("shared_in"))
                routed_in = four.enter_context(nc.semaphore("routed_in"))
                mix(nc, f32, f16, u32, ALU, ACT, X, res, attn, wo_split, xm, gate_split, bo_rows, ident32,
                    eps_col, w_split_d, weights, shared_in, routed_in, weight_of, slot_of, column_of)
                feed_forward(nc, f32, f16, ALU, ACT, res, attn, ident32, eps_col, weights, shared_in, routed_in,
                             weight_of, slot_of, column_of, sorted_x, sorted_y, out)


def project(nc, f32, f16, ALU, ACT, x, xT, ctx_n, ctxT, wq, wk, wv, wo, b_qk, bv, bo, lm, gT,
            q_split, k_split, sorted_x, res, wo_split, xm, gate_split, bo_rows, ident32, eps_col,
            attn, values, qstack, kstack):
    es = ExitStack()
    with es:
        def sb(name, shape, dt):
            return es.enter_context(nc.sbuf_tensor(name, shape, dt))

        def sem(name):
            return es.enter_context(nc.semaphore(name))

        xT_sb = sb("xT_sb", [P, DC, S], f32)
        x_split = sb("x_split", [P, 2, DC, S], f16)
        w_in = sb("w_in", [P, 4, DC, D], f32)
        w_split = sb("w_split", [P, 3, 2, DC, D], f16)
        g_in = sb("g_in", [P, DC, NE], f32)
        lm_sb = sb("lm_sb", [P, DC, D], f32)
        ctxT_sb = sb("ctxT_sb", [P, DC, CTX], f32)
        ctx_sb = sb("ctx_sb", [P, CT, D], f32)
        t_act = sb("t_act", [P, CT, D], f32)
        b_cols = sb("b_cols", [P, 2, DC], f32)
        bq_scaled = sb("bq_scaled", [P, DC], f32)
        bv_rows = sb("bv_rows", [P, D], f32)
        qk32 = sb("qk32", [P, 2, QB], f32)
        zero_rows = sb("zero_rows", [P, 1, D], f32)
        qk16 = sb("qk16", [P, 4, 2, QB], f16)
        proj = [es.enter_context(nc.psum_tensor(f"proj{i}", [P, QB], f32)) for i in range(2)]
        vps = [es.enter_context(nc.psum_tensor(f"vps{i}", [P, D], f32)) for i in range(2)]
        tps = [es.enter_context(nc.psum_tensor(f"tps{i}", [P, D], f32)) for i in range(2)]
        mps = es.enter_context(nc.psum_tensor("mps", [P, DC, D], f32))

        xT_in, w_loaded, small_in, ctx_in, res_in = sem("xT_in"), sem("w_loaded"), sem("small_in"), sem("ctx_in"), sem("res_in")
        rows_zeroed, rows_stored = sem("rows_zeroed"), sem("rows_stored")
        pool_zeroed, pool_done, stacks_set = sem("pool_zeroed"), sem("pool_done"), sem("stacks_set")
        hi_done, split_done = sem("hi_done"), sem("split_done")
        qk_ready, qk_copied, qk_hi, qk_lo = sem("qk_ready"), sem("qk_copied"), sem("qk_hi"), sem("qk_lo")
        qk_stored = [sem(f"qk_stored{n}") for n in range(4)]
        bias_scaled = sem("bias_scaled")
        v_ready, v_done = sem("v_ready"), sem("v_done")
        t_ready, t_done, m_ready, m_copied = sem("t_ready"), sem("t_done"), sem("m_ready"), sem("m_copied")

        block = es.enter_context(nc.Block())

        @block.sync
        def _(sp):
            for c in range(DC):
                sp.dma_start(xT_sb[:, c, :], xT[c * P:(c + 1) * P, :]).then_inc(xT_in, 16)
            for n, w in enumerate((wq, wk, wv, wo)):
                sp.dma_start(w_in[:, n], w.rearrange("(c p) n -> p c n", p=P)).then_inc(w_loaded, 16)
            sp.dma_start(res[:], x.rearrange("(t p) d -> p t d", p=P)).then_inc(res_in, 16)
            for q in range(NQ):
                for n in range(4):
                    sp.wait_ge(qk_lo, 4 * q + n + 1)
                    what, c = n // 2, n % 2
                    for half in range(2):
                        sp.dma_start((q_split, k_split)[what][half, c * P:(c + 1) * P, q * QB:(q + 1) * QB],
                                     qk16[:, n, half, :]).then_inc(qk_stored[n], 16)
            sp.wait_ge(rows_zeroed, 1)
            sp.dma_start(sorted_x.rearrange("(t p) d -> p t d", p=P),
                         zero_rows[:].broadcast_to([P, MAX_TILES, D])).then_inc(rows_stored, 16)
            sp.wait_ge(rows_stored, 16)
            sp.wait_ge(res_in, 16)
            for n in range(4):
                sp.wait_ge(qk_stored[n], 16 * 2 * NQ)

        @block.scalar
        def _(act):
            nc.scalar.dma_start(b_cols[:], b_qk).then_inc(small_in, 16)
            nc.scalar.dma_start(g_in[:], gT.rearrange("(c p) n -> p c n", p=P)).then_inc(small_in, 16)
            nc.scalar.dma_start(bo_rows[:], bo.partition_broadcast(P)).then_inc(small_in, 16)
            nc.scalar.dma_start(bv_rows[:], bv.partition_broadcast(P)).then_inc(small_in, 16)
            for c in range(DC):
                nc.scalar.dma_start(ctxT_sb[:, c, :], ctxT[c * P:(c + 1) * P, :]).then_inc(ctx_in, 16)
            nc.scalar.dma_start(lm_sb[:], lm.rearrange("(c p) n -> p c n", p=P)).then_inc(ctx_in, 16)
            nc.scalar.dma_start(ctx_sb[:, 0:CT - 1, :], ctx_n[0:(CT - 1) * P, :].rearrange("(t p) d -> p t d", p=P)).then_inc(ctx_in, 16)
            nc.scalar.dma_start(ctx_sb[0:CLAST, CT - 1, :], ctx_n[(CT - 1) * P:CTX, :]).then_inc(ctx_in, 16)
            act.wait_ge(small_in, 16 * 4)
            nc.scalar.activation(bq_scaled[:], b_cols[:, 0], ACT.Copy, scale=0.25).then_inc(bias_scaled, 1)
            act.wait_ge(bias_scaled, 1)
            for g in range(4 * NQ):
                what, c = (g % 4) // 2, g % 2
                act.wait_ge(qk_ready, g + 1)
                if g >= 2:
                    act.wait_ge(qk_lo, g - 1)
                nc.scalar.activation(qk32[:, g % 2], proj[g % 2][:], ACT.Identity,
                                     bias=bq_scaled[:, c:c + 1] if what == 0 else b_cols[:, 1, c:c + 1],
                                     scale=DH ** -0.5 if what == 0 else 1.0).then_inc(qk_copied, 1)
            for t in range(CT):
                n = P if t < CT - 1 else CLAST
                act.wait_ge(t_ready, t + 1)
                nc.scalar.activation(t_act[0:n, t], tps[t % 2][0:n], ACT.Gelu).then_inc(t_done, 1)

        @block.gpsimd
        def _(pool):
            nc.gpsimd.memset(zero_rows[:], 0.0).then_inc(rows_zeroed, 1)
            nc.gpsimd.memset(ident32[:], 0.0).then_inc(pool_zeroed, 1)
            nc.gpsimd.memset(eps_col[:], EPS).then_inc(pool_done, 1)
            nc.gpsimd.memset(values[:, :, :, DH:VW], 0.0).then_inc(pool_zeroed, 1)
            pool.wait_ge(pool_zeroed, 2)
            nc.gpsimd.affine_select(out=ident32[:], in_=ident32[:], compare_op=ALU.not_equal, fill=1.0,
                                    base=0, pattern=[[-1, P]], channel_multiplier=1).then_inc(pool_done, 1)
            nc.gpsimd.memset(values[:, :, :, DH:DH + 1], 1.0).then_inc(pool_done, 1)
            pool.wait_ge(pool_done, 3)

        @block.vector
        def _(dve):
            def split(hi, lo, whole_, n):
                nc.vector.tensor_copy(hi, whole_).then_inc(hi_done, 1)
                dve.wait_ge(hi_done, n)
                nc.vector.tensor_tensor(lo, whole_, hi, ALU.subtract).then_inc(split_done, 1)

            nc.vector.memset(kstack[ZROW:P], 0.0).then_inc(stacks_set, 1)
            nc.vector.memset(qstack[ZROW:P], 0.0).then_inc(stacks_set, 1)
            dve.wait_ge(stacks_set, 1)
            nc.vector.memset(kstack[MROW:MROW + 1], 1.0).then_inc(stacks_set, 1)
            dve.wait_ge(w_loaded, 16 * 4)
            for n in range(2):
                split(w_split[:, n, 0], w_split[:, n, 1], w_in[:, n], n + 1)
            dve.wait_ge(xT_in, 16 * DC)
            for q in range(NQ):
                cols = slice(q * QB, (q + 1) * QB)
                split(x_split[:, 0, :, cols], x_split[:, 1, :, cols], xT_sb[:, :, cols], 3 + q)
            split(w_split[:, 2, 0], w_split[:, 2, 1], w_in[:, 2], 3 + NQ)
            split(wo_split[:, 0], wo_split[:, 1], w_in[:, 3], 4 + NQ)
            dve.wait_ge(small_in, 16 * 4)
            split(gate_split[:, 0], gate_split[:, 1], g_in[:], 5 + NQ)
            for g in range(4 * NQ):
                dve.wait_ge(qk_copied, g + 1)
                if g >= 4:
                    dve.wait_ge(qk_stored[g % 4], 32 * (g // 4))
                nc.vector.tensor_copy(qk16[:, g % 4, 0], qk32[:, g % 2]).then_inc(qk_hi, 1)
                dve.wait_ge(qk_hi, g + 1)
                nc.vector.tensor_tensor(qk16[:, g % 4, 1], qk32[:, g % 2], qk16[:, g % 4, 0],
                                        ALU.subtract).then_inc(qk_lo, 1)
            for t in range(NT):
                dve.wait_ge(v_ready, t + 1)
                nc.vector.tensor_tensor(values[:, :, t, 0:DH], vps[t % 2][:].rearrange("p (h d) -> p h d", d=DH),
                                        bv_rows[:].rearrange("p (h d) -> p h d", d=DH), ALU.add).then_inc(v_done, 1)
            dve.wait_ge(m_ready, 1)
            nc.vector.tensor_copy(xm[:], mps[:]).then_inc(m_copied, 1)

        @block.tensor
        def _(pe):
            products = [(0, 0), (0, 1), (1, 0)]
            for g in range(4 * NQ):
                q, what, c = g // 4, (g % 4) // 2, g % 2
                pe.wait_ge(split_done, 3 + q)
                if g >= 2:
                    pe.wait_ge(qk_copied, g - 1)
                n = 0
                for k in range(DC):
                    for a, b in products:
                        mm = nc.tensor.matmul(proj[g % 2][:], w_split[:, what, a, k, c * P:(c + 1) * P],
                                              x_split[:, b, k, q * QB:(q + 1) * QB], start=(n == 0), stop=(n == 5))
                        n += 1
                mm.then_inc(qk_ready, 1)
            pe.wait_ge(split_done, 3 + NQ)
            for t in range(NT):
                if t >= 2:
                    pe.wait_ge(v_done, t - 1)
                n = 0
                for k in range(DC):
                    for a, b in products:
                        mm = nc.tensor.matmul(vps[t % 2][:], x_split[:, a, k, t * P:(t + 1) * P],
                                              w_split[:, 2, b, k], start=(n == 0), stop=(n == 5))
                        n += 1
                mm.then_inc(v_ready, 1)
            pe.wait_ge(ctx_in, 16 * 5)
            for t in range(CT):
                n = P if t < CT - 1 else CLAST
                if t >= 2:
                    pe.wait_ge(t_done, t - 1)
                for k in range(DC):
                    mm = nc.tensor.matmul(tps[t % 2][0:n], ctxT_sb[:, k, t * P:t * P + n], lm_sb[:, k],
                                          start=(k == 0), stop=(k == DC - 1))
                mm.then_inc(t_ready, 1)
            for c in range(DC):
                for t in range(CT):
                    n = P if t < CT - 1 else CLAST
                    pe.wait_ge(t_done, t + 1)
                    mm = nc.tensor.matmul(mps[:, c], t_act[0:n, t, c * P:(c + 1) * P], ctx_sb[0:n, t],
                                          start=(t == 0), stop=(t == CT - 1))
            mm.then_inc(m_ready, 1)


def attend(nc, f32, f16, bf16, ALU, ACT, X, q_split, k_split, w_all, w_split_d, ident32, attn, values, qstack, kstack):
    es = ExitStack()
    with es:
        def sb(name, shape, dt):
            return es.enter_context(nc.sbuf_tensor(name, shape, dt))

        def sem(name):
            return es.enter_context(nc.semaphore(name))

        ident16 = sb("ident16", [P, P], bf16)
        hide_keys = sb("hide_keys", [P, P], bf16)
        hide_queries = sb("hide_queries", [P, P], bf16)
        zeros16 = sb("zeros16", [P, P], bf16)
        ones16 = sb("ones16", [P, QB], bf16)
        fold = sb("fold", [P, VW], f32)
        probs = sb("probs", [P, 2, TPQ * QB], f32)
        v_head = sb("v_head", [P, 2, NT, VW], f32)
        partial = sb("partial", [P, NT, NQ], f32)
        neg_max = sb("neg_max", [P, NT], f32)
        max_row = sb("max_row", [NT, P], f16)
        acc_sb = sb("acc_sb", [P, 2, QB], f32)
        inv = sb("inv", [P, NQ, TPQ, 1], f32)
        w_in = sb("a_w_in", [P, 2, WU], f32)
        w_scale = sb("w_scale", [P, 1], f32)
        w_out = sb("a_w_out", [P, 2, 2, WU], f16)
        scores = [es.enter_context(nc.psum_tensor(f"scores{i}", [P, 2 * QB], f32)) for i in range(2)]
        ring = [es.enter_context(nc.psum_tensor(f"ring{i}", [P, QB], f32)) for i in range(NRING)]
        acc = es.enter_context(nc.psum_tensor("acc", [P, QB], f32))

        const_zero, const_done = sem("const_zero"), sem("const_done")
        stack_in = [sem(f"stack_in{n}") for n in range(NSTACK)]
        max_in = sem("max_in")
        scores_ready, exp_done = sem("scores_ready"), sem("exp_done")
        ring_ready, ring_done = sem("ring_ready"), sem("ring_done")
        max_found = sem("max_found")
        v_ready, pv_done, acc_copied = sem("v_ready"), sem("pv_done"), sem("acc_copied")
        inv_ready = sem("inv_ready")
        w_loaded = [sem(f"w_loaded{n}") for n in range(2)]
        w_stored = [sem(f"w_stored{n}") for n in range(2)]
        scale_set, w_hi, w_lo = sem("scale_set"), sem("w_hi"), sem("w_lo")

        half_width = []
        for qb, k0 in QUADS:
            w = [QB - P * j if k0 == qb * TPQ else QB for j in range(TPQ)]
            half_width.append((w[0:2], w[2:4]))

        block = es.enter_context(nc.Block())

        @block.sync
        def _(sp):
            def load_stack(h, slot):
                for s in range(SLOTS):
                    for dst, src, half in ((qstack, q_split, s // 2), (kstack, k_split, s % 2)):
                        sp.dma_start(dst[s * DH:(s + 1) * DH, slot, :],
                                     src[half, bass.ds(h * DH, DH), :]).then_inc(stack_in[slot], 16)

            def load_max(slot, n):
                sp.wait_ge(ring_done, n)
                sp.dma_start(qstack[MROW:MROW + 1, slot, :], max_row[:, :]).then_inc(max_in, 16)

            def load_weights(h, parity):
                sp.dma_start(w_in[:, parity], w_all[:, bass.ds(h * WU, WU)]).then_inc(w_loaded[parity], 16)

            def store_weights(h, parity):
                address_first(sp, h * WU * 2)
                sp.wait_ge(w_lo, h + 1)
                sp.dma_start(w_split_d[:, :, bass.ds(h * WU, WU)].rearrange("a p w -> p a w"),
                             w_out[:, parity]).then_inc(w_stored[parity], 16)

            for h in range(NSTACK):
                load_stack(h, h)
            for h in range(2):
                load_weights(h, h)
            load_max(0, NFIRST)

            def turn(i, last):
                for j in range(NSTACK):
                    if not (last and j == NSTACK - 1):
                        load_max((j + 1) % NSTACK, entries_before(i + j, "max", 0, False))
                    if not last:
                        address_first(sp, (i + (j + NSTACK)) * DH * S * 2)
                        sp.wait_ge(scores_ready, i * (2 * NQUAD) + 2 * NQUAD * (j + 1))
                        load_stack(i + (j + NSTACK), j)
                    store_weights(i + j, j % 2)
                    if not (last and j >= NSTACK - 2):
                        load_weights(i + (j + 2), j % 2)

            with sp.Fori(0, H // NSTACK - 1) as k:
                turn(k * NSTACK, False)
            turn(H - NSTACK, True)
            for parity in range(2):
                sp.wait_ge(w_stored[parity], 16 * (H // 2))

        @block.gpsimd
        def _(pool):
            nc.gpsimd.memset(ident16[:], 0.0).then_inc(const_zero, 1)
            nc.gpsimd.memset(hide_keys[:], 0.0).then_inc(const_zero, 1)
            nc.gpsimd.memset(hide_queries[:], 0.0).then_inc(const_zero, 1)
            nc.gpsimd.memset(zeros16[:], 0.0).then_inc(const_done, 1)
            nc.gpsimd.memset(ones16[:], 1.0).then_inc(const_done, 1)
            nc.gpsimd.memset(fold[:], 0.0).then_inc(const_zero, 1)
            nc.gpsimd.memset(w_scale[:], WSCALE).then_inc(scale_set, 1)
            pool.wait_ge(scale_set, 1)
            nc.gpsimd.memset(v_head[:, 1], 1.0).then_inc(const_done, 1)
            nc.gpsimd.memset(partial[:], NEG * 10.0).then_inc(const_done, 1)
            pool.wait_ge(const_zero, 4)
            nc.gpsimd.affine_select(out=ident16[:], in_=ident16[:], compare_op=ALU.not_equal, fill=1.0,
                                    base=0, pattern=[[-1, P]], channel_multiplier=1).then_inc(const_done, 1)
            nc.gpsimd.affine_select(out=hide_keys[:], in_=hide_keys[:], compare_op=ALU.is_ge, fill=NEG,
                                    base=0, pattern=[[-1, P]], channel_multiplier=1).then_inc(const_done, 1)
            nc.gpsimd.affine_select(out=hide_queries[:], in_=hide_queries[:], compare_op=ALU.is_ge, fill=NEG,
                                    base=0, pattern=[[1, P]], channel_multiplier=-1).then_inc(const_done, 1)
            for r in range(P // VW):
                pool.wait_ge(const_zero, 4 + r)
                nc.gpsimd.affine_select(out=fold[:], in_=fold[:], compare_op=ALU.not_equal, fill=1.0,
                                        base=-VW * r, pattern=[[-1, VW]], channel_multiplier=1).then_inc(const_zero, 1)
            pool.wait_ge(const_zero, 4 + P // VW)

            def copy_values(h, n, slot, first):
                if not first:
                    pool.wait_ge(pv_done, n * NQUAD - (NQUAD - 2))
                nc.gpsimd.tensor_copy(v_head[:, slot], values[:, bass.ds(h, 1)].rearrange("p o t v -> p (o t) v")).then_inc(v_ready, 1)

            def first_halves(k, parity):
                if not isinstance(k, int):
                    pool.wait_ge(w_stored[parity], k * 16)
                pool.wait_ge(w_loaded[parity], k * 16 + 16)
                nc.gpsimd.tensor_tensor(w_out[:, parity, 0], w_in[:, parity], w_scale[:].broadcast_to([P, WU]),
                                        ALU.mult).then_inc(w_hi, 1)

            copy_values(0, 0, 0, True)
            first_halves(0, 0)
            copy_values(1, 1, 1, False)
            first_halves(0, 1)
            with pool.Fori(1, H // 2) as k:
                for j in range(2):
                    copy_values(k * 2 + j, k * 2 + j, j, False)
                    first_halves(k, j)

        @block.scalar
        def _(act):
            act.wait_ge(const_done, 7)
            for half in range(2):
                for j in range(2):
                    at = (2 * half + j) * QB
                    fill = nc.scalar.activation(probs[:, 1, at:at + QB], ones16[:], ACT.Copy)
                fill.then_inc(exp_done, 1)

            def copy_acc(h, qb, quads, folded):
                act.wait_ge(pv_done, quads)
                act.wait_ge(ring_ready, folded)
                nc.scalar.activation(acc_sb[:, qb % 2], acc[:], ACT.Copy).then_inc(acc_copied, 1)

            def head(i, j, last):
                h = i + j
                for s, (qb, k0) in enumerate(QUADS):
                    for half in range(2):
                        w = sum(half_width[s][half])
                        act.wait_ge(scores_ready, h * (2 * NQUAD) + (2 * s + half + 1))
                        if half == 0:
                            act.wait_ge(pv_done, h * NQUAD + (s + 1))
                        nc.scalar.activation(probs[:, s % 2, half * 2 * QB:half * 2 * QB + w],
                                             scores[half][:, 0:w], ACT.Exp).then_inc(exp_done, 1)
                    if s == 0:
                        copy_acc(h, NQ - 1, h * NQUAD + 2, entries_before(h, "fold", 1, False) - NENTRY)
                    for b in range(NQ - 1):
                        if s == LAST_QUAD[b] + 1:
                            copy_acc(h, b, h * NQUAD + (LAST_QUAD[b] + 3),
                                     entries_before(h, "fold", 2, False) - NENTRY if b == 0 else
                                     entries_before(h, "fold", (b - 2) % NQ, last))

            turns(act, head)
            copy_acc(H, NQ - 1, H * NQUAD + 2, entries_before(H - 1, "fold", 1, True))

        @block.tensor
        def _(pe):
            pe.wait_ge(const_done, 7)
            pe.wait_ge(const_zero, 4 + P // VW)

            def form_piece(bank, slot, n):
                t, c, w = PIECES[n]
                diagonal = c + w == (t + 1) * P
                mm = nc.tensor.matmul(bank[:, 0:w], qstack[0:MROW, slot, t * P:(t + 1) * P],
                                      kstack[0:MROW, slot, c:c + w], start=True, stop=not diagonal)
                if diagonal:
                    mm = nc.tensor.matmul(bank[:, w - P:w], ident16[:], hide_keys[:], start=False, stop=True)
                return mm

            def fold_block(bank, qb):
                for t in range(TPQ):
                    mm = nc.tensor.matmul(bank[:, t * VW:(t + 1) * VW], acc_sb[:, qb % 2, t * P:(t + 1) * P],
                                          fold[:], start=True, stop=True)
                return mm

            def turn_max(bank):
                return nc.tensor.transpose(bank[0:NT, 0:P], neg_max[:], ident32[:])

            nc.tensor.matmul(acc[:], zeros16[:], ones16[:], start=True, stop=False).then_inc(pv_done, 1)
            pe.wait_ge(stack_in[0], STACK_DMAS)
            for n in range(NPIECE):
                if n >= NRING:
                    pe.wait_ge(ring_done, n - NRING + 1)
                form_piece(ring[n % NRING], 0, n).then_inc(ring_ready, 1)
            pe.wait_ge(max_found, 1)
            turn_max(ring[NPIECE % NRING]).then_inc(ring_ready, 1)

            def scores_half(h, slot, s, half):
                qb, k0 = QUADS[s]
                pe.wait_ge(exp_done, h * (2 * NQUAD) + (2 * s + half + 1))
                at = 0
                for j in (2 * half, 2 * half + 1):
                    w = half_width[s][half][j % 2]
                    kt = k0 + j
                    diagonal = k0 == qb * TPQ
                    mm = nc.tensor.matmul(scores[half][:, at:at + w], kstack[0:MROW + 1, slot, kt * P:(kt + 1) * P],
                                          qstack[0:MROW + 1, slot, (qb + 1) * QB - w:(qb + 1) * QB],
                                          start=True, stop=not diagonal)
                    if diagonal:
                        mm = nc.tensor.matmul(scores[half][:, at:at + P], ident16[:], hide_queries[:],
                                              start=False, stop=True)
                    at += w
                mm.then_inc(scores_ready, 1)

            def weigh(h, slot, s, exps):
                qb, k0 = QUADS[s]
                pe.wait_ge(exp_done, exps)
                first, last = k0 == 0, s == LAST_QUAD[qb]
                if first:
                    pe.wait_ge(acc_copied, h * NQ + (qb + 1))
                    pe.wait_ge(v_ready, h + 1)
                if qb == 0:
                    nc.tensor.matmul(acc[:], zeros16[:], ones16[:], start=True, stop=False)
                for j in range(TPQ):
                    w = half_width[s][j // 2][j % 2]
                    at = j // 2 * 2 * QB + (0 if j % 2 == 0 else half_width[s][j // 2][0])
                    mm = nc.tensor.matmul(acc[VW * j:VW * (j + 1), QB - w:QB], v_head[:, slot, k0 + j],
                                          probs[:, s % 2, at:at + w], start=first and qb > 0, stop=last)
                mm.then_inc(pv_done, 1)

            def head(i, j, last):
                h = i + j
                slot, next_slot = j, (j + 1) % NSTACK
                pe.wait_ge(max_in, h * 16 + 16)
                if not last:
                    pe.wait_ge(stack_in[next_slot], (i // NSTACK + 1 + (j + 1) // NSTACK) * STACK_DMAS
                               if isinstance(i, int) else i * (STACK_DMAS // NSTACK) + (1 + (j + 1) // NSTACK) * STACK_DMAS)
                order = ring_order(last)
                entry = 0

                def through_ring(items):
                    nonlocal entry
                    for kind, n in items:
                        bank = ring[(NFIRST + entry) % NRING]
                        pe.wait_ge(ring_done, h * NENTRY + (NFIRST + entry - NRING + 1))
                        if kind == "piece":
                            mm = form_piece(bank, next_slot, n)
                        elif kind == "max":
                            pe.wait_ge(max_found, h + 2)
                            mm = turn_max(bank)
                        else:
                            pe.wait_ge(acc_copied, h * NQ + ((n + 1) % NQ + 1))
                            mm = fold_block(bank, n)
                        mm.then_inc(ring_ready, 1)
                        entry += 1

                for s in range(NQUAD):
                    scores_half(h, slot, s, 0)
                    through_ring(order[s][0])
                    scores_half(h, slot, s, 1)
                    through_ring(order[s][1])
                    if s == 0:
                        weigh(None, (j + 1) % 2, NQUAD - 1, h * (2 * NQUAD) + 2)
                    else:
                        weigh(h, j % 2, s - 1, h * (2 * NQUAD) + (2 * s + 2))
                    through_ring(order[s][2])

            turns(pe, head)
            weigh(None, (H - 1) % 2, NQUAD - 1, H * 2 * NQUAD + 2)
            pe.wait_ge(acc_copied, H * NQ + 1)
            pe.wait_ge(ring_done, NENTRIES - NRING)
            fold_block(ring[(NENTRIES - 1) % NRING], NQ - 1).then_inc(ring_ready, 1)

        @block.vector
        def _(dve):
            dve.wait_ge(const_done, 7)

            def reduce_piece(bank, n):
                t, c, w = PIECES[n]
                nc.vector.tensor_reduce(out=partial[:, t, c // QB:c // QB + 1], in_=bank[:, 0:w],
                                        axis=X, op=ALU.max).then_inc(ring_done, 1)

            def find_max():
                nc.vector.tensor_reduce(out=neg_max[:], in_=partial[:], axis=X, op=ALU.max,
                                        negate=True).then_inc(max_found, 1)

            def copy_max(bank):
                nc.vector.tensor_copy(max_row[:], bank[0:NT, 0:P]).then_inc(ring_done, 1)

            def norm_block(bank, col, n, qb):
                folded = bank[:, 0:TPQ * VW].rearrange("p (t v) -> p t v", v=VW)
                nc.vector.reciprocal(inv[:, qb], folded[:, :, DH:DH + 1]).then_inc(inv_ready, 1)
                dve.wait_ge(inv_ready, n)
                nc.vector.tensor_tensor(attn[:, qb * TPQ:(qb + 1) * TPQ, bass.ds(col, DH)], folded[:, :, 0:DH],
                                        inv[:, qb].broadcast_to([P, TPQ, DH]), ALU.mult).then_inc(ring_done, 1)

            for n in range(NPIECE):
                dve.wait_ge(ring_ready, n + 1)
                reduce_piece(ring[n % NRING], n)
            dve.wait_ge(ring_done, NPIECE)
            find_max()
            dve.wait_ge(ring_ready, NFIRST)
            copy_max(ring[NPIECE % NRING])

            def head(i, j, last):
                h = i + j
                order = RING_OF_LAST if last else RING_OF_HEAD
                for entry, (kind, n) in enumerate(order):
                    bank = ring[(NFIRST + entry) % NRING]
                    if kind == "max":
                        dve.wait_ge(ring_done, h * NENTRY + (NFIRST + entry))
                        find_max()
                    dve.wait_ge(ring_ready, h * NENTRY + (NFIRST + entry + 1))
                    if kind == "piece":
                        reduce_piece(bank, n)
                    elif kind == "max":
                        dve.wait_ge(max_in, h * 16 + 16)
                        copy_max(bank)
                    elif n == NQ - 1:
                        norm_block(bank, h * DH, h * NQ + 1, n)
                    else:
                        norm_block(bank, h * DH + DH, h * NQ + (n + 2), n)
                dve.wait_ge(w_hi, h + 1)
                nc.vector.scalar_tensor_tensor(out=w_out[:, j % 2, 1], in0=w_in[:, j % 2], scalar=WSCALE,
                                               in1=w_out[:, j % 2, 0], op0=ALU.mult, op1=ALU.subtract).then_inc(w_lo, 1)

            turns(dve, head)
            dve.wait_ge(ring_ready, NENTRIES)
            norm_block(ring[(NENTRIES - 1) % NRING], H * DH, H * NQ + 1, NQ - 1)


def address_first(engine, address):
    if not isinstance(address, int):
        engine.to_reg(address)


def turns(engine, head):
    with engine.Fori(0, H // NSTACK - 1) as k:
        for j in range(NSTACK):
            head(k * NSTACK, j, False)
    for j in range(NSTACK):
        head(H - NSTACK, j, j == NSTACK - 1)


def mix(nc, f32, f16, u32, ALU, ACT, X, res, attn, wo_split, xm, gate_split, bo_rows, ident32,
        eps_col, w_split_d, weights, shared_in, routed_in, weight_of, slot_of, column_of):
    es = ExitStack()
    with es:
        def sb(name, shape, dt):
            return es.enter_context(nc.sbuf_tensor(name, shape, dt))

        def sem(name):
            return es.enter_context(nc.semaphore(name))

        yT32 = sb("yT32", [P, 2, DC, QB], f32)
        yT = [yT32[:, i].rearrange("p c n -> p (c n)").bitcast(f16).rearrange("p (s c n) -> p s c n", s=2, c=DC)
              for i in range(2)]
        summed = sb("summed", [P, 2, TPQ, D], f32)
        stats = sb("stats", [P, 2, TPQ, 6], f32)
        mean_var = sb("mean_var", [P, 2, TPQ, 2], f32)
        sd = sb("sd", [P, 2, TPQ], f32)
        rstd = sb("rstd", [P, 2, TPQ], f32)
        logits = sb("logits", [P, NT, NE], f32)
        top = sb("top", [P, NT, 8], f32)
        top_at = sb("top_at", [P, NT, 8], u32)
        at32 = sb("at32", [P, NT, 2], f32)
        gap = sb("gap", [P, NT, 1], f32)
        gap_exp = sb("gap_exp", [P, NT, 1], f32)
        den = sb("den", [P, NT, 1], f32)
        experts = sb("experts", [P, 1, NE], f32)
        hot = sb("hot", [P, 2, NT, NE], f32)
        PADT = NT // 2
        PADE = NE // 2
        picked = sb("picked", [P, NT, NE], f32)
        scan = [sb(f"scan{i}", [P, PADT + NT, NE], f32) for i in range(2)]
        before = sb("before", [P, P], f32)
        ones = sb("ones", [P, P], f32)
        thresholds = sb("thresholds", [P, 1, NT], f32)
        tile_no = sb("tile_no", [P, MAX_TILES, 1], f32)
        tscan = [sb(f"tscan{i}", [P, PADE + NE], f32) for i in range(2)]
        spare = yT32[:, 0].rearrange("p c n -> p (c n)")
        above = spare[:, 0:NT * NE].rearrange("p (e t) -> p e t", t=NT)
        place = spare[:, NT * NE:2 * NT * NE].rearrange("p (t e) -> p t e", e=NE)
        chosen = spare[:, 2 * NT * NE:4 * NT * NE].rearrange("p (r t e) -> p r t e", r=2, e=NE)
        past = spare[:, 4 * NT * NE:(4 * NT + MAX_TILES) * NE].rearrange("p (t e) -> p t e", e=NE)
        slot32 = sb("slot32", [P, 2, NT], f32)
        expert_of = sb("expert_of", [P, MAX_TILES], f32)
        tps = [es.enter_context(nc.psum_tensor(f"turned{i}", [P, DC, QB], f32)) for i in range(2)]
        ops = [es.enter_context(nc.psum_tensor(f"ops{i}", [P, TPQ, D], f32)) for i in range(2)]

        rank = ops[0][:, 0, 0:NT * NE].rearrange("p (t e) -> p t e", e=NE)
        total = ops[0][:, TPQ // 2, 0:NE].rearrange("p (e o) -> p e o", o=1)
        SCANNED = 10
        CONSTS = 9

        biased, turned, hi_done, lo_done = sem("biased"), sem("turned"), sem("hi_done"), sem("lo_done")
        product, added, stats_done, aggr_done = sem("product"), sem("added"), sem("stats_done"), sem("aggr_done")
        sd_done, rstd_done, ln_done = sem("sd_done"), sem("rstd_done"), sem("ln_done")
        logits_done, top_done, vstep, exp_done, consts_ready = sem("logits_done"), sem("top_done"), sem("vstep"), sem("mx_exp_done"), sem("consts_ready")
        ones_zero, counts_ready = sem("ones_zero"), sem("counts_ready")
        NI = 3 * NQ
        NM = 2 * NQ
        block = es.enter_context(nc.Block())

        @block.sync
        def _(sp):
            sp.dma_start(weights[:, :, NE * WE:], w_split_d[:, :, NE * WE:].rearrange("a p w -> p a w")).then_inc(shared_in, 16)
            for e in range(NE):
                sp.dma_start(weights[:, :, e * WE:(e + 1) * WE],
                             w_split_d[:, :, e * WE:(e + 1) * WE].rearrange("a p w -> p a w")).then_inc(routed_in, 16)

        def halves(n):
            return yT[n % 2]

        def los(n):
            return n + 1 if n < NQ else n + 1 - NQ

        @block.tensor
        def _(pe):
            def wait_read(n):
                pe.wait_ge(hi_done, n + 1)
                if n // NQ != 1:
                    pe.wait_ge(lo_done, los(n))

            def turn(n):
                step, g = divmod(n, NQ)
                if n >= 2:
                    wait_read(n - 2)
                if step:
                    pe.wait_ge(ln_done, (n - NQ + 1))
                for c in range(DC):
                    for t in range(TPQ):
                        tile = g * TPQ + t
                        src = attn[:, tile, DH + c * P:DH + (c + 1) * P] if step == 0 else res[:, tile, c * P:(c + 1) * P]
                        mm = nc.tensor.transpose(tps[n % 2][:, c, t * P:(t + 1) * P], src, ident32[:])
                mm.then_inc(turned, 1)

            def multiply(n):
                step = n // NQ
                w = (wo_split, xm, gate_split)[step]
                width = D if step < 2 else NE
                wait_read(n)
                if n >= 2:
                    pe.wait_ge(added, n - 1)
                for t in range(TPQ):
                    if step == 1:
                        for k in range(DC):
                            mm = nc.tensor.matmul(ops[n % 2][:, t], yT32[:, n % 2, k, t * P:(t + 1) * P], w[:, k],
                                                  start=(k == 0), stop=(k == DC - 1))
                        continue
                    m = 0
                    for k in range(DC):
                        for a, b in ((0, 0), (0, 1), (1, 0)):
                            mm = nc.tensor.matmul(ops[n % 2][:, t, 0:width], halves(n)[:, a, k, t * P:(t + 1) * P],
                                                  w[:, b, k], start=(m == 0), stop=(m == 5))
                            m += 1
                mm.then_inc(product, 1)

            turn(0)
            for n in range(NI):
                if n + 1 < NI:
                    turn(n + 1)
                multiply(n)
            pe.wait_ge(vstep, SCANNED)
            pe.wait_ge(added, NI)
            pe.wait_ge(consts_ready, CONSTS)
            nc.tensor.matmul(rank, before[:], picked[:], start=True, stop=False)
            nc.tensor.matmul(rank, ones[:], scan[0][:, PADT - 1:PADT - 1 + NT], start=False, stop=True)
            nc.tensor.matmul(total[:, :, 0], ones[:], scan[0][:, PADT + NT - 1], start=True, stop=True).then_inc(counts_ready, 1)

        @block.scalar
        def _(act):
            def hi(n):
                act.wait_ge(turned, n + 1)
                if n >= 2:
                    act.wait_ge(product, n - 1)
                nc.scalar.activation(yT32[:, n % 2] if n // NQ == 1 else halves(n)[:, 0], tps[n % 2][:],
                                     ACT.Copy).then_inc(hi_done, 1)

            hi(0)
            for n in range(NI):
                if n + 1 < NI:
                    hi(n + 1)
                if n < NM:
                    act.wait_ge(aggr_done, TPQ * (n + 1))
                    if n >= 2:
                        act.wait_ge(rstd_done, n - 1)
                    nc.scalar.activation(sd[:, n % 2], mean_var[:, n % 2, :, 1], ACT.Sqrt, bias=eps_col[:]).then_inc(sd_done, 1)
            act.wait_ge(vstep, 1)
            nc.scalar.activation(gap_exp[:], gap[:], ACT.Exp).then_inc(exp_done, 1)

        @block.gpsimd
        def _(pool):
            for g in range(NQ):
                nc.gpsimd.tensor_tensor(res[:, g * TPQ:(g + 1) * TPQ], res[:, g * TPQ:(g + 1) * TPQ],
                                        bo_rows[:].rearrange("p (o d) -> p o d", o=1).broadcast_to([P, TPQ, D]), ALU.add).then_inc(biased, 1)
            for dst, pattern in ((experts, [[0, 1], [1, NE]]), (thresholds, [[0, 1], [P, NT]]),
                                 (tile_no, [[1, MAX_TILES], [0, 1]])):
                nc.gpsimd.iota(dst[:], pattern=pattern, base=0, channel_multiplier=0,
                               allow_small_or_imprecise_dtypes=True).then_inc(consts_ready, 1)
            for dst in (*scan, *tscan):
                nc.gpsimd.memset(dst[:], 0.0).then_inc(consts_ready, 1)
            nc.gpsimd.memset(ones[:], 1.0).then_inc(consts_ready, 1)
            nc.gpsimd.memset(before[:], 1.0).then_inc(ones_zero, 1)
            pool.wait_ge(ones_zero, 1)
            nc.gpsimd.affine_select(out=before[:], in_=before[:], compare_op=ALU.is_gt, fill=0.0,
                                    base=0, pattern=[[1, P]], channel_multiplier=-1).then_inc(consts_ready, 1)
            for n in range(NM):
                pool.wait_ge(rstd_done, n + 1)
                pool.wait_ge(added, n + 1)
                g = n % NQ
                for t in range(TPQ):
                    ln = nc.gpsimd.tensor_scalar(res[:, g * TPQ + t], summed[:, n % 2, t], mean_var[:, n % 2, t, 0:1],
                                                 rstd[:, n % 2, t:t + 1], ALU.subtract, ALU.mult)
                ln.then_inc(ln_done, 1)

        @block.vector
        def _(dve):
            def lo(n):
                if n // NQ == 1:
                    return
                dve.wait_ge(hi_done, n + 1)
                nc.vector.tensor_tensor(halves(n)[:, 1], tps[n % 2][:], halves(n)[:, 0], ALU.subtract).then_inc(lo_done, 1)

            lo(0)
            for n in range(NI):
                if n + 1 < NI:
                    lo(n + 1)
                step, g = divmod(n, NQ)
                tiles = slice(g * TPQ, (g + 1) * TPQ)
                dve.wait_ge(product, n + 1)
                if step == 2:
                    nc.vector.tensor_copy(logits[:, tiles], ops[n % 2][:, :, 0:NE]).then_inc(added, 1)
                    continue
                if step == 0:
                    dve.wait_ge(biased, g + 1)
                else:
                    dve.wait_ge(ln_done, n - NQ + 1)
                if n >= 2:
                    dve.wait_ge(ln_done, n - 1)
                nc.vector.tensor_tensor(summed[:, n % 2], ops[n % 2][:], res[:, tiles], ALU.add).then_inc(added, 1)
                dve.wait_ge(added, n + 1)
                if n >= 2:
                    dve.wait_ge(sd_done, n - 1)
                for t in range(TPQ):
                    nc.vector.bn_stats(stats[:, n % 2, t], summed[:, n % 2, t]).then_inc(stats_done, 1)
                for t in range(TPQ):
                    dve.wait_ge(stats_done, n * TPQ + t + 1)
                    nc.vector.bn_aggr(mean_var[:, n % 2, t], stats[:, n % 2, t]).then_inc(aggr_done, 1)
                dve.wait_ge(sd_done, n + 1)
                nc.vector.reciprocal(rstd[:, n % 2], sd[:, n % 2]).then_inc(rstd_done, 1)
            dve.wait_ge(added, NI)
            for t in range(NT):
                nc.vector.max(top[:, t], logits[:, t]).then_inc(top_done, 1)
            for t in range(NT):
                dve.wait_ge(top_done, t + 1)
                nc.vector.max_index(top_at[:, t], top[:, t], logits[:, t]).then_inc(top_done, 1)
            nc.vector.tensor_tensor(gap[:], top[:, :, 1:2], top[:, :, 0:1], ALU.subtract).then_inc(vstep, 1)
            dve.wait_ge(top_done, 2 * NT)
            nc.vector.tensor_copy(at32[:], top_at[:, :, 0:2]).then_inc(vstep, 1)
            dve.wait_ge(consts_ready, CONSTS)
            dve.wait_ge(vstep, 2)
            for r in range(2):
                nc.vector.tensor_tensor(hot[:, r], experts[:].broadcast_to([P, NT, NE]),
                                        at32[:, :, r:r + 1].broadcast_to([P, NT, NE]), ALU.is_equal).then_inc(vstep, 1)
            dve.wait_ge(vstep, 4)
            nc.vector.tensor_tensor(picked[:], hot[:, 0], hot[:, 1], ALU.add).then_inc(vstep, 1)
            nc.vector.tensor_tensor(scan[0][:, PADT:], hot[:, 0], hot[:, 1], ALU.add).then_inc(vstep, 1)
            for k in range(4):
                src, dst = scan[k % 2], scan[(k + 1) % 2]
                dve.wait_ge(vstep, 6 + k)
                nc.vector.tensor_tensor(dst[:, PADT:], src[:, PADT:], src[:, PADT - 2 ** k:PADT - 2 ** k + NT],
                                        ALU.add).then_inc(vstep, 1)
            dve.wait_ge(counts_ready, 1)
            nc.vector.tensor_tensor(above[:], total.broadcast_to([P, NE, NT]), thresholds[:].broadcast_to([P, NE, NT]),
                                    ALU.is_gt).then_inc(vstep, 1)
            dve.wait_ge(vstep, 11)
            nc.vector.tensor_reduce(out=tscan[0][:, PADE:], in_=above[:], axis=X, op=ALU.add).then_inc(vstep, 1)
            for k in range(3):
                src, dst = tscan[k % 2], tscan[(k + 1) % 2]
                dve.wait_ge(vstep, 12 + k)
                nc.vector.tensor_tensor(dst[:, PADE:], src[:, PADE:], src[:, PADE - 2 ** k:PADE - 2 ** k + NE],
                                        ALU.add).then_inc(vstep, 1)
            first_tile = tscan[1][:, PADE - 1:PADE - 1 + NE].rearrange("p (o e) -> p o e", o=1)
            end_tile = tscan[1][:, PADE:].rearrange("p (o e) -> p o e", o=1)
            dve.wait_ge(vstep, 15)
            nc.vector.scalar_tensor_tensor(out=place[:], in0=first_tile.broadcast_to([P, NT, NE]), scalar=float(P),
                                           in1=rank, op0=ALU.mult, op1=ALU.add).then_inc(vstep, 1)
            dve.wait_ge(vstep, 16)
            for r in range(2):
                nc.vector.tensor_tensor(chosen[:, r], hot[:, r], place[:], ALU.mult).then_inc(vstep, 1)
            dve.wait_ge(vstep, 18)
            nc.vector.tensor_reduce(out=slot32[:], in_=chosen[:], axis=X, op=ALU.add).then_inc(vstep, 1)
            dve.wait_ge(vstep, 19)
            nc.vector.tensor_copy(slot_of[:], slot32[:]).then_inc(vstep, 1)
            nc.vector.tensor_tensor(past[:], tile_no[:].broadcast_to([P, MAX_TILES, NE]),
                                    end_tile.broadcast_to([P, MAX_TILES, NE]), ALU.is_ge).then_inc(vstep, 1)
            dve.wait_ge(vstep, 21)
            nc.vector.tensor_reduce(out=expert_of[:], in_=past[:], axis=X, op=ALU.add).then_inc(vstep, 1)
            dve.wait_ge(vstep, 22)
            nc.vector.tensor_scalar(column_of[:], expert_of[:], NE - 1.0, float(WE), ALU.min, ALU.mult).then_inc(vstep, 1)
            dve.wait_ge(exp_done, 1)
            nc.vector.tensor_scalar(den[:], gap_exp[:], 1.0, WSCALE, ALU.add, ALU.mult).then_inc(vstep, 1)
            dve.wait_ge(vstep, 24)
            nc.vector.reciprocal(weight_of[:, :, 0:1], den[:]).then_inc(vstep, 1)
            dve.wait_ge(vstep, 25)
            nc.vector.tensor_tensor(weight_of[:, :, 1:2], weight_of[:, :, 0:1], gap_exp[:], ALU.mult).then_inc(vstep, 1)


def feed_forward(nc, f32, f16, ALU, ACT, res, attn, ident32, eps_col, weights, shared_in, routed_in,
                 weight_of, slot_of, column_of, sorted_x, sorted_y, out):
    es = ExitStack()
    with es:
        def sb(name, shape, dt):
            return es.enter_context(nc.sbuf_tensor(name, shape, dt))

        def sem(name):
            return es.enter_context(nc.semaphore(name))

        HEAD = NT // 2
        R0, R1 = HEAD, HEAD + MAX_TILES
        NALL = NT + MAX_TILES
        HB = QB // P
        NB = HC // HB
        NG = 8

        x_rows = sb("x_rows", [P, 2, D], f32)
        xT = sb("f_xT", [P, 2, 2, DC, P], f16)
        hid32 = sb("hid32", [P, NB, QB], f32)
        hid = sb("hid", [P, 2, 2, HC, P], f16)
        y_rows = sb("y_rows", [P, 2, D], f32)
        gathered = attn[:].rearrange("p t d -> p (t d)")[:, 0:NG * 2 * D].rearrange("p (n r d) -> p n r d", n=NG, r=2)
        stats = sb("f_stats", [P, NT, 6], f32)
        mean_var = sb("f_mean_var", [P, NT, 2], f32)
        sd = sb("f_sd", [P, NT], f32)
        rstd = sb("f_rstd", [P, NT], f32)
        tps = [es.enter_context(nc.psum_tensor(f"f_tps{i}", [P, DC, P], f32)) for i in range(2)]
        hps = [es.enter_context(nc.psum_tensor(f"f_hps{i}", [P, NB, QB], f32)) for i in range(2)]
        yps = [es.enter_context(nc.psum_tensor(f"f_yps{i}", [P, D], f32)) for i in range(2)]

        scattered, gathered_in = [sem(f"scattered{g}") for g in range(NT // TPQ)], [sem(f"gathered_in{g}") for g in range(NG)]
        rows_in, rows_out = [sem(f"rows_in{i}") for i in range(2)], [sem(f"rows_out{i}") for i in range(2)]
        turned, x_hi, x_lo = sem("f_turned"), sem("x_hi"), sem("x_lo")
        h_ready, silu_done, hid_hi, hid_lo = sem("h_ready"), sem("silu_done"), sem("hid_hi"), sem("hid_lo")
        y_ready, y_done, combined = sem("y_ready"), sem("y_done"), sem("combined")
        stats_done, aggr_done, sd_done, rstd_done, final_done, stored = (
            sem("f_stats_done"), sem("f_aggr_done"), sem("f_sd_done"), sem("f_rstd_done"), sem("final_done"), sem("stored"))
        block = es.enter_context(nc.Block())

        def shared(n):
            if not isinstance(n, int) or R0 <= n < R1:
                return None
            return n if n < R0 else n - MAX_TILES

        def in_turn(engine, step, first, last, ahead=0):
            start, pairs = R0 + 2, (R1 - ahead - R0 - 2) // 2
            for n in range(first, start):
                step(n, n % 2)
            with engine.Fori(0, pairs) as k:
                for j in range(2):
                    step(k * 2 + (start + j), (start + j) % 2)
            for n in range(start + 2 * pairs, last):
                step(n, n % 2)

        def rows_before(n, parity):
            return (n - R0 - (n - R0) % 2) * 8 if isinstance(n, int) else (n - (R0 + (parity - R0) % 2)) * 8

        @block.sync
        def _(sp):
            for g in range(NT // TPQ):
                sp.wait_ge(scattered[g], 16 * 2 * TPQ)

            def load(n, parity):
                sp.dma_start(x_rows[:, parity], sorted_x[bass.ds((n - R0) * P, P), :]).then_inc(rows_in[parity], 16)

            def store(n, parity):
                address_first(sp, (n - R0) * P * D * 4)
                sp.wait_ge(y_done, n + 1)
                sp.dma_start(sorted_y[bass.ds((n - R0) * P, P), :], y_rows[:, parity]).then_inc(rows_out[parity], 16)

            for n in (R0, R0 + 1):
                load(n, n % 2)

            def both(n, parity):
                if not isinstance(n, int) or n + 2 < R1:
                    address_first(sp, (n + 2 - R0) * P * D * 4)
                    sp.wait_ge(turned, n + 1)
                    load(n + 2, parity)
                if not isinstance(n, int) or n > R0:
                    store(n - 1, 1 - parity)

            in_turn(sp, both, R0, R1, 2)
            store(R1 - 1, (R1 - 1) % 2)
            for g in range(NT // TPQ):
                tiles = slice(g * TPQ, (g + 1) * TPQ)
                sp.wait_ge(final_done, TPQ * (g + 1))
                sp.dma_start(out[g * QB:(g + 1) * QB, :].rearrange("(t p) d -> p t d", p=P), res[:, tiles]).then_inc(stored, 16)
            sp.wait_ge(stored, 16 * (NT // TPQ))

        @block.gpsimd
        def _(pool):
            for t in range(NT):
                for r in range(2):
                    nc.gpsimd.indirect_dma_start(
                        out=sorted_x, out_offset=bass.IndirectOffsetOnAxis(ap=slot_of[:, r, t:t + 1], axis=0),
                        in_=res[:, t], in_offset=None).then_inc(scattered[t // TPQ], 16)
            for i in range(2):
                pool.wait_ge(rows_out[i], 16 * len(range(R0 + (i - R0) % 2, R1, 2)))
            for t in range(NT):
                if t >= NG:
                    pool.wait_ge(combined, 2 * (t - NG + 1))
                for r in range(2):
                    nc.gpsimd.indirect_dma_start(
                        out=gathered[:, t % NG, r], out_offset=None, in_=sorted_y,
                        in_offset=bass.IndirectOffsetOnAxis(ap=slot_of[:, r, t:t + 1], axis=0)).then_inc(gathered_in[t % NG], 16)

        @block.scalar
        def _(act):
            def first_half_x(n, parity):
                act.wait_ge(turned, n + 1)
                if not isinstance(n, int) or n >= 2:
                    act.wait_ge(h_ready, n * NB - NB)
                nc.scalar.activation(xT[:, parity, 0], tps[parity][:], ACT.Copy).then_inc(x_hi, 1)

            def activate(n, parity):
                for b in range(NB):
                    act.wait_ge(h_ready, n * NB + (b + 1))
                    if not isinstance(n, int) or n >= 1:
                        act.wait_ge(hid_lo, n * NB + (b + 1 - NB))
                    nc.scalar.activation(hid32[:, b], hps[parity][:, b], ACT.Silu, scale=1.0 / WSCALE).then_inc(silu_done, 1)
                    act.wait_ge(silu_done, n * NB + (b + 1))
                    if not isinstance(n, int) or n >= 2:
                        act.wait_ge(y_ready, n - 1)
                    nc.scalar.activation(hid[:, parity, 0, b * HB:(b + 1) * HB], hid32[:, b], ACT.Copy).then_inc(hid_hi, 1)

            def step(n, parity):
                if not isinstance(n, int) or n + 2 < NALL:
                    first_half_x(n + 2, parity)
                if not isinstance(n, int) or n + 1 < NALL:
                    activate(n + 1, 1 - parity)

            first_half_x(0, 0)
            first_half_x(1, 1)
            activate(0, 0)
            in_turn(act, step, 0, NALL)
            act.wait_ge(aggr_done, NT)
            nc.scalar.activation(sd[:], mean_var[:, :, 1], ACT.Sqrt, bias=eps_col[:]).then_inc(sd_done, 1)

        @block.tensor
        def _(pe):
            products = ((0, 0), (0, 1), (1, 0))

            def turn(n, parity):
                t = shared(n)
                if t is None:
                    pe.wait_ge(rows_in[parity], rows_before(n, parity) + 16)
                if not isinstance(n, int) or n >= 2:
                    pe.wait_ge(x_lo, n - 1)
                for c in range(DC):
                    cols = slice(c * P, (c + 1) * P)
                    mm = nc.tensor.transpose(tps[parity][:, c], x_rows[:, parity, cols] if t is None else res[:, t, cols],
                                             ident32[:])
                mm.then_inc(turned, 1)

            def column(n):
                if shared(n) is not None:
                    return NE * WE
                return pe.value_load(column_of[0:1, bass.ds(n - R0, 1)], min_val=0, max_val=(NE - 1) * WE)

            def widen(n, parity):
                at = column(n)
                pe.wait_ge(x_lo, n + 1)
                for b in range(NB):
                    if not isinstance(n, int) or n >= 2:
                        pe.wait_ge(silu_done, n * NB + (b + 1 - 2 * NB))
                    for j in range(HB):
                        m = 0
                        for k in range(DC):
                            for a, c in products:
                                mm = nc.tensor.matmul(hps[parity][:, b, j * P:(j + 1) * P],
                                                      weights[:, a, bass.ds(at + (k * HID + (b * HB + j) * P), P)],
                                                      xT[:, parity, c, k], start=(m == 0), stop=(m == 5))
                                m += 1
                    mm.then_inc(h_ready, 1)

            def narrow(n, parity):
                at = column(n)
                if not isinstance(n, int) or n >= 2:
                    pe.wait_ge(y_done, n - 1)
                m = 0
                for j in range(HC):
                    if j % HB == 0:
                        pe.wait_ge(hid_lo, n * NB + (j // HB + 1))
                    for a, c in products:
                        mm = nc.tensor.matmul(yps[parity][:], hid[:, parity, a, j],
                                              weights[:, c, bass.ds(at + (WE // 2 + j * D), D)],
                                              start=(m == 0), stop=(m == 3 * HC - 1))
                        m += 1
                mm.then_inc(y_ready, 1)

            def step(n, parity):
                if isinstance(n, int) and n + 1 == R0:
                    pe.wait_ge(routed_in, 16 * NE)
                if not isinstance(n, int) or n + 2 < NALL:
                    turn(n + 2, parity)
                if not isinstance(n, int) or n + 1 < NALL:
                    widen(n + 1, 1 - parity)
                narrow(n, parity)

            turn(0, 0)
            turn(1, 1)
            pe.wait_ge(shared_in, 16)
            widen(0, 0)
            in_turn(pe, step, 0, NALL, 2)

        @block.vector
        def _(dve):
            def second_half_x(n, parity):
                dve.wait_ge(x_hi, n + 1)
                nc.vector.tensor_tensor(xT[:, parity, 1], tps[parity][:], xT[:, parity, 0], ALU.subtract).then_inc(x_lo, 1)

            def second_halves(n, parity):
                for b in range(NB):
                    chunks = slice(b * HB, (b + 1) * HB)
                    dve.wait_ge(hid_hi, n * NB + (b + 1))
                    nc.vector.tensor_tensor(hid[:, parity, 1, chunks], hid32[:, b].rearrange("p (j n) -> p j n", n=P),
                                            hid[:, parity, 0, chunks], ALU.subtract).then_inc(hid_lo, 1)

            def take(n, parity):
                t = shared(n)
                dve.wait_ge(y_ready, n + 1)
                if t is None:
                    if not isinstance(n, int) or n >= R0 + 2:
                        dve.wait_ge(rows_out[parity], rows_before(n, parity))
                    nc.vector.tensor_copy(y_rows[:, parity], yps[parity][:]).then_inc(y_done, 1)
                    return
                if t < HEAD:
                    dve.wait_ge(scattered[t // TPQ], 16 * 2 * TPQ)
                nc.vector.scalar_tensor_tensor(out=res[:, t], in0=yps[parity][:], scalar=1.0 / WSCALE, in1=res[:, t],
                                               op0=ALU.mult, op1=ALU.add).then_inc(y_done, 1)

            def combine(t):
                dve.wait_ge(gathered_in[t % NG], 32 * (t // NG + 1))
                dve.wait_ge(y_done, NALL if t >= HEAD else R0)
                for r in range(2):
                    if r:
                        dve.wait_ge(combined, 2 * t + 1)
                    nc.vector.scalar_tensor_tensor(out=res[:, t], in0=gathered[:, t % NG, r], scalar=weight_of[:, t, r:r + 1],
                                                   in1=res[:, t], op0=ALU.mult, op1=ALU.add).then_inc(combined, 1)

            def statistics(t):
                dve.wait_ge(combined, 2 * t + 2)
                nc.vector.bn_stats(stats[:, t], res[:, t]).then_inc(stats_done, 1)
                dve.wait_ge(stats_done, t + 1)
                nc.vector.bn_aggr(mean_var[:, t], stats[:, t]).then_inc(aggr_done, 1)

            def step(n, parity):
                if not isinstance(n, int) or n + 2 < NALL:
                    second_half_x(n + 2, parity)
                if not isinstance(n, int) or n + 1 < NALL:
                    second_halves(n + 1, 1 - parity)
                take(n, parity)
                if isinstance(n, int) and n > R1:
                    combine(n - R1 - 1)
                    statistics(n - R1 - 1)

            second_half_x(0, 0)
            second_half_x(1, 1)
            second_halves(0, 0)
            in_turn(dve, step, 0, NALL)
            for t in range(NALL - R1 - 1, NT):
                combine(t)
                statistics(t)
            dve.wait_ge(sd_done, 1)
            nc.vector.reciprocal(rstd[:], sd[:]).then_inc(rstd_done, 1)
            dve.wait_ge(rstd_done, 1)
            for t in range(NT):
                nc.vector.tensor_scalar(res[:, t], res[:, t], mean_var[:, t, 0:1], rstd[:, t:t + 1],
                                        ALU.subtract, ALU.mult).then_inc(final_done, 1)


def kernel(**inputs):
    import numpy as np
    import concourse.bacc as bacc
    from concourse import mybir
    from concourse.bass_utils import run_bass_kernel_spmd

    def lay_out(w1, w2):
        first = w1.reshape(NX, HID, DC, P).transpose(3, 0, 2, 1).reshape(P, NX, WE // 2)
        second = w2.reshape(NX, D, HC, P).transpose(3, 0, 2, 1).reshape(P, NX, WE // 2)
        return np.concatenate([first, second], axis=2).reshape(P, NX * WE)

    a = {k: np.asarray(v) for k, v in inputs.items()}
    arrays = {
        "x": a["x"][0],
        "xT": a["x"][0].T,
        "ctx_n": a["ctx_1024"][0],
        "ctxT": a["ctx_1024"][0].T,
        "wq": a["L0_attn_wq"], "wk": a["L0_attn_wk"], "wv": a["L0_attn_wv"], "wo": a["L0_attn_wo"],
        "b_qk": np.stack([a["L0_attn_bq"], a["L0_attn_bk"]]).reshape(2, DC, P).transpose(2, 0, 1),
        "bv": a["L0_attn_bv"], "bo": a["L0_attn_bo"],
        "lm": a["L0_xattn_learnable_matrix"],
        "w_all": lay_out(np.concatenate([a["L0_ffn_experts_w1"], a["L0_ffn_shared_w1"][None]]),
                         np.concatenate([a["L0_ffn_experts_w2"], a["L0_ffn_shared_w2"][None]])),
        "gT": a["L0_ffn_gate_w"].T,
    }
    arrays = {k: np.ascontiguousarray(v) for k, v in arrays.items()}
    nc = bacc.Bacc("TRN2", target_bir_lowering=False, num_devices=1)
    args = {k: nc.dram_tensor(k, v.shape, mybir.dt.from_np(v.dtype), kind="ExternalInput").ap() for k, v in arrays.items()}
    out = nc.dram_tensor("out", (S, D), mybir.dt.float32, kind="ExternalOutput").ap()
    decoder_layer(nc, out=out, **args)
    r = run_bass_kernel_spmd(nc, [arrays], core_ids=[0])
    return r.results[0]["out"].reshape(1, S, D)
```

```python
import numpy as np
import concourse.bass as bass
from concourse import mybir
from contextlib import ExitStack

S = 2048
D = 256
H = 16
DH = D // H
CTX = 1601
HID = 1024
NE = 8
P = 128
DC = D // P
NT = S // P
QB = 512
NQ = S // QB
TPQ = QB // P
HC = HID // P
CT = (CTX + P - 1) // P
CLAST = CTX - (CT - 1) * P
EPS = 1e-5
NX = NE + 1
WE = 2 * DC * HID
WU = NX * WE // H
TB = 2
TW = TB * P
MAX_TILES = 2 * S // TW + NE - 1
NSLOT = MAX_TILES * TW
ROW = D + 4
BEST_SLOT, TOKEN, GATE, GATE_DIFF = range(D, ROW)
NEG = -1.0e30
WSCALE = 256.0

SLOTS = 4
MROW = 96
ZROW = SLOTS * DH
NSTACK = 4

QUADS = [(qb, 4 * k) for qb in range(NQ) for k in range(qb + 1)]
NQUAD = len(QUADS)
PIECES = [(t, c, min(QB, (t + 1) * P - c)) for t in range(NT) for c in range(0, (t + 1) * P, QB)]
NPIECE = len(PIECES)
VW = 32
LAST_QUAD = [max(s for s, (b, _) in enumerate(QUADS) if b == qb) for qb in range(NQ)]
STACK_DMAS = 16 * 2 * SLOTS
NRING = 3


PLACES = {4: (0, 1, 1, 2), 5: (0, 1, 1, 2, 2)}


def ring_order(last):
    quads = [[[], [], []] for _ in range(NQUAD)]
    if not last:
        load = [[0, []] for _ in range(NQUAD - 2)]
        for n in sorted(range(NPIECE), key=lambda n: -PIECES[n][2]):
            least = min(load, key=lambda x: x[0])
            least[0] += PIECES[n][2] + 64
            least[1].append(n)
        for s, (_, mine) in enumerate(load):
            for k, n in enumerate(mine):
                quads[s][PLACES[len(mine)][k]].append(("piece", n))
        quads[NQUAD - 2][1].append(("max", 0))
    for half in range(2):
        quads[1 + half][1].insert(0, ("fold", half))
        quads[3 + half][1].insert(0, ("turn", half))
    return quads


RING = ring_order(False)
RING_OF_HEAD = [x for quad in RING for place in quad for x in place]
RING_OF_LAST = [x for quad in ring_order(True) for place in quad for x in place]
NENTRY = len(RING_OF_HEAD)
NFIRST = NRING
VFIRST = NT - 5
NENTRIES = NFIRST + (H - 1) * NENTRY + len(RING_OF_LAST) + 4
assert NENTRY % NRING == 0


def form_piece(nc, bank, qstack, kstack, ident16, hide_keys, slot, n):
    t, c, w = PIECES[n]
    diagonal = c + w == (t + 1) * P
    mm = nc.tensor.matmul(bank[:, 0:w], qstack[0:MROW, slot, t * P:(t + 1) * P],
                          kstack[0:MROW, slot, c:c + w], start=True, stop=not diagonal)
    if diagonal:
        mm = nc.tensor.matmul(bank[:, w - P:w], ident16[:], hide_keys[:], start=False, stop=True)
    return mm


def reduce_piece(nc, X, ALU, bank, partial, n):
    t, c, w = PIECES[n]
    return nc.vector.tensor_reduce(out=partial[:, t, c // QB:c // QB + 1], in_=bank[:, 0:w], axis=X, op=ALU.max)


def load_stack(sp, qstack, kstack, q_split, k_split, h, slot, signal):
    for s in range(SLOTS):
        for dst, src, half in ((qstack, q_split, s // 2), (kstack, k_split, s % 2)):
            sp.dma_start(dst[s * DH:(s + 1) * DH, slot, :], src[half, bass.ds(h * DH, DH), :]).then_inc(signal, 16)


def entries_before(h, kind, n, last):
    order = RING_OF_LAST if last else RING_OF_HEAD
    return h * NENTRY + (NFIRST + order.index((kind, n)) + 1)


def decoder_layer(nc, x, xT, ctx_n, ctxT, wq, wk, wv, wo, b_qk, bv, bo, lm, w_all, gT, out):
    f32, f16, bf16, u32 = mybir.dt.float32, mybir.dt.float16, mybir.dt.bfloat16, mybir.dt.uint32
    ALU = mybir.AluOpType
    ACT = mybir.ActivationFunctionType
    X = mybir.AxisListType.X

    q_split = nc.dram_tensor("q_split", (2, D, S), f16).ap()
    k_split = nc.dram_tensor("k_split", (2, D, S), f16).ap()
    w_split_d = nc.dram_tensor("w_split_d", (2, P, NX * WE), f16).ap()
    sorted_x = nc.dram_tensor("sorted_x", (NSLOT, ROW), f32).ap()
    by_token = nc.dram_tensor("by_token", (3 * S + NSLOT, D), f32).ap()

    whole = ExitStack()
    with whole:
        def keep(name, shape, dt):
            return whole.enter_context(nc.sbuf_tensor(name, shape, dt))

        rows = keep("rows", [P, NT, ROW], f32)
        res = rows[:, :, 0:D]
        mats = keep("mats", [P, 2 * DC * D], f32)
        wo_split = mats[:, 0:DC * D].bitcast(f16).rearrange("p (s c n) -> p s c n", s=2, c=DC)
        xm = mats[:, DC * D:].rearrange("p (c n) -> p c n", c=DC)
        gate_split = keep("gate_split", [P, 2, DC, NE], f16)
        ident32 = keep("ident32", [P, P], f32)
        eps_col = keep("eps_col", [P, 1], f32)
        slot_of = keep("slot_of", [P, 2, NT], u32)
        column_of = keep("column_of", [P, MAX_TILES], u32)
        with ExitStack() as two:
            attn = two.enter_context(nc.sbuf_tensor("attn", [P, NT, DH + D], f32))
            with ExitStack() as three:
                bo_rows = three.enter_context(nc.sbuf_tensor("bo_rows", [P, D], f32))
                values = three.enter_context(nc.sbuf_tensor("values", [P, H, NT, VW], f32))
                qstack = three.enter_context(nc.sbuf_tensor("qstack", [P, NSTACK, S], f16))
                kstack = three.enter_context(nc.sbuf_tensor("kstack", [P, NSTACK, S], f16))
                ident16 = three.enter_context(nc.sbuf_tensor("ident16", [P, P], bf16))
                hide_keys = three.enter_context(nc.sbuf_tensor("hide_keys", [P, P], bf16))
                partial = three.enter_context(nc.sbuf_tensor("partial", [P, NT, NQ], f32))
                neg_max = three.enter_context(nc.sbuf_tensor("neg_max", [P, NT], f32))
                max_row = three.enter_context(nc.sbuf_tensor("max_row", [NT, P], f16))
                hide_queries = three.enter_context(nc.sbuf_tensor("hide_queries", [P, P], bf16))
                zeros16 = three.enter_context(nc.sbuf_tensor("zeros16", [P, P], bf16))
                ones16 = three.enter_context(nc.sbuf_tensor("ones16", [P, QB], bf16))
                fold = three.enter_context(nc.sbuf_tensor("fold", [P, VW], f32))
                w_scale = three.enter_context(nc.sbuf_tensor("w_scale", [P, 1], f32))
                no_token = three.enter_context(nc.sbuf_tensor("no_token", [P, 1, ROW], f32))
                stack_in = [three.enter_context(nc.semaphore(f"stack_in{n}")) for n in range(NSTACK)]
                max_in = three.enter_context(nc.semaphore("max_in"))
                project(nc, f32, f16, ALU, ACT, x, xT, ctx_n, ctxT, wq, wk, wv, wo, b_qk, bv, bo, lm, gT,
                        q_split, k_split, res, wo_split, xm, gate_split, bo_rows, ident32, eps_col,
                        values, qstack, kstack, ident16, hide_keys, partial, X, neg_max, max_row,
                        hide_queries, zeros16, ones16, fold, w_scale, no_token, stack_in, max_in)
                attend(nc, f32, f16, ALU, ACT, X, q_split, k_split, w_all, w_split_d, res, bo_rows, ident32,
                       attn, values, qstack, kstack, ident16, hide_keys, partial, neg_max, max_row,
                       hide_queries, zeros16, ones16, fold, w_scale, no_token, sorted_x, stack_in, max_in)
            weights = two.enter_context(nc.sbuf_tensor("weights", [P, 2, NX * WE], f16))
            finish(nc, f32, f16, u32, ALU, ACT, X, rows, res, attn, mats, wo_split, xm, gate_split, ident32, eps_col, w_split_d,
                   weights, slot_of, column_of, sorted_x, by_token, out)


def project(nc, f32, f16, ALU, ACT, x, xT, ctx_n, ctxT, wq, wk, wv, wo, b_qk, bv, bo, lm, gT,
            q_split, k_split, res, wo_split, xm, gate_split, bo_rows, ident32, eps_col,
            values, qstack, kstack, ident16, hide_keys, partial, X, neg_max, max_row,
            hide_queries, zeros16, ones16, fold, w_scale, no_token, stack_in, max_in):
    es = ExitStack()
    with es:
        def sb(name, shape, dt):
            return es.enter_context(nc.sbuf_tensor(name, shape, dt))

        def sem(name):
            return es.enter_context(nc.semaphore(name))

        xT_sb = sb("xT_sb", [P, DC, S], f32)
        x_split = sb("x_split", [P, 2, DC, S], f16)
        w_in = sb("w_in", [P, 4, DC, D], f32)
        w_split = sb("w_split", [P, 3, 2, DC, D], f16)
        g_in = sb("g_in", [P, DC, NE], f32)
        lm_sb = sb("lm_sb", [P, DC, D], f32)
        ctxT_sb = sb("ctxT_sb", [P, DC, CTX], f32)
        ctx_sb = sb("ctx_sb", [P, CT, D], f32)
        t_act = sb("t_act", [P, CT, D], f32)
        b_cols = sb("b_cols", [P, 2, DC], f32)
        bq_scaled = sb("bq_scaled", [P, DC], f32)
        bv_rows = sb("bv_rows", [P, D], f32)
        qk32 = sb("qk32", [P, 2, QB], f32)
        qk16 = sb("qk16", [P, 4, 2, QB], f16)
        proj = [es.enter_context(nc.psum_tensor(f"proj{i}", [P, QB], f32)) for i in range(2)]
        vps = [es.enter_context(nc.psum_tensor(f"vps{i}", [P, D], f32)) for i in range(2)]
        tps = [es.enter_context(nc.psum_tensor(f"tps{i}", [P, D], f32)) for i in range(2)]
        mps = es.enter_context(nc.psum_tensor("mps", [P, DC, D], f32))

        xT_in = [sem(f"xT_in{q}") for q in range(NQ)]
        qk_w_in, vo_w_in, small_in, ctx_in, res_in = sem("qk_w_in"), sem("vo_w_in"), sem("small_in"), sem("ctx_in"), sem("res_in")
        piece_ready, piece_done = sem("piece_ready"), sem("piece_done")
        first_max_found, first_max_turned, first_max_row = sem("first_max_found"), sem("first_max_turned"), sem("first_max_row")
        fold_set = sem("fold_set")
        rows_zeroed = sem("rows_zeroed")
        pool_zeroed, pool_done, stacks_set = sem("pool_zeroed"), sem("pool_done"), sem("stacks_set")
        hi_done, split_done = sem("hi_done"), sem("split_done")
        qk_ready, qk_copied, qk_hi, qk_lo = sem("qk_ready"), sem("qk_copied"), sem("qk_hi"), sem("qk_lo")
        qk_stored = [sem(f"qk_stored{n}") for n in range(4)]
        bias_scaled = sem("bias_scaled")
        v_ready, v_done = sem("v_ready"), sem("v_done")
        t_ready, t_done, m_ready, m_copied = sem("t_ready"), sem("t_done"), sem("m_ready"), sem("m_copied")

        OTHERS = 4 * (NQ - 1) + 1
        block = es.enter_context(nc.Block())

        @block.sync
        def _(sp):
            for n, w in enumerate((wq, wk)):
                sp.dma_start(w_in[:, n], w.rearrange("(c p) n -> p c n", p=P)).then_inc(qk_w_in, 16)
            for q in range(NQ):
                cols = slice(q * QB, (q + 1) * QB)
                sp.dma_start(xT_sb[:, :, cols], xT[:, cols].rearrange("(c p) n -> p c n", p=P)).then_inc(xT_in[q], 16)
            for n, w in enumerate((wv, wo)):
                sp.dma_start(w_in[:, 2 + n], w.rearrange("(c p) n -> p c n", p=P)).then_inc(vo_w_in, 16)
            for q in range(NQ):
                for n in range(4):
                    sp.wait_ge(qk_lo, 4 * q + n + 1)
                    what, c = n // 2, n % 2
                    for half in range(2):
                        sp.dma_start((q_split, k_split)[what][half, c * P:(c + 1) * P, q * QB:(q + 1) * QB],
                                     qk16[:, n, half, :]).then_inc(qk_stored[n], 16)
                if q < DC:
                    sp.dma_start(ctxT_sb[:, q, :], ctxT[q * P:(q + 1) * P, :]).then_inc(ctx_in, 16)
                if q == 1:
                    sp.dma_start(lm_sb[:], lm.rearrange("(c p) n -> p c n", p=P)).then_inc(ctx_in, 16)
            for n in range(4):
                sp.wait_ge(qk_stored[n], 16 * 2 * NQ)
            load_stack(sp, qstack, kstack, q_split, k_split, 0, 0, stack_in[0])
            sp.dma_start(ctx_sb[:, 0:CT - 1, :], ctx_n[0:(CT - 1) * P, :].rearrange("(t p) d -> p t d", p=P)).then_inc(ctx_in, 16)
            sp.dma_start(ctx_sb[0:CLAST, CT - 1, :], ctx_n[(CT - 1) * P:CTX, :]).then_inc(ctx_in, 16)
            sp.dma_start(res, x.rearrange("(t p) d -> p t d", p=P)).then_inc(res_in, 16)
            for h in range(1, NSTACK):
                load_stack(sp, qstack, kstack, q_split, k_split, h, h, stack_in[h])
            sp.wait_ge(first_max_row, 1)
            sp.dma_start(qstack[MROW:MROW + 1, 0, :], max_row[:, :]).then_inc(max_in, 16)
            sp.wait_ge(res_in, 16)

        @block.scalar
        def _(act):
            nc.scalar.dma_start(b_cols[:], b_qk).then_inc(small_in, 16)
            nc.scalar.dma_start(g_in[:], gT.rearrange("(c p) n -> p c n", p=P)).then_inc(small_in, 16)
            nc.scalar.dma_start(bo_rows[:], bo.partition_broadcast(P)).then_inc(small_in, 16)
            nc.scalar.dma_start(bv_rows[:], bv.partition_broadcast(P)).then_inc(small_in, 16)
            act.wait_ge(qk_w_in, 16 * 2)
            nc.scalar.activation(w_split[:, 0:2, 0], w_in[:, 0:2], ACT.Copy).then_inc(hi_done, 1)

            def first_half_x(q):
                cols = slice(q * QB, (q + 1) * QB)
                act.wait_ge(xT_in[q], 16)
                nc.scalar.activation(x_split[:, 0, :, cols], xT_sb[:, :, cols], ACT.Copy).then_inc(hi_done, 1)

            first_half_x(0)
            act.wait_ge(small_in, 16 * 4)
            nc.scalar.activation(bq_scaled[:], b_cols[:, 0], ACT.Copy, scale=0.25).then_inc(bias_scaled, 1)
            act.wait_ge(bias_scaled, 1)
            for g in range(4 * NQ):
                if g % 4 == 0 and g // 4 + 1 < NQ:
                    first_half_x(g // 4 + 1)
                if g == OTHERS:
                    act.wait_ge(vo_w_in, 16 * 2)
                    nc.scalar.activation(w_split[:, 2, 0], w_in[:, 2], ACT.Copy).then_inc(hi_done, 1)
                    nc.scalar.activation(wo_split[:, 0], w_in[:, 3], ACT.Copy).then_inc(hi_done, 1)
                    nc.scalar.activation(gate_split[:, 0], g_in[:], ACT.Copy).then_inc(hi_done, 1)
                what, c = (g % 4) // 2, g % 2
                act.wait_ge(qk_ready, g + 1)
                if g >= 2:
                    act.wait_ge(qk_lo, g - 1)
                nc.scalar.activation(qk32[:, g % 2], proj[g % 2][:], ACT.Identity,
                                     bias=bq_scaled[:, c:c + 1] if what == 0 else b_cols[:, 1, c:c + 1],
                                     scale=DH ** -0.5 if what == 0 else 1.0).then_inc(qk_copied, 1)
            for t in range(CT):
                n = P if t < CT - 1 else CLAST
                act.wait_ge(t_ready, t + 1)
                nc.scalar.activation(t_act[0:n, t], tps[t % 2][0:n], ACT.Gelu).then_inc(t_done, 1)

        @block.gpsimd
        def _(pool):
            nc.gpsimd.memset(no_token[:], 0.0).then_inc(rows_zeroed, 1)
            pool.wait_ge(rows_zeroed, 1)
            nc.gpsimd.memset(no_token[:, :, TOKEN:TOKEN + 1], 2.0 * S).then_inc(rows_zeroed, 1)
            nc.gpsimd.memset(ident32[:], 0.0).then_inc(pool_zeroed, 1)
            nc.gpsimd.memset(eps_col[:], EPS).then_inc(pool_done, 1)
            nc.gpsimd.memset(values[:, :, :, DH:VW], 0.0).then_inc(pool_zeroed, 1)
            nc.gpsimd.memset(ident16[:], 0.0).then_inc(pool_zeroed, 1)
            nc.gpsimd.memset(hide_keys[:], 0.0).then_inc(pool_zeroed, 1)
            nc.gpsimd.memset(hide_queries[:], 0.0).then_inc(pool_zeroed, 1)
            nc.gpsimd.memset(partial[:], NEG * 10.0).then_inc(pool_done, 1)
            pool.wait_ge(pool_zeroed, 5)
            nc.gpsimd.affine_select(out=ident16[:], in_=ident16[:], compare_op=ALU.not_equal, fill=1.0,
                                    base=0, pattern=[[-1, P]], channel_multiplier=1).then_inc(pool_done, 1)
            nc.gpsimd.affine_select(out=hide_keys[:], in_=hide_keys[:], compare_op=ALU.is_ge, fill=NEG,
                                    base=0, pattern=[[-1, P]], channel_multiplier=1).then_inc(pool_done, 1)
            nc.gpsimd.affine_select(out=ident32[:], in_=ident32[:], compare_op=ALU.not_equal, fill=1.0,
                                    base=0, pattern=[[-1, P]], channel_multiplier=1).then_inc(pool_done, 1)
            nc.gpsimd.memset(values[:, :, :, DH:DH + 1], 1.0).then_inc(pool_done, 1)
            pool.wait_ge(pool_done, 6)
            nc.gpsimd.affine_select(out=hide_queries[:], in_=hide_queries[:], compare_op=ALU.is_ge, fill=NEG,
                                    base=0, pattern=[[1, P]], channel_multiplier=-1).then_inc(pool_done, 1)
            nc.gpsimd.memset(zeros16[:], 0.0).then_inc(pool_done, 1)
            nc.gpsimd.memset(ones16[:], 1.0).then_inc(pool_done, 1)
            nc.gpsimd.memset(w_scale[:], WSCALE).then_inc(pool_done, 1)
            nc.gpsimd.memset(fold[:], 0.0).then_inc(fold_set, 1)
            for r in range(P // VW):
                pool.wait_ge(fold_set, 1 + r)
                nc.gpsimd.affine_select(out=fold[:], in_=fold[:], compare_op=ALU.not_equal, fill=1.0,
                                        base=-VW * r, pattern=[[-1, VW]], channel_multiplier=1).then_inc(fold_set, 1)
            pool.wait_ge(fold_set, 1 + P // VW)
            pool.wait_ge(pool_done, 10)
            pool.wait_ge(rows_zeroed, 2)
            nc.gpsimd.memset(kstack[ZROW:P], 0.0).then_inc(stacks_set, 1)
            nc.gpsimd.memset(qstack[ZROW:P], 0.0).then_inc(stacks_set, 1)
            pool.wait_ge(stacks_set, 2)
            nc.gpsimd.memset(kstack[MROW:MROW + 1], 1.0).then_inc(stacks_set, 1)
            pool.wait_ge(stacks_set, 3)

        @block.vector
        def _(dve):
            def second_half(lo, hi, whole_, n):
                dve.wait_ge(hi_done, n)
                nc.vector.tensor_tensor(lo, whole_, hi, ALU.subtract).then_inc(split_done, 1)

            def second_half_x(q):
                cols = slice(q * QB, (q + 1) * QB)
                second_half(x_split[:, 1, :, cols], x_split[:, 0, :, cols], xT_sb[:, :, cols], 2 + q)

            second_half(w_split[:, 0:2, 1], w_split[:, 0:2, 0], w_in[:, 0:2], 1)
            second_half_x(0)
            for g in range(4 * NQ):
                if g % 4 == 1 and g // 4 + 1 < NQ:
                    second_half_x(g // 4 + 1)
                if g == OTHERS + 1:
                    second_half(w_split[:, 2, 1], w_split[:, 2, 0], w_in[:, 2], 2 + NQ)
                dve.wait_ge(qk_copied, g + 1)
                if g >= 4:
                    dve.wait_ge(qk_stored[g % 4], 32 * (g // 4))
                nc.vector.tensor_copy(qk16[:, g % 4, 0], qk32[:, g % 2]).then_inc(qk_hi, 1)
                dve.wait_ge(qk_hi, g + 1)
                nc.vector.tensor_tensor(qk16[:, g % 4, 1], qk32[:, g % 2], qk16[:, g % 4, 0],
                                        ALU.subtract).then_inc(qk_lo, 1)
            second_half(wo_split[:, 1], wo_split[:, 0], w_in[:, 3], 3 + NQ)
            second_half(gate_split[:, 1], gate_split[:, 0], g_in[:], 4 + NQ)

            def take_piece(n):
                dve.wait_ge(piece_ready, n + 1)
                reduce_piece(nc, X, ALU, proj[n % 2], partial, n).then_inc(piece_done, 1)

            for t in range(NT):
                dve.wait_ge(v_ready, t + 1)
                nc.vector.tensor_tensor(values[:, :, t, 0:DH], vps[t % 2][:].rearrange("p (h d) -> p h d", d=DH),
                                        bv_rows[:].rearrange("p (h d) -> p h d", d=DH), ALU.add).then_inc(v_done, 1)
                if t >= VFIRST:
                    take_piece(t - VFIRST)
            for n in range(NT - VFIRST, NPIECE):
                take_piece(n)
            dve.wait_ge(piece_done, NPIECE)
            nc.vector.tensor_reduce(out=neg_max[:], in_=partial[:], axis=X, op=ALU.max, negate=True).then_inc(first_max_found, 1)
            dve.wait_ge(first_max_turned, 1)
            nc.vector.tensor_copy(max_row[:], proj[NPIECE % 2][0:NT, 0:P]).then_inc(first_max_row, 1)
            dve.wait_ge(m_ready, 1)
            nc.vector.tensor_copy(xm, mps[:]).then_inc(m_copied, 1)

        @block.tensor
        def _(pe):
            products = [(0, 0), (0, 1), (1, 0)]
            for g in range(4 * NQ):
                q, what, c = g // 4, (g % 4) // 2, g % 2
                pe.wait_ge(split_done, 2 + q)
                if g >= 2:
                    pe.wait_ge(qk_copied, g - 1)
                n = 0
                for k in range(DC):
                    for a, b in products:
                        mm = nc.tensor.matmul(proj[g % 2][:], w_split[:, what, a, k, c * P:(c + 1) * P],
                                              x_split[:, b, k, q * QB:(q + 1) * QB], start=(n == 0), stop=(n == 5))
                        n += 1
                mm.then_inc(qk_ready, 1)
            pe.wait_ge(split_done, 2 + NQ)
            early = 0

            def next_piece():
                nonlocal early
                if early < NPIECE:
                    if early == 0:
                        pe.wait_ge(stack_in[0], STACK_DMAS)
                        pe.wait_ge(pool_done, 6)
                        pe.wait_ge(stacks_set, 3)
                    if early < 2:
                        pe.wait_ge(qk_copied, 4 * NQ)
                    else:
                        pe.wait_ge(piece_done, early - 1)
                    form_piece(nc, proj[early % 2], qstack, kstack, ident16, hide_keys, 0, early).then_inc(piece_ready, 1)
                    early += 1

            for t in range(NT):
                if t >= 2:
                    pe.wait_ge(v_done, t - 1)
                n = 0
                for k in range(DC):
                    for a, b in products:
                        mm = nc.tensor.matmul(vps[t % 2][:], x_split[:, a, k, t * P:(t + 1) * P],
                                              w_split[:, 2, b, k], start=(n == 0), stop=(n == 5))
                        n += 1
                mm.then_inc(v_ready, 1)
                if t >= VFIRST:
                    next_piece()
            pe.wait_ge(ctx_in, 16 * 5)
            for t in range(CT):
                n = P if t < CT - 1 else CLAST
                if t >= 2:
                    pe.wait_ge(t_done, t - 1)
                for k in range(DC):
                    mm = nc.tensor.matmul(tps[t % 2][0:n], ctxT_sb[:, k, t * P:t * P + n], lm_sb[:, k],
                                          start=(k == 0), stop=(k == DC - 1))
                mm.then_inc(t_ready, 1)
                next_piece()
            assert early + DC * CT - 2 > NPIECE
            for c in range(DC):
                for t in range(CT):
                    n = P if t < CT - 1 else CLAST
                    pe.wait_ge(t_done, t + 1)
                    mm = nc.tensor.matmul(mps[:, c], t_act[0:n, t, c * P:(c + 1) * P], ctx_sb[0:n, t],
                                          start=(t == 0), stop=(t == CT - 1))
                    if early < NPIECE:
                        next_piece()
                    elif c == DC - 1 and t == CT - 2:
                        pe.wait_ge(first_max_found, 1)
                        nc.tensor.transpose(proj[NPIECE % 2][0:NT, 0:P], neg_max[:], ident32[:]).then_inc(first_max_turned, 1)
            mm.then_inc(m_ready, 1)


def attend(nc, f32, f16, ALU, ACT, X, q_split, k_split, w_all, w_split_d, res, bo_rows, ident32, attn, values,
           qstack, kstack, ident16, hide_keys, partial, neg_max, max_row, hide_queries, zeros16, ones16, fold, w_scale,
           no_token, sorted_x, stack_in, max_in):
    es = ExitStack()
    with es:
        def sb(name, shape, dt):
            return es.enter_context(nc.sbuf_tensor(name, shape, dt))

        def sem(name):
            return es.enter_context(nc.semaphore(name))

        probs = sb("probs", [P, 2, TPQ * QB], f32)
        v_head = sb("v_head", [P, 2, NT, VW], f32)
        acc_sb = sb("acc_sb", [P, 2, NQ, QB], f32)
        folded = sb("folded", [P, QB], f32)
        inv = sb("inv", [P, 2, 2, NQ, 1], f32)
        w_in = sb("a_w_in", [P, 2, WU], f32)
        w_out = sb("a_w_out", [P, 2, 2, WU], f16)
        scores = [es.enter_context(nc.psum_tensor(f"scores{i}", [P, 2 * QB], f32)) for i in range(2)]
        ring = [es.enter_context(nc.psum_tensor(f"ring{i}", [P, QB], f32)) for i in range(NRING)]
        acc = es.enter_context(nc.psum_tensor("acc", [P, QB], f32))

        const_done = sem("const_done")
        scores_ready, exp_done = sem("scores_ready"), sem("exp_done")
        ring_ready, ring_done = sem("ring_ready"), sem("ring_done")
        max_found = sem("max_found")
        v_ready, pv_done, acc_copied = sem("v_ready"), sem("pv_done"), sem("acc_copied")
        inv_ready = sem("inv_ready")
        w_loaded = [sem(f"w_loaded{n}") for n in range(2)]
        w_stored = [sem(f"w_stored{n}") for n in range(2)]
        rows_stored = sem("rows_stored")
        w_hi, w_lo, biased = sem("w_hi"), sem("w_lo"), sem("biased")

        half_width = []
        for qb, k0 in QUADS:
            w = [QB - P * j if k0 == qb * TPQ else QB for j in range(TPQ)]
            half_width.append((w[0:2], w[2:4]))

        block = es.enter_context(nc.Block())

        @block.sync
        def _(sp):
            def load_max(slot, n):
                sp.wait_ge(ring_done, n)
                sp.dma_start(qstack[MROW:MROW + 1, slot, :], max_row[:, :]).then_inc(max_in, 16)

            def load_weights(h, parity):
                sp.dma_start(w_in[:, parity], w_all[:, bass.ds(h * WU, WU)]).then_inc(w_loaded[parity], 16)

            def store_weights(h, parity):
                address_first(sp, h * WU * 2)
                sp.wait_ge(w_lo, h + 1)
                sp.dma_start(w_split_d[:, :, bass.ds(h * WU, WU)].rearrange("a p w -> p a w"),
                             w_out[:, parity]).then_inc(w_stored[parity], 16)

            for h in range(2):
                load_weights(h, h)
            sp.dma_start(sorted_x.rearrange("(t p) d -> p t d", p=P),
                         no_token[:].broadcast_to([P, NSLOT // P, ROW])).then_inc(rows_stored, 16)

            def turn(i, last):
                for j in range(NSTACK):
                    if not (last and j == NSTACK - 1):
                        load_max((j + 1) % NSTACK, entries_before(i + j, "max", 0, False))
                    if not last:
                        address_first(sp, (i + (j + NSTACK)) * DH * S * 2)
                        sp.wait_ge(scores_ready, i * (2 * NQUAD) + 2 * NQUAD * (j + 1))
                        load_stack(sp, qstack, kstack, q_split, k_split, i + (j + NSTACK), j, stack_in[j])
                    store_weights(i + j, j % 2)
                    if not (last and j >= NSTACK - 2):
                        load_weights(i + (j + 2), j % 2)

            with sp.Fori(0, H // NSTACK - 1) as k:
                turn(k * NSTACK, False)
            turn(H - NSTACK, True)
            for parity in range(2):
                sp.wait_ge(w_stored[parity], 16 * (H // 2))
            sp.wait_ge(rows_stored, 16)

        @block.gpsimd
        def _(pool):
            nc.gpsimd.memset(v_head[:, 1], 1.0).then_inc(const_done, 1)
            nc.gpsimd.memset(acc_sb[:, 1, 0:NQ - 1], 1.0).then_inc(const_done, 1)

            def copy_values(h, n, slot, first):
                if not first:
                    pool.wait_ge(pv_done, n * NQUAD - (NQUAD - 2))
                nc.gpsimd.tensor_copy(v_head[:, slot], values[:, bass.ds(h, 1)].rearrange("p o t v -> p (o t) v")).then_inc(v_ready, 1)

            def first_halves(k, parity):
                if not isinstance(k, int):
                    pool.wait_ge(w_stored[parity], k * 16)
                pool.wait_ge(w_loaded[parity], k * 16 + 16)
                nc.gpsimd.tensor_tensor(w_out[:, parity, 0], w_in[:, parity], w_scale[:].broadcast_to([P, WU]),
                                        ALU.mult).then_inc(w_hi, 1)

            copy_values(0, 0, 0, True)
            first_halves(0, 0)
            copy_values(1, 1, 1, False)
            first_halves(0, 1)
            for g in range(NQ):
                tiles = slice(g * TPQ, (g + 1) * TPQ)
                nc.gpsimd.tensor_tensor(res[:, tiles], res[:, tiles],
                                        bo_rows[:].rearrange("p (o d) -> p o d", o=1).broadcast_to([P, TPQ, D]),
                                        ALU.add).then_inc(biased, 1)
            pool.wait_ge(biased, NQ)
            with pool.Fori(1, H // 2) as k:
                for j in range(2):
                    copy_values(k * 2 + j, k * 2 + j, j, False)
                    first_halves(k, j)

        @block.scalar
        def _(act):
            for half in range(2):
                for j in range(2):
                    at = (2 * half + j) * QB
                    fill = nc.scalar.activation(probs[:, 1, at:at + QB], ones16[:], ACT.Copy)
                fill.then_inc(exp_done, 1)

            def copy_acc(parity, qb, quads):
                act.wait_ge(pv_done, quads)
                nc.scalar.activation(acc_sb[:, parity, qb], acc[:], ACT.Copy).then_inc(acc_copied, 1)

            def head(i, j, last):
                h = i + j
                for s, (qb, k0) in enumerate(QUADS):
                    for half in range(2):
                        w = sum(half_width[s][half])
                        act.wait_ge(scores_ready, h * (2 * NQUAD) + (2 * s + half + 1))
                        if half == 0:
                            act.wait_ge(pv_done, h * NQUAD + (s + 1))
                        nc.scalar.activation(probs[:, s % 2, half * 2 * QB:half * 2 * QB + w],
                                             scores[half][:, 0:w], ACT.Exp).then_inc(exp_done, 1)
                    if s == 0:
                        copy_acc((j + 1) % 2, NQ - 1, h * NQUAD + 2)
                    for b in range(NQ - 1):
                        if s == LAST_QUAD[b] + 1:
                            if b == 0:
                                act.wait_ge(inv_ready, h * 2 + 2)
                            copy_acc(j % 2, b, h * NQUAD + (LAST_QUAD[b] + 3))

            turns(act, head)
            copy_acc((H - 1) % 2, NQ - 1, H * NQUAD + 2)

        @block.tensor
        def _(pe):
            pe.wait_ge(const_done, 2)

            def fold_half(bank, parity, half):
                cols = slice(half * QB // 2, (half + 1) * QB // 2)
                for b in range(NQ):
                    mm = nc.tensor.matmul(bank[VW * b:VW * (b + 1), 0:QB // 2], fold[:], acc_sb[:, parity, b, cols],
                                          start=True, stop=True)
                return mm

            def turn_half(bank, half):
                for t in range(TPQ // 2):
                    at = half * QB // 2 + t * P
                    mm = nc.tensor.transpose(bank[:, t * P:(t + 1) * P], folded[:, at:at + P], ident32[:])
                return mm

            def turn_max(bank):
                return nc.tensor.transpose(bank[0:NT, 0:P], neg_max[:], ident32[:])

            nc.tensor.matmul(acc[:], zeros16[:], ones16[:], start=True, stop=False).then_inc(pv_done, 1)
            for bank in ring:
                mm = nc.tensor.matmul(bank[:], zeros16[:], ones16[:], start=True, stop=True)
            mm.then_inc(ring_ready, NRING)

            def scores_half(h, slot, s, half):
                qb, k0 = QUADS[s]
                pe.wait_ge(exp_done, h * (2 * NQUAD) + (2 * s + half + 1))
                at = 0
                for j in (2 * half, 2 * half + 1):
                    w = half_width[s][half][j % 2]
                    kt = k0 + j
                    diagonal = k0 == qb * TPQ
                    mm = nc.tensor.matmul(scores[half][:, at:at + w], kstack[0:MROW + 1, slot, kt * P:(kt + 1) * P],
                                          qstack[0:MROW + 1, slot, (qb + 1) * QB - w:(qb + 1) * QB],
                                          start=True, stop=not diagonal)
                    if diagonal:
                        mm = nc.tensor.matmul(scores[half][:, at:at + P], ident16[:], hide_queries[:],
                                              start=False, stop=True)
                    at += w
                mm.then_inc(scores_ready, 1)

            def weigh(h, slot, s, exps):
                qb, k0 = QUADS[s]
                pe.wait_ge(exp_done, exps)
                first, last = k0 == 0, s == LAST_QUAD[qb]
                if first:
                    pe.wait_ge(acc_copied, h * NQ + (qb + 1))
                    pe.wait_ge(v_ready, h + 1)
                if qb == 0:
                    nc.tensor.matmul(acc[:], zeros16[:], ones16[:], start=True, stop=False)
                for j in range(TPQ):
                    w = half_width[s][j // 2][j % 2]
                    at = j // 2 * 2 * QB + (0 if j % 2 == 0 else half_width[s][j // 2][0])
                    mm = nc.tensor.matmul(acc[VW * j:VW * (j + 1), QB - w:QB], v_head[:, slot, k0 + j],
                                          probs[:, s % 2, at:at + w], start=first and qb > 0, stop=last)
                mm.then_inc(pv_done, 1)

            def head(i, j, last):
                h = i + j
                slot, next_slot = j, (j + 1) % NSTACK
                pe.wait_ge(max_in, h * 16 + 16)
                if not last:
                    pe.wait_ge(stack_in[next_slot], (i // NSTACK + 1 + (j + 1) // NSTACK) * STACK_DMAS
                               if isinstance(i, int) else i * (STACK_DMAS // NSTACK) + (1 + (j + 1) // NSTACK) * STACK_DMAS)
                order = ring_order(last)
                entry = 0

                def through_ring(items):
                    nonlocal entry
                    for kind, n in items:
                        bank = ring[(NFIRST + entry) % NRING]
                        pe.wait_ge(ring_done, h * NENTRY + (NFIRST + entry - NRING + 1))
                        if kind == "piece":
                            mm = form_piece(nc, bank, qstack, kstack, ident16, hide_keys, next_slot, n)
                        elif kind == "max":
                            pe.wait_ge(max_found, h + 1)
                            mm = turn_max(bank)
                        elif kind == "fold":
                            pe.wait_ge(acc_copied, h * NQ + 1)
                            mm = fold_half(bank, (j + 1) % 2, n)
                        else:
                            pe.wait_ge(ring_done, entries_before(h, "fold", n, last))
                            mm = turn_half(bank, n)
                        mm.then_inc(ring_ready, 1)
                        entry += 1

                for s in range(NQUAD):
                    scores_half(h, slot, s, 0)
                    through_ring(order[s][0])
                    scores_half(h, slot, s, 1)
                    through_ring(order[s][1])
                    if s == 0:
                        weigh(None, (j + 1) % 2, NQUAD - 1, h * (2 * NQUAD) + 2)
                    else:
                        weigh(h, j % 2, s - 1, h * (2 * NQUAD) + (2 * s + 2))
                    through_ring(order[s][2])

            turns(pe, head)
            weigh(None, (H - 1) % 2, NQUAD - 1, H * 2 * NQUAD + 2)
            pe.wait_ge(acc_copied, H * NQ + 1)
            for k in range(4):
                kind, half, bank = k // 2, k % 2, ring[(NENTRIES - 4 + k) % NRING]
                pe.wait_ge(ring_done, NENTRIES - 4 + k - NRING + 1)
                if kind == 0:
                    fold_half(bank, (H - 1) % 2, half).then_inc(ring_ready, 1)
                else:
                    pe.wait_ge(ring_done, NENTRIES - 4 + half + 1)
                    turn_half(bank, half).then_inc(ring_ready, 1)

        @block.vector
        def _(dve):
            def find_max():
                nc.vector.tensor_reduce(out=neg_max[:], in_=partial[:], axis=X, op=ALU.max,
                                        negate=True).then_inc(max_found, 1)

            def copy_max(bank):
                nc.vector.tensor_copy(max_row[:], bank[0:NT, 0:P]).then_inc(ring_done, 1)

            def copy_folded(bank, half):
                nc.vector.tensor_copy(folded[:, half * QB // 2:(half + 1) * QB // 2], bank[:, 0:QB // 2]).then_inc(ring_done, 1)

            def norm_half(bank, col, n, half):
                turned = bank[:, 0:TPQ // 2 * P].rearrange("p (t b v) -> p t b v", t=TPQ // 2, b=NQ)
                tiles = attn[:].rearrange("p (b t) d -> p t b d", t=TPQ)[:, half * TPQ // 2:(half + 1) * TPQ // 2]
                nc.vector.reciprocal(inv[:, half], turned[:, :, :, DH:DH + 1]).then_inc(inv_ready, 1)
                dve.wait_ge(inv_ready, n + 4)
                nc.vector.tensor_tensor(tiles[:, :, :, bass.ds(col, DH)], turned[:, :, :, 0:DH],
                                        inv[:, half].broadcast_to([P, TPQ // 2, NQ, DH]), ALU.mult).then_inc(ring_done, 1)

            nc.vector.memset(inv[:], 1.0).then_inc(inv_ready, 4)
            dve.wait_ge(inv_ready, 4)
            dve.wait_ge(ring_ready, NFIRST)
            nc.vector.tensor_copy(folded[:, 0:1], ring[0][:, 0:1]).then_inc(ring_done, NRING)

            def head(i, j, last):
                h = i + j
                order = RING_OF_LAST if last else RING_OF_HEAD
                for entry, (kind, n) in enumerate(order):
                    bank = ring[(NFIRST + entry) % NRING]
                    if kind == "max":
                        dve.wait_ge(ring_done, h * NENTRY + (NFIRST + entry))
                        find_max()
                    dve.wait_ge(ring_ready, h * NENTRY + (NFIRST + entry + 1))
                    if kind == "piece":
                        reduce_piece(nc, X, ALU, bank, partial, n).then_inc(ring_done, 1)
                    elif kind == "max":
                        dve.wait_ge(max_in, h * 16 + 16)
                        copy_max(bank)
                    elif kind == "fold":
                        copy_folded(bank, n)
                    else:
                        norm_half(bank, h * DH, h * 2 + (n + 1), n)
                dve.wait_ge(w_hi, h + 1)
                nc.vector.scalar_tensor_tensor(out=w_out[:, j % 2, 1], in0=w_in[:, j % 2], scalar=WSCALE,
                                               in1=w_out[:, j % 2, 0], op0=ALU.mult, op1=ALU.subtract).then_inc(w_lo, 1)

            turns(dve, head)
            for k in range(4):
                kind, half, bank = k // 2, k % 2, ring[(NENTRIES - 4 + k) % NRING]
                dve.wait_ge(ring_ready, NENTRIES - 4 + k + 1)
                if kind == 0:
                    copy_folded(bank, half)
                else:
                    norm_half(bank, H * DH, H * 2 + half + 1, half)


def address_first(engine, address):
    if not isinstance(address, int):
        engine.to_reg(address)


def turns(engine, head):
    with engine.Fori(0, H // NSTACK - 1) as k:
        for j in range(NSTACK):
            head(k * NSTACK, j, False)
    for j in range(NSTACK):
        head(H - NSTACK, j, j == NSTACK - 1)


def finish(nc, f32, f16, u32, ALU, ACT, X, rows, res, attn, mats, wo_split, xm, gate_split, ident32, eps_col, w_split_d,
           weights, slot_of, column_of, sorted_x, by_token, out):
    es = ExitStack()
    with es:
        def sb(name, shape, dt):
            return es.enter_context(nc.sbuf_tensor(name, shape, dt))

        def sem(name):
            return es.enter_context(nc.semaphore(name))

        HEAD = 6
        R0, R1 = HEAD, HEAD + MAX_TILES
        NALL = S // TW + MAX_TILES
        HB = QB // TW
        NB = HC // HB
        NG = 4
        NC = S // TW
        HELD = TPQ // TB
        EARLY = NT - TPQ
        BY_POOL = 3
        NI = 3 * NQ
        NM = 2 * NQ
        PADT = NT // 2
        PADE = NE // 2

        work = sb("work", [P, 2 * 2 * DC * QB], f32)
        yT32 = work[:, 0:2 * DC * QB].rearrange("p (i c n) -> p i c n", i=2, c=DC)
        yT = [yT32[:, i].rearrange("p c n -> p (c n)").bitcast(f16).rearrange("p (s c n) -> p s c n", s=2, c=DC)
              for i in range(2)]
        summed = work[:, 2 * DC * QB:].rearrange("p (i t d) -> p i t d", i=2, t=TPQ)
        stats = sb("stats", [P, 2, TPQ, 6], f32)
        mean_var = sb("mean_var", [P, 2, TPQ, 2], f32)
        sd = sb("sd", [P, 2, TPQ], f32)
        rstd = sb("rstd", [P, 2, TPQ], f32)
        shift = sb("shift", [P, 2, TPQ], f32)
        heads = attn[:].rearrange("p t d -> p (t d)")

        def region(first, *shape):
            names = "abcd"[:len(shape)]
            return heads[:, first:first + int(np.prod(shape))].rearrange(
                f"p ({' '.join(names)}) -> p {' '.join(names)}", **dict(zip(names[1:], shape[1:])))

        returned = region(0, NG, 2, TB, D)
        held = region(0, HELD * TB, D)
        XR, YR = 2 * NG * TB * D // 2, 2 * NG * TB * D // 2 + 2 * TB * ROW
        x_rows = region(XR, 2, TB, ROW)
        y_rows = region(YR, 2, TB, D)
        at = HELD * TB * D
        logits = region(at, NT, NE)
        key = region(at + NT * NE, NT, NE)
        hot = region(at + 2 * NT * NE, 2, NT, NE)
        picked = region(at + 4 * NT * NE, NT, NE)
        scan = [region(at + 5 * NT * NE + i * (PADT + NT) * NE, PADT + NT, NE) for i in range(2)]
        at = YR
        rest = region(at, NT, NE)
        above = region(at, NE, NT)
        place = region(at + NT * NE, NT, NE)
        chosen = region(at + 2 * NT * NE, 2, NT, NE)
        best = sb("best", [P, 2, NT, 1], f32)
        first = sb("first", [P, NT, 1], f32)
        gap = sb("gap", [P, NT, 1], f32)
        gap_exp = sb("gap_exp", [P, NT, 1], f32)
        den = sb("den", [P, NT, 1], f32)
        before = sb("before", [P, P], f32)
        ones = sb("ones", [P, P], f32)
        downward = sb("downward", [P, 1, NE], f32)
        thresholds = sb("thresholds", [P, 1, NT], f32)
        tile_no = sb("tile_no", [P, MAX_TILES, 1], f32)
        own_slot = sb("own_slot", [P, MAX_TILES, TB], f32)
        second = sb("second", [P, 2, TB], f32)
        goal = sb("goal", [P, 2, TB], f32)
        behind = sb("behind", [P, 2, TB], f32)
        extra = sb("extra", [P, 2, TB], f32)
        gate = sb("gate", [P, 2, TB, 1], f32)
        dest = sb("dest", [P, 2, TB], u32)
        tscan = [sb(f"tscan{i}", [P, PADE + NE], f32) for i in range(2)]
        slot32 = sb("slot32", [P, 2, NT], f32)
        past = sb("past", [P, MAX_TILES, NE], f32)
        expert_of = sb("expert_of", [P, MAX_TILES], f32)
        xT = mats[:].bitcast(f16).rearrange("p (i s c n) -> p i s c n", i=2, s=2, c=DC)
        hid32 = sb("hid32", [P, 2, QB], f32)
        hid = work[:].bitcast(f16).rearrange("p (i s j n) -> p i s j n", i=2, s=2, j=HC)
        f_stats = sb("f_stats", [P, NT, 6], f32)
        f_mean_var = sb("f_mean_var", [P, NT, 2], f32)
        f_sd = sb("f_sd", [P, NT], f32)
        f_rstd = sb("f_rstd", [P, NT], f32)
        f_shift = sb("f_shift", [P, NT], f32)

        tps = [es.enter_context(nc.psum_tensor(f"turned{i}", [P, DC, QB], f32)) for i in range(2)]
        ops = [es.enter_context(nc.psum_tensor(f"ops{i}", [P, TPQ, D], f32)) for i in range(2)]
        hps = [tps[b // DC][:, b % DC] for b in range(NB)]
        f_tps = [ops[0][:, TPQ // 2 * i:TPQ // 2 * (i + 1)].rearrange("p t d -> p (t d)").rearrange("p (c n) -> p c n", c=DC)
                 for i in range(2)]
        yps = [ops[1][:, TPQ // 2 * i:TPQ // 2 * (i + 1)] for i in range(2)]
        rank = ops[1][:, TPQ // 2, 0:NT * NE].rearrange("p (t e) -> p t e", e=NE)
        total = ops[1][:, TPQ // 2, NT * NE:NT * NE + NE].rearrange("p (e o) -> p e o", o=1)
        CONSTS = 11

        shared_in, routed_in = sem("shared_in"), sem("routed_in")
        turned, hi_done, lo_done = sem("turned"), sem("hi_done"), sem("lo_done")
        product, added, stats_done, aggr_done = sem("product"), sem("added"), sem("stats_done"), sem("aggr_done")
        sd_done, rstd_done, shift_done, ln_done = sem("sd_done"), sem("rstd_done"), sem("shift_done"), sem("ln_done")
        ones_zero, consts_ready = sem("ones_zero"), sem("consts_ready")
        chosen_step, count_step, counts_ready, place_step = sem("chosen_step"), sem("count_step"), sem("counts_ready"), sem("place_step")
        slots_ready, columns_step, columns_ready = sem("slots_ready"), sem("columns_step"), sem("columns_ready")
        found_step = sem("found_step")
        gap_found, gap_exp_done, gates_step = sem("gap_found"), sem("gap_exp_done"), sem("gates_step")
        scattered, returned_in = [sem(f"scattered{g}") for g in range(NT // TPQ)], [sem(f"returned_in{g}") for g in range(NG)]
        rows_in, rows_out = [sem(f"rows_in{i}") for i in range(2)], [sem(f"rows_out{i}") for i in range(2)]
        f_turned, x_hi, x_lo = sem("f_turned"), sem("x_hi"), sem("x_lo")
        h_ready, silu_done, hid_hi, hid_lo = sem("h_ready"), sem("silu_done"), sem("hid_hi"), sem("hid_lo")
        y_ready, y_done, released, pair_added, combined = (
            sem("y_ready"), sem("y_done"), sem("released"), sem("pair_added"), sem("combined"))
        f_stats_done, f_aggr_done, f_sd_done, f_rstd_done, f_shift_done = (
            sem("f_stats_done"), sem("f_aggr_done"), sem("f_sd_done"), sem("f_rstd_done"), sem("f_shift_done"))
        early_final, pool_final, late_final, dve_final, stored = sem("early_final"), sem("pool_final"), sem("late_final"), sem("dve_final"), sem("stored")
        block = es.enter_context(nc.Block())

        def los(n):
            return n + 1 if n < NQ else n + 1 - NQ

        def shared(n):
            if not isinstance(n, int) or R0 <= n < R1:
                return None
            return n if n < R0 else n - MAX_TILES

        def in_turn(engine, step, first, last, ahead=0):
            start, pairs = R0 + 2, (R1 - ahead - R0 - 2) // 2
            for n in range(first, start):
                step(n, n % 2)
            with engine.Fori(0, pairs) as k:
                for j in range(2):
                    step(k * 2 + (start + j), (start + j) % 2)
            for n in range(start + 2 * pairs, last):
                step(n, n % 2)

        def rows_before(n, parity, per=16):
            return (n - R0 - (n - R0) % 2) * (per // 2) if isinstance(n, int) else (n - (R0 + (parity - R0) % 2)) * (per // 2)

        @block.sync
        def _(sp):
            sp.dma_start(weights[:, :, NE * WE:], w_split_d[:, :, NE * WE:].rearrange("a p w -> p a w")).then_inc(shared_in, 16)
            for e in range(NE):
                sp.dma_start(weights[:, :, e * WE:(e + 1) * WE],
                             w_split_d[:, :, e * WE:(e + 1) * WE].rearrange("a p w -> p a w")).then_inc(routed_in, 16)
            for g in range(NT // TPQ):
                sp.wait_ge(scattered[g], 16 * 2 * TPQ)

            def load(n, parity):
                sp.dma_start(x_rows[:, parity],
                             sorted_x[bass.ds((n - R0) * TW, TW), :].rearrange("(t p) d -> p t d", p=P)).then_inc(rows_in[parity], 16)

            for n in (R0, R0 + 1):
                load(n, n % 2)

            def both(n, parity):
                if not isinstance(n, int) or n + 2 < R1:
                    address_first(sp, (n + 2 - R0) * TW * ROW * 4)
                    sp.wait_ge(f_turned, n + 1)
                    sp.wait_ge(found_step, (n - R0) * 6 + 6)
                    load(n + 2, parity)

            in_turn(sp, both, R0, R1, 2)
            for i in range(2):
                sp.wait_ge(rows_out[i], 16 * TB * len(range(R0 + (i - R0) % 2, R1, 2)))
            sp.wait_ge(released, HELD * TB)
            for c in range(NC):
                if c >= NG:
                    sp.wait_ge(combined, c - NG + 1)
                for r in range(2):
                    sp.dma_start(returned[:, c % NG, r],
                                 by_token[r * S + c * TW:r * S + (c + 1) * TW, :].rearrange("(t p) d -> p t d", p=P)
                                 ).then_inc(returned_in[c % NG], 16)

            def save(g):
                tiles = slice(g * TPQ, (g + 1) * TPQ)
                sp.dma_start(out[g * QB:(g + 1) * QB, :].rearrange("(t p) d -> p t d", p=P), res[:, tiles]).then_inc(stored, 16)

            for g in range(EARLY // TPQ):
                sp.wait_ge(early_final, min(TPQ * (g + 1), EARLY - BY_POOL))
                if g == EARLY // TPQ - 1:
                    sp.wait_ge(pool_final, BY_POOL)
                save(g)
            sp.wait_ge(late_final, TPQ // 2)
            sp.wait_ge(dve_final, TPQ // 2)
            save(EARLY // TPQ)
            sp.wait_ge(stored, 16 * (NT // TPQ))

        @block.gpsimd
        def _(pool):
            for dst, pattern, base in ((downward, [[0, 1], [-1, NE]], NE), (thresholds, [[0, 1], [TW, NT]], 0),
                                       (tile_no, [[1, MAX_TILES], [0, 1]], 0)):
                nc.gpsimd.iota(dst[:], pattern=pattern, base=base, channel_multiplier=0,
                               allow_small_or_imprecise_dtypes=True).then_inc(consts_ready, 1)
            nc.gpsimd.iota(own_slot[:], pattern=[[TW, MAX_TILES], [P, TB]], base=0, channel_multiplier=1,
                           allow_small_or_imprecise_dtypes=True).then_inc(consts_ready, 1)
            nc.gpsimd.iota(rows[:, :, TOKEN:TOKEN + 1], pattern=[[P, NT], [0, 1]], base=0, channel_multiplier=1,
                           allow_small_or_imprecise_dtypes=True).then_inc(consts_ready, 1)
            pool.wait_ge(turned, NQ)
            for dst in (*scan, *tscan):
                nc.gpsimd.memset(dst[:] if dst in tscan else dst, 0.0).then_inc(consts_ready, 1)
            nc.gpsimd.memset(ones[:], 1.0).then_inc(consts_ready, 1)
            nc.gpsimd.memset(before[:], 1.0).then_inc(ones_zero, 1)
            pool.wait_ge(ones_zero, 1)
            nc.gpsimd.affine_select(out=before[:], in_=before[:], compare_op=ALU.is_gt, fill=0.0,
                                    base=0, pattern=[[1, P]], channel_multiplier=-1).then_inc(consts_ready, 1)
            pool.wait_ge(slots_ready, 2)
            pool.wait_ge(gates_step, 4)
            pool.wait_ge(ln_done, NM)
            for t in range(NT):
                for r in range(2):
                    nc.gpsimd.indirect_dma_start(
                        out=sorted_x, out_offset=bass.IndirectOffsetOnAxis(ap=slot_of[:, r, t:t + 1], axis=0),
                        in_=rows[:, t], in_offset=None).then_inc(scattered[t // TPQ], 16)
            for n in range(R0, R1):
                pool.wait_ge(y_done, n + 1)
                for i in range(TB):
                    nc.gpsimd.indirect_dma_start(
                        out=by_token, out_offset=bass.IndirectOffsetOnAxis(ap=dest[:, n % 2, i:i + 1], axis=0),
                        in_=y_rows[:, n % 2, i], in_offset=None).then_inc(rows_out[n % 2], 16)
            for c in range(NC):
                pool.wait_ge(returned_in[c % NG], 32 * (c // NG + 1))
                nc.gpsimd.tensor_tensor(returned[:, c % NG, 0], returned[:, c % NG, 0], returned[:, c % NG, 1],
                                        ALU.add).then_inc(pair_added, 1)
            pool.wait_ge(f_shift_done, 1)
            for t in range(EARLY - BY_POOL, EARLY):
                nc.gpsimd.tensor_scalar(res[:, t], res[:, t], f_mean_var[:, t, 0:1], f_rstd[:, t:t + 1],
                                        ALU.subtract, ALU.mult).then_inc(pool_final, 1)

        @block.scalar
        def _(act):
            def hi(n):
                act.wait_ge(turned, n + 1)
                if n >= 2:
                    act.wait_ge(product, n - 1)
                nc.scalar.activation(yT32[:, n % 2] if n // NQ == 1 else yT[n % 2][:, 0], tps[n % 2][:],
                                     ACT.Copy).then_inc(hi_done, 1)

            def normalise(n):
                g = n % NQ
                act.wait_ge(aggr_done, TPQ * (n + 1))
                if n >= 2:
                    act.wait_ge(rstd_done, n - 1)
                nc.scalar.activation(sd[:, n % 2], mean_var[:, n % 2, :, 1], ACT.Sqrt, bias=eps_col[:]).then_inc(sd_done, 1)
                act.wait_ge(shift_done, n + 1)
                for t in range(TPQ):
                    ln = nc.scalar.activation(res[:, g * TPQ + t], summed[:, n % 2, t], ACT.Identity,
                                              bias=shift[:, n % 2, t:t + 1], scale=rstd[:, n % 2, t:t + 1])
                ln.then_inc(ln_done, 1)

            hi(0)
            hi(1)
            for n in range(NI):
                if n + 2 < NI:
                    hi(n + 2)
                if n < NM:
                    normalise(n)
            act.wait_ge(ln_done, NM)

            def first_half_x(n, parity):
                act.wait_ge(f_turned, n + 1)
                if not isinstance(n, int) or n >= 2:
                    act.wait_ge(h_ready, n * NB - NB)
                nc.scalar.activation(xT[:, parity, 0], f_tps[parity], ACT.Copy).then_inc(x_hi, 1)

            def activate(n, parity):
                for b in range(NB):
                    act.wait_ge(h_ready, n * NB + (b + 1))
                    if not isinstance(n, int) or n >= 1 or b >= 2:
                        act.wait_ge(hid_lo, n * NB + (b + 1 - 2))
                    nc.scalar.activation(hid32[:, b % 2], hps[b], ACT.Silu, scale=1.0 / WSCALE).then_inc(silu_done, 1)
                    act.wait_ge(silu_done, n * NB + (b + 1))
                    if not isinstance(n, int) or n >= 2:
                        act.wait_ge(y_ready, n - 1)
                    nc.scalar.activation(hid[:, parity, 0, b * HB:(b + 1) * HB], hid32[:, b % 2].rearrange("p (j n) -> p j n", n=TW),
                                         ACT.Copy).then_inc(hid_hi, 1)

            def step(n, parity):
                if not isinstance(n, int) or n + 1 < NALL:
                    activate(n + 1, 1 - parity)
                if not isinstance(n, int) or n + 2 < NALL:
                    first_half_x(n + 2, parity)

            first_half_x(0, 0)
            first_half_x(1, 1)
            activate(0, 0)
            act.wait_ge(gap_found, 1)
            nc.scalar.activation(gap_exp[:], gap[:], ACT.Exp).then_inc(gap_exp_done, 1)
            in_turn(act, step, 0, NALL)

            def deviation(first_tile, last_tile):
                act.wait_ge(f_aggr_done, last_tile)
                nc.scalar.activation(f_sd[:, first_tile:last_tile], f_mean_var[:, first_tile:last_tile, 1], ACT.Sqrt,
                                     bias=eps_col[:]).then_inc(f_sd_done, 1)

            def last_norm(t, signal):
                nc.scalar.activation(res[:, t], res[:, t], ACT.Identity, bias=f_shift[:, t:t + 1],
                                     scale=f_rstd[:, t:t + 1]).then_inc(signal, 1)

            deviation(0, EARLY)
            act.wait_ge(f_shift_done, 1)
            for t in range(EARLY - BY_POOL):
                last_norm(t, early_final)
            deviation(EARLY, NT)
            act.wait_ge(f_shift_done, 2)
            for t in range(EARLY, EARLY + TPQ // 2):
                last_norm(t, late_final)

        @block.tensor
        def _(pe):
            products = ((0, 0), (0, 1), (1, 0))

            def wait_read(n):
                pe.wait_ge(hi_done, n + 1)
                if n // NQ != 1:
                    pe.wait_ge(lo_done, los(n))

            def turn_item(n):
                step, g = divmod(n, NQ)
                if n >= 2:
                    wait_read(n - 2)
                if step:
                    pe.wait_ge(ln_done, (n - NQ + 1))
                for c in range(DC):
                    for t in range(TPQ):
                        tile = g * TPQ + t
                        src = attn[:, tile, DH + c * P:DH + (c + 1) * P] if step == 0 else res[:, tile, c * P:(c + 1) * P]
                        mm = nc.tensor.transpose(tps[n % 2][:, c, t * P:(t + 1) * P], src, ident32[:])
                mm.then_inc(turned, 1)

            def multiply(n):
                step = n // NQ
                w = (wo_split, xm, gate_split)[step]
                width = D if step < 2 else NE
                wait_read(n)
                if n >= 2:
                    pe.wait_ge(added, n - 1)
                for t in range(TPQ):
                    if step == 1:
                        for k in range(DC):
                            mm = nc.tensor.matmul(ops[n % 2][:, t], yT32[:, n % 2, k, t * P:(t + 1) * P], w[:, k],
                                                  start=(k == 0), stop=(k == DC - 1))
                        continue
                    m = 0
                    for k in range(DC):
                        for a, b in products:
                            mm = nc.tensor.matmul(ops[n % 2][:, t, 0:width], yT[n % 2][:, a, k, t * P:(t + 1) * P],
                                                  w[:, b, k], start=(m == 0), stop=(m == 5))
                            m += 1
                mm.then_inc(product, 1)

            turn_item(0)
            for n in range(NI):
                if n + 1 < NI:
                    turn_item(n + 1)
                multiply(n)

            def rank_tokens():
                pe.wait_ge(count_step, 5)
                pe.wait_ge(consts_ready, CONSTS)
                nc.tensor.matmul(rank, before[:], picked, start=True, stop=False)
                nc.tensor.matmul(rank, ones[:], scan[0][:, PADT - 1:PADT - 1 + NT], start=False, stop=True)
                nc.tensor.matmul(total[:, :, 0], ones[:], scan[0][:, PADT + NT - 1], start=True, stop=True).then_inc(counts_ready, 1)

            def turn(n, parity):
                t = shared(n)
                if t is None:
                    pe.wait_ge(rows_in[parity], rows_before(n, parity) + 16)
                if not isinstance(n, int) or n >= 2:
                    pe.wait_ge(x_lo, n - 1)
                for c in range(DC):
                    cols = slice(c * P, (c + 1) * P)
                    for i in range(TB):
                        mm = nc.tensor.transpose(f_tps[parity][:, c, i * P:(i + 1) * P],
                                                 x_rows[:, parity, i, cols] if t is None else res[:, t * TB + i, cols], ident32[:])
                mm.then_inc(f_turned, 1)

            def column(n):
                if shared(n) is not None:
                    return NE * WE
                return pe.value_load(column_of[0:1, bass.ds(n - R0, 1)], min_val=0, max_val=(NE - 1) * WE)

            def widen(n, parity):
                at = column(n)
                pe.wait_ge(x_lo, n + 1)
                for b in range(NB):
                    if not isinstance(n, int) or n >= 1:
                        pe.wait_ge(silu_done, n * NB + (b + 1 - NB))
                    for j in range(HB):
                        m = 0
                        for k in range(DC):
                            for a, c in products:
                                mm = nc.tensor.matmul(hps[b][:, j * TW:(j + 1) * TW],
                                                      weights[:, a, bass.ds(at + (k * HID + (b * HB + j) * P), P)],
                                                      xT[:, parity, c, k], start=(m == 0), stop=(m == 5))
                                m += 1
                    mm.then_inc(h_ready, 1)

            def narrow(n, parity):
                at = column(n)
                if not isinstance(n, int) or n >= 2:
                    pe.wait_ge(y_done, n - 1)
                for i in range(TB):
                    m = 0
                    for j in range(HC):
                        if i == 0 and j % HB == 0:
                            pe.wait_ge(hid_lo, n * NB + (j // HB + 1))
                        for a, c in products:
                            mm = nc.tensor.matmul(yps[parity][:, i], hid[:, parity, a, j, i * P:(i + 1) * P],
                                                  weights[:, c, bass.ds(at + (WE // 2 + j * D), D)],
                                                  start=(m == 0), stop=(m == 3 * HC - 1))
                            m += 1
                mm.then_inc(y_ready, 1)

            def step(n, parity):
                if isinstance(n, int) and n + 1 == R0:
                    pe.wait_ge(routed_in, 16 * NE)
                    pe.wait_ge(columns_ready, 1)
                if not isinstance(n, int) or n + 1 < NALL:
                    widen(n + 1, 1 - parity)
                if not isinstance(n, int) or n + 2 < NALL:
                    turn(n + 2, parity)
                if isinstance(n, int) and n == 1:
                    pe.wait_ge(place_step, 6)
                narrow(n, parity)

            pe.wait_ge(added, NI)
            turn(0, 0)
            turn(1, 1)
            pe.wait_ge(shared_in, 16)
            widen(0, 0)
            rank_tokens()
            in_turn(pe, step, 0, NALL, 2)

        @block.vector
        def _(dve):
            def lo(n):
                if n // NQ == 1:
                    return
                dve.wait_ge(hi_done, n + 1)
                nc.vector.tensor_tensor(yT[n % 2][:, 1], tps[n % 2][:], yT[n % 2][:, 0], ALU.subtract).then_inc(lo_done, 1)

            def add_residual(n):
                g = n % NQ
                if n >= NQ:
                    dve.wait_ge(ln_done, n - NQ + 1)
                if n >= 2:
                    dve.wait_ge(ln_done, n - 1)
                nc.vector.tensor_tensor(summed[:, n % 2], ops[n % 2][:], res[:, g * TPQ:(g + 1) * TPQ], ALU.add).then_inc(added, 1)
                dve.wait_ge(added, n + 1)
                if n >= 2:
                    dve.wait_ge(sd_done, n - 1)
                for t in range(TPQ):
                    nc.vector.bn_stats(stats[:, n % 2, t], summed[:, n % 2, t]).then_inc(stats_done, 1)
                for t in range(TPQ):
                    dve.wait_ge(stats_done, n * TPQ + t + 1)
                    nc.vector.bn_aggr(mean_var[:, n % 2, t], stats[:, n % 2, t]).then_inc(aggr_done, 1)

            def find_scale(n):
                dve.wait_ge(sd_done, n + 1)
                nc.vector.reciprocal(rstd[:, n % 2], sd[:, n % 2]).then_inc(rstd_done, 1)
                dve.wait_ge(rstd_done, n + 1)
                nc.vector.scalar_tensor_tensor(out=shift[:, n % 2], in0=mean_var[:, n % 2, :, 0], scalar=-1.0,
                                               in1=rstd[:, n % 2], op0=ALU.mult, op1=ALU.mult).then_inc(shift_done, 1)

            def choose():
                steps = 0

                def then(instruction):
                    nonlocal steps
                    steps += 1
                    instruction.then_inc(chosen_step, 1)
                    dve.wait_ge(chosen_step, steps)

                dve.wait_ge(added, NI)
                dve.wait_ge(consts_ready, CONSTS)
                for r, found in enumerate((logits, rest)):
                    if r == 1:
                        then(nc.vector.scalar_tensor_tensor(out=rest, in0=hot[:, 0], scalar=NEG, in1=logits,
                                                            op0=ALU.mult, op1=ALU.add))
                    then(nc.vector.tensor_reduce(out=best[:, r], in_=found, axis=X, op=ALU.max))
                    then(nc.vector.tensor_tensor(key, found, best[:, r].broadcast_to([P, NT, NE]), ALU.is_equal))
                    then(nc.vector.tensor_tensor(key, key, downward[:].broadcast_to([P, NT, NE]), ALU.mult))
                    then(nc.vector.tensor_reduce(out=first[:], in_=key, axis=X, op=ALU.max))
                    then(nc.vector.tensor_tensor(hot[:, r], key, first[:].broadcast_to([P, NT, NE]), ALU.is_equal))
                then(nc.vector.tensor_tensor(picked, hot[:, 0], hot[:, 1], ALU.add))

            def count_tiles():
                nc.vector.tensor_copy(scan[0][:, PADT:], picked).then_inc(count_step, 1)
                for k in range(4):
                    src, dst = scan[k % 2], scan[(k + 1) % 2]
                    dve.wait_ge(count_step, k + 1)
                    nc.vector.tensor_tensor(dst[:, PADT:], src[:, PADT:], src[:, PADT - 2 ** k:PADT - 2 ** k + NT],
                                            ALU.add).then_inc(count_step, 1)

            def place_tokens():
                dve.wait_ge(counts_ready, 1)
                nc.vector.tensor_tensor(above, total.broadcast_to([P, NE, NT]), thresholds[:].broadcast_to([P, NE, NT]),
                                        ALU.is_gt).then_inc(place_step, 1)
                dve.wait_ge(place_step, 1)
                nc.vector.tensor_reduce(out=tscan[0][:, PADE:], in_=above, axis=X, op=ALU.add).then_inc(place_step, 1)
                for k in range(3):
                    src, dst = tscan[k % 2], tscan[(k + 1) % 2]
                    dve.wait_ge(place_step, 2 + k)
                    nc.vector.tensor_tensor(dst[:, PADE:], src[:, PADE:], src[:, PADE - 2 ** k:PADE - 2 ** k + NE],
                                            ALU.add).then_inc(place_step, 1)
                first_tile = tscan[1][:, PADE - 1:PADE - 1 + NE].rearrange("p (o e) -> p o e", o=1)
                dve.wait_ge(place_step, 5)
                nc.vector.scalar_tensor_tensor(out=place, in0=first_tile.broadcast_to([P, NT, NE]), scalar=float(TW),
                                               in1=rank, op0=ALU.mult, op1=ALU.add).then_inc(place_step, 1)
                dve.wait_ge(place_step, 6)
                for r in range(2):
                    nc.vector.tensor_tensor(chosen[:, r], hot[:, r], place, ALU.mult).then_inc(place_step, 1)
                dve.wait_ge(place_step, 8)
                nc.vector.tensor_reduce(out=slot32[:], in_=chosen, axis=X, op=ALU.add).then_inc(place_step, 1)
                dve.wait_ge(place_step, 9)
                nc.vector.tensor_copy(slot_of[:], slot32[:]).then_inc(slots_ready, 1)
                nc.vector.tensor_copy(rows[:, :, BEST_SLOT], slot32[:, 0]).then_inc(slots_ready, 1)

            def find_gap():
                nc.vector.tensor_tensor(gap[:], best[:, 1], best[:, 0], ALU.subtract).then_inc(gap_found, 1)

            def find_columns():
                end_tile = tscan[1][:, PADE:].rearrange("p (o e) -> p o e", o=1)
                nc.vector.tensor_tensor(past[:], tile_no[:].broadcast_to([P, MAX_TILES, NE]),
                                        end_tile.broadcast_to([P, MAX_TILES, NE]), ALU.is_ge).then_inc(columns_step, 1)
                dve.wait_ge(columns_step, 1)
                nc.vector.tensor_reduce(out=expert_of[:], in_=past[:], axis=X, op=ALU.add).then_inc(columns_step, 1)
                dve.wait_ge(columns_step, 2)
                nc.vector.tensor_scalar(column_of[:], expert_of[:], NE - 1.0, float(WE), ALU.min, ALU.mult).then_inc(columns_ready, 1)

            def find_gates():
                dve.wait_ge(gap_exp_done, 1)
                nc.vector.tensor_scalar(den[:], gap_exp[:], 1.0, WSCALE, ALU.add, ALU.mult).then_inc(gates_step, 1)
                dve.wait_ge(gates_step, 1)
                nc.vector.reciprocal(rows[:, :, GATE:GATE + 1], den[:]).then_inc(gates_step, 1)
                dve.wait_ge(gates_step, 2)
                nc.vector.tensor_tensor(den[:], rows[:, :, GATE:GATE + 1], gap_exp[:], ALU.mult).then_inc(gates_step, 1)
                dve.wait_ge(gates_step, 3)
                nc.vector.tensor_tensor(rows[:, :, GATE_DIFF:GATE_DIFF + 1], den[:], rows[:, :, GATE:GATE + 1],
                                        ALU.subtract).then_inc(gates_step, 1)

            lo(0)
            lo(1)
            for n in range(NI):
                dve.wait_ge(product, n + 1)
                if n < NM:
                    add_residual(n)
                else:
                    g = n - NM
                    nc.vector.tensor_copy(logits[:, g * TPQ:(g + 1) * TPQ], ops[n % 2][:, :, 0:NE]).then_inc(added, 1)
                if n + 2 < NI:
                    lo(n + 2)
                if n < NM:
                    find_scale(n)

            def second_half_x(n, parity):
                dve.wait_ge(x_hi, n + 1)
                nc.vector.tensor_tensor(xT[:, parity, 1], f_tps[parity], xT[:, parity, 0], ALU.subtract).then_inc(x_lo, 1)

            def second_halves(n, parity):
                for b in range(NB):
                    chunks = slice(b * HB, (b + 1) * HB)
                    dve.wait_ge(hid_hi, n * NB + (b + 1))
                    nc.vector.tensor_tensor(hid[:, parity, 1, chunks], hid32[:, b % 2].rearrange("p (j n) -> p j n", n=TW),
                                            hid[:, parity, 0, chunks], ALU.subtract).then_inc(hid_lo, 1)

            def find_rows(n, parity):
                steps = (n - R0) * 6
                if not isinstance(n, int) or n >= R0 + 2:
                    dve.wait_ge(rows_out[parity], rows_before(n, parity, 16 * TB))
                nc.vector.tensor_tensor(second[:, parity], x_rows[:, parity, :, BEST_SLOT],
                                        own_slot[:, bass.ds(n - R0, 1)].rearrange("p o t -> p (o t)"),
                                        ALU.not_equal).then_inc(found_step, 1)
                dve.wait_ge(found_step, steps + 1)
                nc.vector.scalar_tensor_tensor(out=goal[:, parity], in0=second[:, parity], scalar=float(S),
                                               in1=x_rows[:, parity, :, TOKEN], op0=ALU.mult, op1=ALU.add).then_inc(found_step, 1)
                dve.wait_ge(found_step, steps + 2)
                nc.vector.scalar_tensor_tensor(out=behind[:, parity], in0=goal[:, parity], scalar=2.0 * S,
                                               in1=own_slot[:, bass.ds(n - R0, 1)].rearrange("p o t -> p (o t)"),
                                               op0=ALU.is_ge, op1=ALU.mult).then_inc(found_step, 1)
                dve.wait_ge(found_step, steps + 3)
                nc.vector.tensor_tensor(dest[:, parity], goal[:, parity], behind[:, parity], ALU.add).then_inc(found_step, 1)
                nc.vector.tensor_tensor(extra[:, parity], second[:, parity], x_rows[:, parity, :, GATE_DIFF],
                                        ALU.mult).then_inc(found_step, 1)
                dve.wait_ge(found_step, steps + 5)
                nc.vector.tensor_tensor(gate[:, parity, :, 0], extra[:, parity], x_rows[:, parity, :, GATE],
                                        ALU.add).then_inc(found_step, 1)

            def take(n, parity):
                t = shared(n)
                dve.wait_ge(y_ready, n + 1)
                if t is None:
                    dve.wait_ge(found_step, (n - R0) * 6 + 6)
                    nc.vector.tensor_tensor(y_rows[:, parity], yps[parity], gate[:, parity].broadcast_to([P, TB, D]),
                                            ALU.mult).then_inc(y_done, 1)
                    return
                tiles = slice(t * TB, (t + 1) * TB)
                if t < HELD:
                    nc.vector.tensor_scalar(held[:, tiles], yps[parity], 1.0 / WSCALE, None, ALU.mult).then_inc(y_done, 1)
                    return
                if t < HEAD:
                    dve.wait_ge(scattered[t * TB // TPQ], 16 * 2 * TPQ)
                nc.vector.scalar_tensor_tensor(out=res[:, tiles], in0=yps[parity], scalar=1.0 / WSCALE, in1=res[:, tiles],
                                               op0=ALU.mult, op1=ALU.add).then_inc(y_done, 1)

            def release():
                for g in range(HELD * TB // TPQ):
                    dve.wait_ge(scattered[g], 16 * 2 * TPQ)
                dve.wait_ge(y_done, HELD)
                nc.vector.tensor_tensor(res[:, 0:HELD * TB], res[:, 0:HELD * TB], held, ALU.add).then_inc(released, HELD * TB)

            def combine(c):
                tiles = slice(c * TB, (c + 1) * TB)
                dve.wait_ge(pair_added, c + 1)
                if c < HELD:
                    dve.wait_ge(released, HELD * TB)
                else:
                    dve.wait_ge(y_done, c + 1 if c < HEAD else c + MAX_TILES + 1)
                nc.vector.tensor_tensor(res[:, tiles], res[:, tiles], returned[:, c % NG, 0], ALU.add).then_inc(combined, 1)
                dve.wait_ge(combined, c + 1)
                for t in range(c * TB, (c + 1) * TB):
                    nc.vector.bn_stats(f_stats[:, t], res[:, t]).then_inc(f_stats_done, 1)
                for t in range(c * TB, (c + 1) * TB):
                    dve.wait_ge(f_stats_done, t + 1)
                    nc.vector.bn_aggr(f_mean_var[:, t], f_stats[:, t]).then_inc(f_aggr_done, 1)

            def last_scale(part, first_tile, last_tile):
                tiles = slice(first_tile, last_tile)
                dve.wait_ge(f_sd_done, part)
                nc.vector.reciprocal(f_rstd[:, tiles], f_sd[:, tiles]).then_inc(f_rstd_done, 1)
                dve.wait_ge(f_rstd_done, part)
                nc.vector.scalar_tensor_tensor(out=f_shift[:, tiles], in0=f_mean_var[:, tiles, 0], scalar=-1.0,
                                               in1=f_rstd[:, tiles], op0=ALU.mult, op1=ALU.mult).then_inc(f_shift_done, 1)

            def step(n, parity):
                if not isinstance(n, int) or n + 1 < NALL:
                    second_halves(n + 1, 1 - parity)
                if not isinstance(n, int) or R0 <= n + 1 < R1:
                    find_rows(n + 1, 1 - parity)
                if not isinstance(n, int) or n + 2 < NALL:
                    second_half_x(n + 2, parity)
                if not isinstance(n, int):
                    take(n, parity)
                    return
                if n == NALL - 2:
                    combine(0)
                    combine(1)
                if n == NALL - 1:
                    combine(4)
                    combine(5)
                    last_scale(1, 0, EARLY)
                    combine(6)
                take(n, parity)
                if n == 1:
                    find_columns()
                if n == 3:
                    release()
                if n == NALL - 2:
                    combine(2)
                    combine(3)

            second_half_x(0, 0)
            second_half_x(1, 1)
            choose()
            find_gap()
            count_tiles()
            second_halves(0, 0)
            place_tokens()
            find_gates()
            in_turn(dve, step, 0, NALL)
            combine(NC - 1)
            last_scale(2, EARLY, NT)
            dve.wait_ge(f_shift_done, 2)
            for t in range(EARLY + TPQ // 2, NT):
                nc.vector.tensor_scalar(res[:, t], res[:, t], f_mean_var[:, t, 0:1], f_rstd[:, t:t + 1],
                                        ALU.subtract, ALU.mult).then_inc(dve_final, 1)


def kernel(**inputs):
    import numpy as np
    import concourse.bacc as bacc
    from concourse import mybir
    from concourse.bass_utils import run_bass_kernel_spmd

    def lay_out(w1, w2):
        first = w1.reshape(NX, HID, DC, P).transpose(3, 0, 2, 1).reshape(P, NX, WE // 2)
        second = w2.reshape(NX, D, HC, P).transpose(3, 0, 2, 1).reshape(P, NX, WE // 2)
        return np.concatenate([first, second], axis=2).reshape(P, NX * WE)

    a = {k: np.asarray(v) for k, v in inputs.items()}
    arrays = {
        "x": a["x"][0],
        "xT": a["x"][0].T,
        "ctx_n": a["ctx_1024"][0],
        "ctxT": a["ctx_1024"][0].T,
        "wq": a["L0_attn_wq"], "wk": a["L0_attn_wk"], "wv": a["L0_attn_wv"], "wo": a["L0_attn_wo"],
        "b_qk": np.stack([a["L0_attn_bq"], a["L0_attn_bk"]]).reshape(2, DC, P).transpose(2, 0, 1),
        "bv": a["L0_attn_bv"], "bo": a["L0_attn_bo"],
        "lm": a["L0_xattn_learnable_matrix"],
        "w_all": lay_out(np.concatenate([a["L0_ffn_experts_w1"], a["L0_ffn_shared_w1"][None]]),
                         np.concatenate([a["L0_ffn_experts_w2"], a["L0_ffn_shared_w2"][None]])),
        "gT": a["L0_ffn_gate_w"].T,
    }
    arrays = {k: np.ascontiguousarray(v) for k, v in arrays.items()}
    nc = bacc.Bacc("TRN2", target_bir_lowering=False, num_devices=1)
    args = {k: nc.dram_tensor(k, v.shape, mybir.dt.from_np(v.dtype), kind="ExternalInput").ap() for k, v in arrays.items()}
    out = nc.dram_tensor("out", (S, D), mybir.dt.float32, kind="ExternalOutput").ap()
    decoder_layer(nc, out=out, **args)
    r = run_bass_kernel_spmd(nc, [arrays], core_ids=[0])
    return r.results[0]["out"].reshape(1, S, D)
```
